# Optimizing a Trainium2 kernel written in Bass

```python
import numpy as np
import jax
import jax.numpy as jnp

def _softmax(x, axis=-1):
    return jax.nn.softmax(x, axis=axis)

def _gelu(x):
    return jax.nn.gelu(x, approximate=True)

def _silu(x):
    return jax.nn.silu(x)

def _sigmoid(x):
    return jax.nn.sigmoid(x)

def _layernorm(x, axis=-1, eps=1e-05):
    m = jnp.mean(x, axis=axis, keepdims=True)
    v = jnp.var(x, axis=axis, keepdims=True)
    return (x - m) / jnp.sqrt(v + eps)

def _scatter_add(tgt, idx, src, axis=0):
    return tgt.at[idx].add(src)

def _segment_sum(src, seg, n):
    return jax.ops.segment_sum(src, seg, n)
kernel_name = 'mk_macaron_d1_jaxref_r8_cc907e'

def setup_inputs(seed: int=0):
    np.random.seed(seed)
    _w = jnp.asarray

    def _L0_attn_setup():
        import jax, jax.numpy as jnp
        import numpy as np
        D_MODEL = 512
        D_XB = 128
        D_INNER = 512
        HEADDIM = 128
        DSTATE = 128
        NHEADS = D_INNER // HEADDIM
        DCONV = 4
        INTER = 1792
        EPS = 1e-05
        CHUNK = 128

        def rmsnorm(x, w):
            return x * jax.lax.rsqrt(jnp.mean(x * x, axis=-1, keepdims=True) + EPS) * w

        def silu(x):
            return x * jax.nn.sigmoid(x)

        def mamba2(x, w_in, conv_w, conv_b, A_log, D, dt_bias, w_out):
            B, L, _ = x.shape
            H, P, N = (NHEADS, HEADDIM, DSTATE)
            G = D_XB // P
            rep = H // G
            zxbcdt = x @ w_in.T
            z, xs, Bs, Cs, dt = jnp.split(zxbcdt, [D_INNER, D_INNER + D_XB, D_INNER + 2 * D_XB, 2 * D_INNER + 2 * D_XB], axis=-1)
            xBC = jnp.concatenate([xs, Bs, Cs], axis=-1)
            conv = jax.lax.conv_general_dilated(xBC.transpose(0, 2, 1), conv_w[:, None, :], (1,), [(DCONV - 1, 0)], feature_group_count=conv_w.shape[0])
            xBC = silu(conv.transpose(0, 2, 1) + conv_b)
            xs, Bs, Cs = jnp.split(xBC, [D_XB, 2 * D_XB], axis=-1)
            dt = jax.nn.softplus(dt + dt_bias)
            A = -jnp.exp(A_log)
            xh = jnp.repeat(xs.reshape(B, L, G, P), rep, axis=2)
            Bh = jnp.repeat(Bs.reshape(B, L, G, N), rep, axis=2)
            Ch = Cs.reshape(B, L, H, N)
            c, Q = (L // CHUNK, CHUNK)
            a = (dt * A).reshape(B, c, Q, H).transpose(0, 1, 3, 2)
            dtc = dt.reshape(B, c, Q, H).transpose(0, 1, 3, 2)
            Xc = xh.reshape(B, c, Q, H, P).transpose(0, 1, 3, 2, 4)
            Bc = Bh.reshape(B, c, Q, H, N).transpose(0, 1, 3, 2, 4)
            Cc = Ch.reshape(B, c, Q, H, N).transpose(0, 1, 3, 2, 4)
            cs = jnp.cumsum(a, axis=-1)
            tri = jnp.tril(jnp.ones((Q, Q), bool))
            Ldec = jnp.where(tri, jnp.exp(cs[..., :, None] - cs[..., None, :]), 0.0)
            Xdt = Xc * dtc[..., None]
            att = jnp.einsum('bchqn,bchkn->bchqk', Cc, Bc) * Ldec
            Yd = jnp.einsum('bchqk,bchkp->bchqp', att, Xdt)
            dec_end = jnp.exp(cs[..., -1:] - cs)
            states = jnp.einsum('bchq,bchqn,bchqp->bchpn', dec_end, Bc, Xdt)
            g = jnp.exp(cs[..., -1])

            def step(S, inp):
                gk, st = inp
                return (gk[:, :, None, None] * S + st, S)
            S0 = jnp.zeros((B, H, P, N), x.dtype)
            _, prev = jax.lax.scan(step, S0, (g.transpose(1, 0, 2), states.transpose(1, 0, 2, 3, 4)))
            prev = prev.transpose(1, 0, 2, 3, 4)
            Yo = jnp.einsum('bchqn,bchpn,bchq->bchqp', Cc, prev, jnp.exp(cs))
            Y = (Yd + Yo).transpose(0, 1, 3, 2, 4).reshape(B, L, H, P)
            Y = Y + D[:, None] * xh
            y = Y.reshape(B, L, D_INNER) * silu(z)
            return y @ w_out.T
        key = jax.random.key(seed)
        ks = jax.random.split(key, 10)
        B, L = (2, 256)
        proj_out = 2 * D_INNER + 2 * D_XB + NHEADS
        conv_dim = 2 * D_XB + D_INNER
        return {'hidden_states': jax.random.normal(ks[0], (B, L, D_MODEL), jnp.float32), 'w_in': jax.random.normal(ks[1], (proj_out, D_MODEL), jnp.float32) * 0.02, 'conv_w': jax.random.normal(ks[2], (conv_dim, DCONV), jnp.float32) * 0.1, 'conv_b': jnp.zeros((conv_dim,), jnp.float32), 'A_log': jnp.log(jnp.arange(1, NHEADS + 1, dtype=jnp.float32)), 'D': jnp.ones((NHEADS,), jnp.float32), 'dt_bias': jax.random.normal(ks[3], (NHEADS,), jnp.float32) * 0.1, 'w_out': jax.random.normal(ks[4], (D_MODEL, D_INNER), jnp.float32) * 0.02, 'ln1_w': jnp.ones((D_MODEL,), jnp.float32), 'ln2_w': jnp.ones((D_MODEL,), jnp.float32), 'gate_w': jax.random.normal(ks[5], (INTER, D_MODEL), jnp.float32) * 0.02, 'up_w': jax.random.normal(ks[6], (INTER, D_MODEL), jnp.float32) * 0.02, 'down_w': jax.random.normal(ks[7], (D_MODEL, INTER), jnp.float32) * 0.02}
    _L0_attn_in = _L0_attn_setup()

    def _L0_ffn_setup():
        import jax, jax.numpy as jnp
        import numpy as np
        GROUP_SIZE = 64
        RANK = 16
        ALPHA = 1.0

        def _dequant(qweight, scales, zeros):
            O, I = qweight.shape
            G = I // GROUP_SIZE
            q = qweight.astype(scales.dtype).reshape(O, G, GROUP_SIZE)
            w = (q - zeros[:, :, None]) * scales[:, :, None]
            return w.reshape(O, I)
        key = jax.random.key(seed)
        ks = jax.random.split(key, 7)
        B, S, D_in, D_out = (4, 256, 512, 512)
        n_groups = D_in // GROUP_SIZE
        x = jax.random.normal(ks[0], (B, S, D_in), dtype=jnp.float32)
        qweight = jax.random.randint(ks[1], (D_out, D_in), 0, 16, dtype=jnp.int32)
        scales = jax.random.uniform(ks[2], (D_out, n_groups), dtype=jnp.float32) * 0.02
        zeros = jax.random.uniform(ks[3], (D_out, n_groups), dtype=jnp.float32) * 16.0
        lora_A = jax.random.normal(ks[4], (RANK, D_in), dtype=jnp.float32) / np.sqrt(D_in)
        lora_B = jax.random.normal(ks[5], (D_out, RANK), dtype=jnp.float32) * 0.01
        bias = jax.random.normal(ks[6], (D_out,), dtype=jnp.float32) * 0.02
        return {'x': x, 'qweight': qweight, 'scales': scales, 'zeros': zeros, 'lora_A': lora_A, 'lora_B': lora_B, 'bias': bias}
    _L0_ffn_in = _L0_ffn_setup()
    _d = {'L0_attn_hidden_states': _L0_attn_in['hidden_states'], 'L0_attn_w_in': _L0_attn_in['w_in'], 'L0_attn_conv_w': _L0_attn_in['conv_w'], 'L0_attn_conv_b': _L0_attn_in['conv_b'], 'L0_attn_A_log': _L0_attn_in['A_log'], 'L0_attn_D': _L0_attn_in['D'], 'L0_attn_dt_bias': _L0_attn_in['dt_bias'], 'L0_attn_w_out': _L0_attn_in['w_out'], 'L0_attn_ln1_w': _L0_attn_in['ln1_w'], 'L0_attn_ln2_w': _L0_attn_in['ln2_w'], 'L0_attn_gate_w': _L0_attn_in['gate_w'], 'L0_attn_up_w': _L0_attn_in['up_w'], 'L0_attn_down_w': _L0_attn_in['down_w'], 'L0_ffn_qweight': _L0_ffn_in['qweight'], 'L0_ffn_scales': _L0_ffn_in['scales'], 'L0_ffn_zeros': _L0_ffn_in['zeros'], 'L0_ffn_lora_A': _L0_ffn_in['lora_A'], 'L0_ffn_lora_B': _L0_ffn_in['lora_B'], 'L0_ffn_bias': _L0_ffn_in['bias']}
    _x0 = _d['L0_attn_hidden_states']
    _d['L0_attn_hidden_states'] = jax.random.normal(jax.random.fold_in(jax.random.key(seed), 1), (1, 2048, 512), dtype=_x0.dtype)
    del _x0
    return _d

def reference(L0_attn_hidden_states, L0_attn_w_in, L0_attn_conv_w, L0_attn_conv_b, L0_attn_A_log, L0_attn_D, L0_attn_dt_bias, L0_attn_w_out, L0_attn_ln1_w, L0_attn_ln2_w, L0_attn_gate_w, L0_attn_up_w, L0_attn_down_w, L0_ffn_qweight, L0_ffn_scales, L0_ffn_zeros, L0_ffn_lora_A, L0_ffn_lora_B, L0_ffn_bias):

    def _L0_attn_ref(hidden_states, w_in, conv_w, conv_b, A_log, D, dt_bias, w_out, ln1_w, ln2_w, gate_w, up_w, down_w):
        import jax, jax.numpy as jnp
        import numpy as np
        D_MODEL = 512
        D_XB = 128
        D_INNER = 512
        HEADDIM = 128
        DSTATE = 128
        NHEADS = D_INNER // HEADDIM
        DCONV = 4
        INTER = 1792
        EPS = 1e-05
        CHUNK = 128

        def rmsnorm(x, w):
            return x * jax.lax.rsqrt(jnp.mean(x * x, axis=-1, keepdims=True) + EPS) * w

        def silu(x):
            return x * jax.nn.sigmoid(x)

        def mamba2(x, w_in, conv_w, conv_b, A_log, D, dt_bias, w_out):
            B, L, _ = x.shape
            H, P, N = (NHEADS, HEADDIM, DSTATE)
            G = D_XB // P
            rep = H // G
            zxbcdt = x @ w_in.T
            z, xs, Bs, Cs, dt = jnp.split(zxbcdt, [D_INNER, D_INNER + D_XB, D_INNER + 2 * D_XB, 2 * D_INNER + 2 * D_XB], axis=-1)
            xBC = jnp.concatenate([xs, Bs, Cs], axis=-1)
            conv = jax.lax.conv_general_dilated(xBC.transpose(0, 2, 1), conv_w[:, None, :], (1,), [(DCONV - 1, 0)], feature_group_count=conv_w.shape[0])
            xBC = silu(conv.transpose(0, 2, 1) + conv_b)
            xs, Bs, Cs = jnp.split(xBC, [D_XB, 2 * D_XB], axis=-1)
            dt = jax.nn.softplus(dt + dt_bias)
            A = -jnp.exp(A_log)
            xh = jnp.repeat(xs.reshape(B, L, G, P), rep, axis=2)
            Bh = jnp.repeat(Bs.reshape(B, L, G, N), rep, axis=2)
            Ch = Cs.reshape(B, L, H, N)
            c, Q = (L // CHUNK, CHUNK)
            a = (dt * A).reshape(B, c, Q, H).transpose(0, 1, 3, 2)
            dtc = dt.reshape(B, c, Q, H).transpose(0, 1, 3, 2)
            Xc = xh.reshape(B, c, Q, H, P).transpose(0, 1, 3, 2, 4)
            Bc = Bh.reshape(B, c, Q, H, N).transpose(0, 1, 3, 2, 4)
            Cc = Ch.reshape(B, c, Q, H, N).transpose(0, 1, 3, 2, 4)
            cs = jnp.cumsum(a, axis=-1)
            tri = jnp.tril(jnp.ones((Q, Q), bool))
            Ldec = jnp.where(tri, jnp.exp(cs[..., :, None] - cs[..., None, :]), 0.0)
            Xdt = Xc * dtc[..., None]
            att = jnp.einsum('bchqn,bchkn->bchqk', Cc, Bc) * Ldec
            Yd = jnp.einsum('bchqk,bchkp->bchqp', att, Xdt)
            dec_end = jnp.exp(cs[..., -1:] - cs)
            states = jnp.einsum('bchq,bchqn,bchqp->bchpn', dec_end, Bc, Xdt)
            g = jnp.exp(cs[..., -1])

            def step(S, inp):
                gk, st = inp
                return (gk[:, :, None, None] * S + st, S)
            S0 = jnp.zeros((B, H, P, N), x.dtype)
            _, prev = jax.lax.scan(step, S0, (g.transpose(1, 0, 2), states.transpose(1, 0, 2, 3, 4)))
            prev = prev.transpose(1, 0, 2, 3, 4)
            Yo = jnp.einsum('bchqn,bchpn,bchq->bchqp', Cc, prev, jnp.exp(cs))
            Y = (Yd + Yo).transpose(0, 1, 3, 2, 4).reshape(B, L, H, P)
            Y = Y + D[:, None] * xh
            y = Y.reshape(B, L, D_INNER) * silu(z)
            return y @ w_out.T
        res = hidden_states
        h = rmsnorm(hidden_states, ln1_w)
        h = res + mamba2(h, w_in, conv_w, conv_b, A_log, D, dt_bias, w_out)
        res = h
        h2 = rmsnorm(h, ln2_w)
        mlp = silu(h2 @ gate_w.T) * (h2 @ up_w.T) @ down_w.T
        return res + mlp

    def _L0_ffn_ref(x, qweight, scales, zeros, lora_A, lora_B, bias):
        import jax, jax.numpy as jnp
        import numpy as np
        GROUP_SIZE = 64
        RANK = 16
        ALPHA = 1.0

        def _dequant(qweight, scales, zeros):
            O, I = qweight.shape
            G = I // GROUP_SIZE
            q = qweight.astype(scales.dtype).reshape(O, G, GROUP_SIZE)
            w = (q - zeros[:, :, None]) * scales[:, :, None]
            return w.reshape(O, I)
        W = _dequant(qweight, scales, zeros)
        y = jnp.einsum('bsi,oi->bso', x, W)
        scaling = ALPHA / RANK
        lora = jnp.einsum('bsr,or->bso', jnp.einsum('bsi,ri->bsr', x, lora_A), lora_B)
        return y + scaling * lora + bias
    x = L0_attn_hidden_states
    x = x + 0.5 * _L0_ffn_ref(_layernorm(x, axis=-1), L0_ffn_qweight, L0_ffn_scales, L0_ffn_zeros, L0_ffn_lora_A, L0_ffn_lora_B, L0_ffn_bias)
    x = x + _L0_attn_ref(_layernorm(x, axis=-1), L0_attn_w_in, L0_attn_conv_w, L0_attn_conv_b, L0_attn_A_log, L0_attn_D, L0_attn_dt_bias, L0_attn_w_out, L0_attn_ln1_w, L0_attn_ln2_w, L0_attn_gate_w, L0_attn_up_w, L0_attn_down_w)
    x = x + 0.5 * _L0_ffn_ref(_layernorm(x, axis=-1), L0_ffn_qweight, L0_ffn_scales, L0_ffn_zeros, L0_ffn_lora_A, L0_ffn_lora_B, L0_ffn_bias)
    return x

_drawn_inputs = setup_inputs


def setup_inputs(seed=0):
    import zlib

    import numpy as np

    out = dict(_drawn_inputs(seed))
    spreads = {'L0_attn_conv_b': (0.0, 0.1),
     'L0_attn_D': (1.0, 0.2),
     'L0_attn_ln1_w': (1.0, 0.2),
     'L0_attn_ln2_w': (1.0, 0.2)}
    factors = {}
    for name, (base, spread) in spreads.items():
        noise = np.random.default_rng([zlib.crc32(name.encode()), seed]).standard_normal(out[name].shape)
        drawn = base * np.exp(spread * noise) if base else spread * noise
        out[name] = jnp.asarray(drawn.astype(out[name].dtype))
    for name, factor in factors.items():
        out[name] = (out[name] * factor).astype(out[name].dtype)
    return out
```

```python
from contextlib import ExitStack

import concourse.bass as bass
from concourse import mybir

ALU = mybir.AluOpType
ACT = mybir.ActivationFunctionType
F32 = mybir.dt.float32
F16 = mybir.dt.float16
BF16 = mybir.dt.bfloat16
I32 = mybir.dt.int32
AX_X = mybir.AxisListType.X

P = 128
EPS = 1e-5
ACT_SCALE = 2.0 ** 10
GATED_SCALE = 2.0 ** -54
W_TOP = 14
TINY = 2.0 ** -90
MASKED = -1e30
GROUP = 64
PARTS = ((0, 0), (0, 1), (1, 0))


class Index:

    def __init__(self, value, least):
        self.value, self.least = value, least

    def __mul__(self, k):
        return Index(self.value * k, self.least * k)

    def __add__(self, k):
        return Index(self.value + k, self.least + k)


def at(i):
    return i.value if isinstance(i, Index) else i


def after(eng, event, count):
    sem, start = event if isinstance(event, tuple) else (event, 0)
    if isinstance(count, Index):
        assert count.least + start > 0, (sem, count.least)
        eng.wait_ge(sem, count.value + start)
    elif count > 0:
        eng.wait_ge(sem, count + start)


def build(nc, x_in, w_in_t, conv_w, conv_b, a_log, d_skip, dt_bias, w_out_t, ln1_w, ln2_w,
          gate_t, up_t, down_t, q_t, scales_t, zeros_t, lora_a, lora_b_t, bias, out):
    T, DM = x_in.shape
    KB = DM // P
    NPROJ = w_in_t.shape[1]
    H = a_log.shape[1]
    DI = w_out_t.shape[0]
    CONV = conv_w.shape[0]
    CB = CONV // P
    NTAP = conv_w.shape[1]
    ZB = DI // P
    INTER = gate_t.shape[1]
    RANK = lora_a.shape[0]
    ST = 512
    NS = T // ST
    CH = ST // P
    NCH = T // P
    PAIR = 2 * P
    NP = INTER // PAIR
    assert ZB == H == KB == 4 and CB == 2 + H and NTAP == 4 and INTER % PAIR == 0
    LORA_SCALE = 1.0 / RANK

    ctx = ExitStack()
    with ctx:
        def sb(name, shape, dt=F32):
            return ctx.enter_context(nc.sbuf_tensor(name, shape, dt))

        def sem(name):
            return ctx.enter_context(nc.semaphore(name))

        w_ffn = [sb(f"w_ffn{p}", [P, KB, DM], F16) for p in range(2)]
        w_in = [sb(f"w_in{p}", [P, KB, NPROJ], F16) for p in range(2)]
        w_out = sb("w_out", [P, H, DM])
        raw_gu = sb("raw_gu", [P, 2, KB, PAIR])
        raw_d = sb("raw_d", [P, 2, DM])
        xs = sb("xs", [P, NCH, DM])
        h2T = [sb(f"h2T{p}", [P, KB, T], F16) for p in range(2)]
        stage = sb("stage", [P, KB * NPROJ])
        raw_in = stage[:, :].rearrange("p (k n) -> p k n", k=KB)
        xbc = stage[:, 0:CB * ST].rearrange("p (b t) -> p b t", b=CB)
        szs = stage[:, CB * ST:(CB + ZB) * ST].rearrange("p (h t) -> p h t", h=ZB)
        mA = [stage[:, 1024 * p:1024 * (p + 1)].bitcast(F16).rearrange("p (i t) -> p i t", i=NS) for p in range(2)]
        mB = [stage[:, 2048 + 512 * p:2560 + 512 * p].bitcast(F16).rearrange("p (i t) -> p i t", i=2) for p in range(2)]
        gt = stage[:, 3072:4096].rearrange("p (i t) -> p i t", i=2)
        gp = stage[:, 4096:5120].rearrange("p (i t) -> p i t", i=2)
        half = sb("half", [P, 2 * (2 * KB * P + KB * ST)], F16)
        nT = [[half[:, (2 * s + p) * KB * P:(2 * s + p + 1) * KB * P].rearrange("p (k t) -> p k t", k=KB)
               for p in range(2)] for s in range(2)]
        hT = [half[:, 4 * KB * P + p * KB * ST:4 * KB * P + (p + 1) * KB * ST].rearrange("p (k t) -> p k t", k=KB)
              for p in range(2)]
        w_gu = [half[:, 2048 * p:2048 * (p + 1)].rearrange("p (g k n) -> p g k n", g=2, k=KB) for p in range(2)]
        w_dn = [half[:, 4096 + 1024 * p:5120 + 1024 * p].rearrange("p (b n) -> p b n", b=2) for p in range(2)]
        x_t = sb("x_t", [P, CH, DM])
        n0 = sb("n0", [P, DM])
        hn = sb("hn", [P, DM])
        h2n = sb("h2n", [P, DM])
        n1 = sb("n1", [P, DM])
        x2 = sb("x2", [P, 2, DM])
        junk = sb("junk", [P, DM], BF16)
        pre = sb("pre", [P, 2, ST + NTAP - 1])
        hist = sb("hist", [P, CB, NTAP - 1])
        th = sb("th", [P, 2, ST])
        tm = sb("tm", [P, 2, 2, P])
        Ld = sb("Ld", [P, H, P])
        S = sb("S", [P, 2, H, P])
        ecs = sb("ecs", [P, H, P])
        xds = sb("xds", [P, 2, H, P])
        state = sb("state", [P, H, P])
        q_raw = h2T[0][:, :, :].rearrange("p k t -> p (k t)").bitcast(I32)[:, 0:KB * DM].rearrange("p (k n) -> p k n", k=KB)
        z_bc = h2T[0][:, :, :].rearrange("p k t -> p (k t)").bitcast(F32)[:, KB * DM:2 * KB * DM].rearrange("p (k n) -> p k n", k=KB)
        s_bc = h2T[1][:, :, :].rearrange("p k t -> p (k t)").bitcast(F32)[:, 0:KB * DM].rearrange("p (k n) -> p k n", k=KB)
        wf = h2T[1][:, :, :].rearrange("p k t -> p (k t)").bitcast(F32)[:, KB * DM:2 * KB * DM].rearrange("p (k n) -> p k n", k=KB)
        la = sb("la", [RANK, DM])
        lb = sb("lb", [RANK, DM])
        cT = [[x_t[:, s, p * 256:(p + 1) * 256].bitcast(F16).rearrange("p (k t) -> p k t", k=KB)
               for p in range(2)] for s in range(2)]
        o_t = [x_t[:, 2 + s, :] for s in range(2)]
        c_n = [n0, hn]

        ident = sb("ident", [P, P])
        tri = sb("tri", [P, P])
        mask = sb("mask", [P, P])
        d_diag = sb("d_diag", [P, H, P])
        hb = sb("hb", [P, DM])
        cw = sb("cw", [P, CB, NTAP])
        cb = sb("cb", [P, CB])
        al = sb("al", [P, H])
        dsk = sb("dsk", [P, H])
        dtb = sb("dtb", [P, H])
        ln1 = sb("ln1", [P, KB])
        ln2 = sb("ln2", [P, KB])
        mhalf = sb("mhalf", [P, 1])
        mx = sb("mx", [P, 2])
        mxa = sb("mxa", [P, 2])
        pw = sb("pw", [P, 2])
        sw = sb("sw", [P, 2])
        d_f = sb("d_f", [P, 1])
        d_i = sb("d_i", [P, 1])
        d_ih = sb("d_ih", [P, 1])
        mx3 = sb("mx3", [P, 3])
        mxa3 = sb("mxa3", [P, 3])
        pw3 = sb("pw3", [P, 3])
        sw3 = sb("sw3", [P, 3])
        dgh = sb("dgh", [P, 1])
        d_tmp = sb("d_tmp", [P, 1])
        d_d = sb("d_d", [P, 1])
        st6 = sb("st6", [P, 2, 6])
        mv0 = sb("mv0", [P, 3])
        r0 = sb("r0", [P, 1])
        mvN = sb("mvN", [P, CH, 3])
        rN = sb("rN", [P, CH])
        muC = sb("muC", [P, CH])
        rC = sb("rC", [P, CH])
        rt = sb("rt", [P, 4])
        rr = sb("rr", [P, 1])
        ssq = sb("ssq", [P, 1])
        r2 = sb("r2", [P, 2])
        NT = CH * H
        dt = sb("dt", [P, NT])
        dA = sb("dA", [P, NT])
        a_neg = sb("a_neg", [P, H])
        ncs = sb("ncs", [P, NT])
        sp = sb("sp", [P, 6, NT])
        dec = sb("dec", [P, H])
        wv = sb("wv", [P, 2, H])
        g_last = sb("g_last", [P, 2, H])

        PS = ctx.enter_context(nc.psum_tensor("PS", [P, 8, 512], F32))
        B_FO, B_WO, B_TA, B_TB, B_G, B_CS, B_YT, B_SS = range(8)

        def bank(b):
            return PS[:, b, :]

        def heads(b):
            return PS[:, b, :].rearrange("p (h q) -> p h q", h=H)

        def blocks(b):
            return PS[:, b, :].rearrange("p (k t) -> p k t", k=KB)

        def chunk_of(t, c):
            return t[:, bass.ds(at(c), 1), :].rearrange("p o n -> p (o n)")

        def tokens_of(t, c):
            return t[:, :, bass.ds(at(c * P), P)]

        s_x = [sem(f"s_x{j}") for j in range(CH)]
        s_q = sem("s_q"); s_la = sem("s_la"); s_small = sem("s_small")
        s_win = sem("s_win"); s_wout = sem("s_wout"); s_raw = sem("s_raw")
        s_o = [sem(f"s_o{k}") for k in range(2)]
        e_const = sem("e_const"); e_lora = sem("e_lora"); e_prep = sem("e_prep")
        e_max = sem("e_max"); e_all = sem("e_all"); e_scale = sem("e_scale"); e_whi = sem("e_whi"); e_wlo = sem("e_wlo")
        e_aexp = sem("e_aexp"); e_dve = sem("e_dve"); e_pool = sem("e_pool")
        spare = {n: sem("e_spare_" + n) for n in ("vector", "gpsimd")}
        names = ("st0 ve0 r0 n0 xb t0 hi0 lo0 f x1 st1 ve1 lc rr hn t1 hi1 lo1 mrc "
                 "pi cva hst tapx tap tnh sl dtm spx dtp spu dta csm ncs "
                 "bx bxc cs msk lex dcx wv ecs gl g Sm Sd cp xd yt y ss stt "
                 "n1 wo x2 sq ms r2 h2n t2 hi2 lo2 xsd").split()
        E = {n: sem("e_" + n) for n in names}
        for n in "gu tnb vb pr hib lob d dev wa wb whb fdx mxb alb scx scb dsx dsc".split():
            E[n] = sem("b_" + n)
        for n in "ve r n t hi lo f xb o st".split():
            E["c_" + n] = sem("c_" + n)
        FIRST = 2
        STARTED = {"vector": "x2 y stt lo2 Sm c_o".split(), "gpsimd": ["xsd"], "scalar": [],
                   "tensor": "yt ss t2".split()}
        W = {n: (s, FIRST if any(n in of for of in STARTED.values()) else 0) for n, s in E.items()}

        def start(eng, which):
            for n in STARTED[which]:
                eng.sem_inc(E[n], FIRST)

        def apart(eng):
            eng.sem_inc(spare["vector" if eng is nc.vector else "gpsimd"], 1)

        block = ctx.enter_context(nc.Block())

        @block.sync
        def _(sp_):
            def load_x(c, j):
                sp_.dma_start(x_t[:, j, :], x_in[bass.ds(at(c * P), P), :]).then_inc(s_x[j], 16)

            for k in range(2):
                sp_.sem_inc(s_o[k], 16)
            load_x(0, 0)
            sp_.dma_start(q_raw, q_t.rearrange("(k p) n -> p k n", p=P)).then_inc(s_q, 16)
            for g in range(2):
                rows = slice(g * GROUP, (g + 1) * GROUP)
                for dst, src in ((z_bc, zeros_t), (s_bc, scales_t)):
                    row = src.rearrange("(k g) n -> g k n", g=2)[g:g + 1, :, :]
                    sp_.dma_start(dst[rows, :, :], row.broadcast_to([GROUP, KB, DM])).then_inc(s_q, 16)
            sp_.dma_start(la[:, :], lora_a).then_inc(s_la, 16)
            sp_.dma_start(lb[:, :], lora_b_t).then_inc(s_la, 16)
            sp_.dma_start(hb[:, :], bias.broadcast_to([P, DM])).then_inc(s_small, 16)
            sp_.dma_start(cw[:, :, :], conv_w.rearrange("(b p) t -> p b t", p=P)).then_inc(s_small, 16)
            sp_.dma_start(cb[:, :], conv_b).then_inc(s_small, 16)
            for dst, src in ((al, a_log), (dsk, d_skip), (dtb, dt_bias)):
                sp_.dma_start(dst[:, :], src.broadcast_to([P, H])).then_inc(s_small, 16)
            sp_.dma_start(ln1[:, :], ln1_w).then_inc(s_small, 16)
            sp_.dma_start(ln2[:, :], ln2_w).then_inc(s_small, 16)
            for j in range(1, CH):
                load_x(j, j)
            sp_.dma_start(raw_in, w_in_t.rearrange("(k p) n -> p k n", p=P)).then_inc(s_win, 16)
            sp_.dma_start(w_out[:, :, :], w_out_t.rearrange("(h p) n -> p h n", p=P)).then_inc(s_wout, 16)

            gate_v = gate_t.rearrange("(k p) f -> p k f", p=P)
            up_v = up_t.rearrange("(k p) f -> p k f", p=P)

            def load_pair(p):
                cols = bass.ds(at(p * PAIR), PAIR)
                sp_.dma_start(raw_gu[:, 0, :, :], gate_v[:, :, cols]).then_inc(s_raw, 16)
                sp_.dma_start(raw_gu[:, 1, :, :], up_v[:, :, cols]).then_inc(s_raw, 16)
                sp_.dma_start(raw_d[:, :, :], down_t[cols, :].rearrange("(b p) n -> p b n", p=P)).then_inc(s_raw, 16)

            load_pair(0)
            with sp_.Fori(1, NS) as reg:
                i = Index(reg, 1)
                for j in range(CH):
                    after(sp_, W["x1"], (i + -1) * CH + (j + 1))
                    load_x(i * CH + j, j)
            with sp_.Fori(1, NP) as reg:
                p = Index(reg, 1)
                after(sp_, W["wb"], p * 2)
                load_pair(p)

            out_v = out
            with sp_.Fori(0, NCH // 2) as reg:
                m = Index(reg, 0)
                for k in range(2):
                    after(sp_, W["c_o"], m * 2 + (k + 1))
                    sp_.dma_start(out_v[bass.ds(at((m * 2 + k) * P), P), :], o_t[k]).then_inc(s_o[k], 16)
            for k in range(2):
                sp_.wait_ge(s_o[k], 16 * (NCH // 2 + 1))

        @block.gpsimd
        def _(po):
            n_self = [0]

            def chain(ins):
                n_self[0] += 1
                ins.then_inc(e_pool, 1)
                po.wait_ge(e_pool, n_self[0])

            start(po, "gpsimd")
            chain(po.memset(ident[:, :], 0.0))
            chain(po.affine_select(out=ident[:, :], in_=ident[:, :], compare_op=ALU.not_equal, fill=1.0,
                                   base=0, pattern=[[-1, P]], channel_multiplier=1))
            chain(po.memset(tri[:, :], 1.0))
            chain(po.affine_select(out=tri[:, :], in_=tri[:, :], compare_op=ALU.is_ge, fill=0.0,
                                   base=0, pattern=[[1, P]], channel_multiplier=-1))
            chain(po.memset(mask[:, :], 0.0))
            chain(po.affine_select(out=mask[:, :], in_=mask[:, :], compare_op=ALU.is_ge, fill=MASKED,
                                   base=0, pattern=[[1, P]], channel_multiplier=-1))
            chain(po.memset(mhalf[:, :], -0.5))
            po.wait_ge(s_small, 16 * 8)
            chain(po.tensor_scalar(hb[:, :], hb[:, :], 0.5, None, ALU.mult))
            for h in range(H):
                chain(po.tensor_scalar(d_diag[:, h, :], ident[:, :], dsk[:, h:h + 1], None, ALU.mult))
            po.sem_inc(e_const, 1)

            def rsqrt(dst, src):
                return po.tensor_tensor(dst, src, mhalf[:, :], ALU.pow)

            def ln0(c, j):
                after(po, W["ve0"], c + 1)
                rsqrt(r0[:, :], mv0[:, 2:3]).then_inc(E["r0"], 1)

            def xb(c, j):
                after(po, W["n0"], c + 1)
                po.tensor_tensor(x_t[:, j, :], x_t[:, j, :], hb[:, :], ALU.add).then_inc(E["xb"], 1)

            def ln1_chain(c, j):
                v = mvN[:, j, 1:2]
                base = c * 4
                after(po, W["ve1"], c + 1)
                rsqrt(rN[:, j:j + 1], mvN[:, j, 2:3]).then_inc(E["lc"], 1)
                after(po, W["lc"], base + 1)
                apart(po)
                po.tensor_scalar(rt[:, 0:1], v, rN[:, j:j + 1], rN[:, j:j + 1], ALU.mult, ALU.mult).then_inc(E["lc"], 1)
                after(po, W["lc"], base + 2)
                apart(po)
                po.tensor_scalar(rt[:, 1:2], rt[:, 0:1], EPS, None, ALU.add).then_inc(E["lc"], 1)
                after(po, W["lc"], base + 3)
                rsqrt(rt[:, 2:3], rt[:, 1:2]).then_inc(E["lc"], 1)
                after(po, W["lc"], base + 4)
                after(po, W["hn"], c)
                po.tensor_tensor(rr[:, :], rN[:, j:j + 1], rt[:, 2:3], ALU.mult).then_inc(E["rr"], 1)

            def scan_help1(c, j):
                cols = slice(j * P, (j + 1) * P)
                after(po, W["ecs"], c + 1)
                after(po, W["g"], c + 1)
                po.tensor_tensor(xbc[:, 2:CB, cols], xbc[:, 2:CB, cols], ecs[:, :, :], ALU.mult).then_inc(E["cp"], 1)
                after(po, W["Sm"], c + 1)
                po.tensor_tensor(S[:, j % 2, :, :], S[:, j % 2, :, :], d_diag[:, :, :], ALU.add).then_inc(E["Sd"], 1)

            def rms2(c, j):
                after(po, W["sq"], c + 1)
                apart(po)
                po.tensor_scalar(rt[:, 3:4], ssq[:, :], 1.0 / DM, EPS, ALU.mult, ALU.add).then_inc(E["ms"], 1)
                after(po, W["ms"], c + 1)
                rsqrt(r2[:, j % 2:j % 2 + 1], rt[:, 3:4]).then_inc(E["r2"], 1)
                after(po, W["x2"], c + 1)
                po.tensor_tensor(chunk_of(xs, c), chunk_of(xs, c), x2[:, j % 2, :], ALU.add).then_inc(E["xsd"], 1)

            def body(i, scan, nxt):
                if nxt:
                    n = (i + 1) * CH
                    ln0(n, 0); xb(n, 0)
                for j in range(CH):
                    c = i * CH + j
                    if scan and j < CH - 1:
                        scan_help1(c + 1, j + 1)
                    if nxt and j < CH - 1:
                        ln0(n + (j + 1), j + 1); xb(n + (j + 1), j + 1)
                    if nxt:
                        ln1_chain(n + j, j)
                    if scan:
                        rms2(c, j)
                if nxt:
                    if not scan:
                        resident_max(1)
                    scan_help1(n, 0)

            def resident_max(n):
                po.wait_ge(e_max, n + 1)
                po.partition_all_reduce(mxa[:, n:n + 1], mx[:, n:n + 1], P, bass.bass_isa.ReduceOp.max).then_inc(e_all, 1)

            def pair_max(p):
                after(po, W["mxb"], p + 1)
                apart(po)
                po.partition_all_reduce(mxa3[:, :], mx3[:, :], P, bass.bass_isa.ReduceOp.max).then_inc(E["alb"], 1)

            resident_max(0)
            body(-1, False, True)
            with po.Fori(0, NS - 1) as reg:
                body(Index(reg, 0), True, True)
            body(NS - 1, True, False)
            pair_max(0)
            with po.Fori(1, NP) as reg:
                pair_max(Index(reg, 1))

            def c_norm(c, k):
                after(po, W["c_ve"], c + 1)
                rsqrt(rN[:, k:k + 1], mvN[:, k, 2:3]).then_inc(E["c_r"], 1)
                after(po, W["c_n"], c + 1)
                po.tensor_tensor(chunk_of(xs, c), chunk_of(xs, c), hb[:, :], ALU.add).then_inc(E["c_xb"], 1)

            with po.Fori(0, NCH // 2) as reg:
                for k in range(2):
                    c_norm(Index(reg, 0) * 2 + k, k)

        @block.scalar
        def _(ac):
            ac.wait_ge(s_small, 16 * 8)
            ac.activation(a_neg[:, :], al[:, :], ACT.Exp).then_inc(e_aexp, 1)
            ac.wait_ge(e_scale, 1)
            ac.activation(w_ffn[0][:, :, :], wf, ACT.Copy, scale=sw[:, 0:1]).then_inc(e_whi, 1)

            def w_in_hi():
                ac.wait_ge(e_scale, 2)
                ac.activation(w_in[0][:, :, :], raw_in, ACT.Copy, scale=sw[:, 1:2]).then_inc(e_whi, 1)

            def hi0(c, j):
                after(ac, W["t0"], c + 1)
                after(ac, W["f"], c + -1)
                ac.activation(nT[j % 2][0], blocks(B_TA), ACT.Copy, scale=ACT_SCALE).then_inc(E["hi0"], 1)

            def hi1(c, j):
                after(ac, W["t1"], c + 1)
                ac.activation(hT[0][:, :, j * P:(j + 1) * P], blocks(B_TA), ACT.Copy, scale=ACT_SCALE).then_inc(E["hi1"], 1)

            def hi2(c):
                after(ac, W["t2"], c + 1)
                ac.activation(tokens_of(h2T[0], c), blocks(B_TB), ACT.Copy, scale=ACT_SCALE).then_inc(E["hi2"], 1)

            def norm2(c, j):
                after(ac, W["r2"], c + 1)
                after(ac, W["t2"], c)
                ac.activation(h2n[:, :], x2[:, j % 2, :], ACT.Copy, scale=r2[:, j % 2:j % 2 + 1]).then_inc(E["h2n"], 1)

            def square(c, j):
                after(ac, W["x2"], c + 1)
                ac.activation(junk[:, :], x2[:, j % 2, :], ACT.Square, accum_out=ssq[:, :]).then_inc(E["sq"], 1)

            def scan1(c, j):
                s = j % 2
                after(ac, W["bx"], c + 1)
                after(ac, W["ss"], c + -1)
                ac.activation(tm[:, s, :, :], PS[:, B_TB, 0:2 * P].rearrange("p (a t) -> p a t", a=2), ACT.Copy).then_inc(E["bxc"], 1)
                after(ac, W["msk"], c + 1)
                ac.activation(dec[:, :], dec[:, :], ACT.Exp).then_inc(E["dcx"], 1)
                for h in range(H):
                    last = ac.activation(Ld[:, h, :], Ld[:, h, :], ACT.Exp, bias=ncs[:, j * H + h:j * H + h + 1])
                last.then_inc(E["lex"], 1)
                after(ac, W["cp"], c)
                ac.activation(ecs[:, :, :], heads(B_CS), ACT.Exp).then_inc(E["ecs"], 1)
                ac.activation(g_last[:, s, :], heads(B_CS)[:, :, P - 1:P].rearrange("p h o -> p (h o)"), ACT.Exp).then_inc(E["gl"], 1)

            def scan2(c, j):
                s = j % 2
                after(ac, W["wv"], c + 1)
                for h in range(H):
                    last = ac.activation(xds[:, s, h, :], tm[:, s, 0, :], ACT.Copy, scale=wv[:, s, h:h + 1])
                last.then_inc(E["xd"], 1)

            def conv(i, b):
                w = b % 2
                after(ac, W["pi"], i * (CB + ZB) + (b + 1))
                after(ac, W["tap"], i * CB + (b - 1))
                after(ac, W["hst"], i * CB + (b + 1 - CB))
                ac.activation(pre[:, w, 0:NTAP - 1], hist[:, b, :], ACT.Copy)
                ac.activation(pre[:, w, NTAP - 1:], bank(B_G + w), ACT.Copy)
                last = ac.activation(xbc[:, b, :], bank(B_G + w), ACT.Identity, scale=cw[:, b, NTAP - 1:NTAP], bias=cb[:, b:b + 1])
                last.then_inc(E["cva"], 1)
                after(ac, W["cva"], i * CB + (b + 1))
                ac.activation(hist[:, b, :], pre[:, w, ST:], ACT.Copy).then_inc(E["hst"], 1)

            def tanh(i, b):
                n = i * (CB + ZB) + b
                after(ac, W["sl"], n + -1)
                if b < CB:
                    after(ac, W["tap"], i * CB + (b + 1))
                    ac.activation(th[:, b % 2, :], xbc[:, b, :], ACT.Tanh).then_inc(E["tnh"], 1)
                else:
                    after(ac, W["pi"], n + 1)
                    ac.activation(th[:, b % 2, :], bank(B_G + b % 2), ACT.Tanh, scale=d_ih[:, :]).then_inc(E["tnh"], 1)

            def win(i, scan):
                conv(i, 0)
                if scan:
                    norm2(i * CH + -1, CH - 1)
                conv(i, 1)
                tanh(i, 0)
                if scan:
                    hi2(i * CH + -1)
                for b in range(2, CB):
                    conv(i, b)
                    tanh(i, b - 1)
                tanh(i, CB - 1)
                after(ac, W["dtp"], i + 1)
                ac.activation(sp[:, 2, :], sp[:, 1, :], ACT.Exp).then_inc(E["spu"], 1)
                for b in range(CB, CB + ZB):
                    tanh(i, b)

            def body(i, scan, nxt):
                if nxt:
                    n = (i + 1) * CH
                for j in range(CH):
                    c = i * CH + j
                    if scan and j < CH - 1:
                        scan1(c + 1, j + 1)
                    if scan and j:
                        norm2(c + -1, j - 1)
                    if nxt:
                        hi0(n + j, j)
                    if scan and j < CH - 1:
                        scan2(c + 1, j + 1)
                    if nxt and j:
                        hi1(n + (j - 1), j - 1)
                    if scan:
                        if j:
                            hi2(c + -1)
                        square(c, j)
                if nxt:
                    hi1(n + (CH - 1), CH - 1)
                    if not scan:
                        w_in_hi()
                    win(i + 1, scan)
                    scan1(n, 0)
                    scan2(n, 0)
                else:
                    norm2(c, CH - 1)
                    hi2(c)

            body(-1, False, True)
            with ac.Fori(0, NS - 1) as reg:
                body(Index(reg, 0), True, True)
            body(NS - 1, True, False)

            def hi_gu(x):
                for g in range(2):
                    last = ac.activation(w_gu[0][:, g, :, x * P:(x + 1) * P], raw_gu[:, g, :, x * P:(x + 1) * P], ACT.Copy, scale=sw3[:, g:g + 1])
                return last

            def cut_a(p):
                after(ac, W["scb"], p + 1)
                after(ac, W["gu"], p * (2 * NS) + (-NS))
                hi_gu(0).then_inc(E["whb"], 1)

            def cut_b(p):
                after(ac, W["gu"], p * (2 * NS))
                after(ac, W["d"], p * (NS * CH))
                hi_gu(1)
                ac.activation(w_dn[0], raw_d[:, :, :], ACT.Copy, scale=sw3[:, 2:3]).then_inc(E["whb"], 1)

            def step(p, k):
                s = p * (2 * NS) + k
                after(ac, W["gu"], s + 1)
                after(ac, W["dsc"], p + 1)
                ac.activation(gt[:, k % 2, :], bank(2 * (k % 2)), ACT.Tanh, scale=dgh[:, :]).then_inc(E["tnb"], 1)
                after(ac, W["pr"], s + 1)
                if k >= NS:
                    i = k - NS
                    if i >= 2:
                        after(ac, W["d"], p * (NS * CH) + (i - 1) * CH)
                    dst = mB[0][:, i % 2, :]
                else:
                    dst = mA[0][:, k, :]
                ac.activation(dst, gp[:, k % 2, :], ACT.Copy).then_inc(E["hib"], 1)

            def pair(p, nxt):
                for k in range(2 * NS):
                    step(p, k)
                    if k == 0:
                        cut_b(p)
                    if nxt and k == 2 * NS - 2:
                        cut_a(p + 1)

            cut_a(0)
            pair(0, True)
            with ac.Fori(1, NP - 1) as reg:
                pair(Index(reg, 1), True)
            pair(NP - 1, False)

            def c_hi(c, k):
                after(ac, W["c_t"], c + 1)
                after(ac, W["c_f"], c + -1)
                ac.activation(cT[k][0], blocks(k), ACT.Copy, scale=ACT_SCALE).then_inc(E["c_hi"], 1)

            c_hi(0, 0)
            c_hi(1, 1)
            with ac.Fori(1, NCH // 2) as reg:
                for k in range(2):
                    c_hi(Index(reg, 1) * 2 + k, k)

        @block.vector
        def _(ve):
            n_self = [0]

            def chain(ins):
                n_self[0] += 1
                ins.then_inc(e_dve, 1)
                ve.wait_ge(e_dve, n_self[0])

            def link(ins, s, count):
                ins.then_inc(s, 1)
                after(ve, (s, 0), count)

            start(ve, "vector")
            chain(ve.memset(hist[:, :, :], 0.0))
            chain(ve.memset(state[:, :, :], 0.0))

            def power_of_two(pw_, sw_, top, link_):
                link_(ve.tensor_scalar(top, top, TINY, None, ALU.max))
                link_(ve.tensor_scalar(pw_.bitcast(I32), top.bitcast(I32), 0x7F800000, None, ALU.bitwise_and))
                link_(ve.tensor_scalar(sw_.bitcast(I32), pw_.bitcast(I32), 0x7F800000, None, ALU.bitwise_xor))
                link_(ve.tensor_scalar(sw_, sw_, 2.0 ** (W_TOP - 1), None, ALU.mult))

            def stats(src, mv, stat, e_link, base, e_ve):
                apart(ve)
                link(ve.bn_stats(stat, src), e_link, base + 1)
                apart(ve)
                link(ve.bn_aggr(mv[:, 0:2], stat), e_link, base + 2)
                ve.tensor_scalar(mv[:, 2:3], mv[:, 1:2], EPS, None, ALU.add).then_inc(e_ve, 1)

            def prep0(c, j):
                after(ve, s_x[j], (c * 1 + (CH - j)) * (16 // CH))
                stats(x_t[:, j, :], mv0[:, :], st6[:, 0, :], E["st0"], c * 2, E["ve0"])

            def norm0(c, j):
                after(ve, W["r0"], c + 1)
                after(ve, W["t0"], c)
                ve.tensor_scalar(n0[:, :], x_t[:, j, :], mv0[:, 0:1], r0[:, :], ALU.subtract, ALU.mult).then_inc(E["n0"], 1)

            ve.wait_ge(s_q, 16 * 5)
            chain(ve.tensor_tensor(wf, q_raw, z_bc, ALU.subtract))
            chain(ve.tensor_tensor(wf, wf, s_bc, ALU.mult))
            ve.wait_ge(e_lora, 1)
            for k in range(KB):
                chain(ve.scalar_tensor_tensor(wf[:, k, :], bank(B_G + k), LORA_SCALE, wf[:, k, :], ALU.mult, ALU.add))
            ve.tensor_reduce(mx[:, 0:1], wf, mybir.AxisListType.XY, ALU.max, apply_absolute_value=True).then_inc(e_max, 1)
            ve.wait_ge(e_all, 1)
            power_of_two(pw[:, 0:1], sw[:, 0:1], mxa[:, 0:1], chain)
            ve.sem_inc(e_scale, 1)
            chain(ve.tensor_scalar(d_f[:, :], pw[:, 0:1], 0.5 * 2.0 ** -W_TOP / ACT_SCALE, None, ALU.mult))
            prep0(0, 0)
            ve.wait_ge(e_whi, 1)
            ve.scalar_tensor_tensor(w_ffn[1][:, :, :].rearrange("p k n -> p (k n)"), wf.rearrange("p k n -> p (k n)"),
                                    sw[:, 0:1], w_ffn[0][:, :, :].rearrange("p k n -> p (k n)"),
                                    ALU.mult, ALU.subtract).then_inc(e_wlo, 1)

            def w_in_scales():
                ve.wait_ge(s_win, 16)
                ve.wait_ge(s_small, 16 * 8)
                for k in range(KB):
                    chain(ve.tensor_scalar(raw_in[:, k, :], raw_in[:, k, :], ln1[:, k:k + 1], None, ALU.mult))
                ve.tensor_reduce(mx[:, 1:2], raw_in, mybir.AxisListType.XY, ALU.max, apply_absolute_value=True).then_inc(e_max, 1)
                ve.wait_ge(e_all, 2)
                power_of_two(pw[:, 1:2], sw[:, 1:2], mxa[:, 1:2], chain)
                ve.sem_inc(e_scale, 1)
                chain(ve.tensor_scalar(d_i[:, :], pw[:, 1:2], 2.0 ** -W_TOP / ACT_SCALE, None, ALU.mult))
                chain(ve.tensor_scalar(d_ih[:, :], d_i[:, :], 0.5, None, ALU.mult))
                chain(ve.tensor_scalar(cw[:, :, :], cw[:, :, :], d_ih[:, :], None, ALU.mult))
                chain(ve.tensor_scalar(cb[:, :], cb[:, :], 0.5, None, ALU.mult))
                ve.wait_ge(e_aexp, 1)
                chain(ve.tensor_scalar(a_neg[:, :], a_neg[:, :], -1.0, None, ALU.mult))

            def w_in_lo():
                ve.wait_ge(e_whi, 2)
                ve.scalar_tensor_tensor(w_in[1][:, :, :].rearrange("p k n -> p (k n)"), raw_in.rearrange("p k n -> p (k n)"),
                                        sw[:, 1:2], w_in[0][:, :, :].rearrange("p k n -> p (k n)"),
                                        ALU.mult, ALU.subtract).then_inc(e_wlo, 1)

            def lo(dst, src_bank, hi):
                return ve.scalar_tensor_tensor(dst, blocks(src_bank), ACT_SCALE, hi, ALU.mult, ALU.subtract)

            def lo0(c, j):
                after(ve, W["hi0"], c + 1)
                lo(nT[j % 2][1], B_TA, nT[j % 2][0]).then_inc(E["lo0"], 1)

            def lo1(c, j):
                after(ve, W["hi1"], c + 1)
                cols = slice(j * P, (j + 1) * P)
                lo(hT[1][:, :, cols], B_TA, hT[0][:, :, cols]).then_inc(E["lo1"], 1)

            def lo2(c):
                after(ve, W["hi2"], c + 1)
                lo(tokens_of(h2T[1], c), B_TB, tokens_of(h2T[0], c)).then_inc(E["lo2"], 1)

            def x1_stats(c, j):
                after(ve, W["f"], c + 1)
                after(ve, W["xb"], c + 1)
                link(ve.scalar_tensor_tensor(chunk_of(xs, c), bank(B_FO), d_f[:, :], x_t[:, j, :], ALU.mult, ALU.add),
                     E["x1"], c + 1)
                stats(chunk_of(xs, c), mvN[:, j, :], st6[:, 1, :], E["st1"], c * 2, E["ve1"])

            def norm1(c, j):
                after(ve, W["rr"], c + 1)
                after(ve, W["t1"], c)
                ve.tensor_scalar(hn[:, :], chunk_of(xs, c), mvN[:, j, 0:1], rr[:, :], ALU.subtract, ALU.mult).then_inc(E["hn"], 1)

            def masked(c, j):
                after(ve, W["cs"], c + 1)
                after(ve, W["Sm"], c)
                ve.tensor_tensor(Ld[:, :, :], heads(B_CS), mask[:, :].unsqueeze(1).broadcast_to([P, H, P]), ALU.add)
                ve.tensor_tensor(dec[:, :], heads(B_CS)[:, :, P - 1:P].rearrange("p h o -> p (h o)"), ncs[:, j * H:(j + 1) * H], ALU.add).then_inc(E["msk"], 1)

            def scan1(c, j):
                s = j % 2
                after(ve, W["dcx"], c + 1)
                ve.tensor_tensor(wv[:, s, :], dec[:, :], dt[:, j * H:(j + 1) * H], ALU.mult).then_inc(E["wv"], 1)
                after(ve, W["g"], c + 1)
                after(ve, W["lex"], c + 1)
                after(ve, W["yt"], c + -1)
                for h in range(H):
                    last = ve.scalar_tensor_tensor(S[:, s, h, :], heads(B_G)[:, h, :], dt[:, j * H + h:j * H + h + 1], Ld[:, h, :],
                                                   ALU.mult, ALU.mult)
                last.then_inc(E["Sm"], 1)

            def scan2(c, j):
                s = j % 2
                cols = slice(j * P, (j + 1) * P)
                after(ve, W["yt"], c + 1)
                ve.scalar_tensor_tensor(szs[:, :, cols], heads(B_YT), d_ih[:, :], szs[:, :, cols], ALU.mult, ALU.mult).then_inc(E["y"], 1)
                after(ve, W["ss"], c + 1)
                after(ve, W["gl"], c + 1)
                for h in range(H):
                    last = ve.scalar_tensor_tensor(state[:, h, :], state[:, h, :], g_last[:, s, h:h + 1], heads(B_SS)[:, h, :],
                                                   ALU.mult, ALU.add)
                last.then_inc(E["stt"], 1)

            def residual2(c, j):
                after(ve, W["x2"], c)
                link(ve.tensor_scalar(n1[:, :], chunk_of(xs, c), muC[:, j:j + 1], rC[:, j:j + 1], ALU.subtract, ALU.mult),
                     E["n1"], c + 1)
                after(ve, W["wo"], c + 1)
                after(ve, W["xsd"], c + -1)
                ve.tensor_tensor(x2[:, j % 2, :], n1[:, :], bank(B_WO), ALU.add).then_inc(E["x2"], 1)

            def taps(i, b):
                w = b % 2
                after(ve, W["cva"], i * CB + (b + 1))
                base = (i * CB + b) * 2
                for k in range(NTAP - 1):
                    ins = ve.scalar_tensor_tensor(xbc[:, b, :], pre[:, w, k:k + ST], cw[:, b, k:k + 1], xbc[:, b, :],
                                                  ALU.mult, ALU.add)
                    if k < NTAP - 2:
                        link(ins, E["tapx"], base + (k + 1))
                ins.then_inc(E["tap"], 1)

            def silu(i, b):
                after(ve, W["tnh"], i * (CB + ZB) + (b + 1))
                if b < CB:
                    dst, v = xbc[:, b, :], xbc[:, b, :]
                else:
                    dst, v = szs[:, b - CB, :], bank(B_G + b % 2)
                ve.scalar_tensor_tensor(dst, th[:, b % 2, :], 1.0, v, ALU.add, ALU.mult).then_inc(E["sl"], 1)

            N_SP = 16

            def softplus(i):
                base = i * N_SP
                n = [0]

                def lk(ins):
                    n[0] += 1
                    link(ins, E["spx"], base + n[0])

                v, m, u, s1, s2, q = (sp[:, k, :] for k in range(6))

                def rep(t):
                    return t[:, :].unsqueeze(1).broadcast_to([P, CH, H])

                def four(t):
                    return t.rearrange("p (c h) -> p c h", c=CH)

                after(ve, W["dtm"], i + 1)
                lk(ve.scalar_tensor_tensor(four(v), four(PS[:, B_SS, 0:NT]), d_i[:, :], rep(dtb), ALU.mult, ALU.add))
                lk(ve.tensor_scalar(m, v, -1.0, None, ALU.mult))
                ve.tensor_tensor(m, m, v, ALU.min).then_inc(E["dtp"], 1)
                after(ve, W["spu"], i + 1)
                lk(ve.tensor_scalar(s1, u, 2.0, None, ALU.add))
                lk(ve.reciprocal(s2, s1))
                lk(ve.tensor_tensor(s1, u, s2, ALU.mult))
                lk(ve.tensor_tensor(s2, s1, s1, ALU.mult))
                lk(ve.tensor_scalar(q, s2, 1.0 / 15, None, ALU.mult))
                for k in (13, 11, 9, 7, 5, 3):
                    lk(ve.scalar_tensor_tensor(q, q, 1.0 / k, s2, ALU.add, ALU.mult))
                lk(ve.scalar_tensor_tensor(q, q, 1.0, s1, ALU.add, ALU.mult))
                lk(ve.tensor_scalar(v, v, 0.0, None, ALU.max))
                lk(ve.scalar_tensor_tensor(dt[:, :], q, 2.0, v, ALU.mult, ALU.add))
                assert n[0] == N_SP, n[0]
                ve.tensor_tensor(four(dA[:, :]), four(dt[:, :]), rep(a_neg), ALU.mult).then_inc(E["dta"], 1)

            def win(i, scan):
                taps(i, 0)
                taps(i, 1)
                silu(i, 0)
                if scan:
                    lo2(i * CH + -1)
                for b in range(2, CB):
                    taps(i, b)
                    silu(i, b - 1)
                silu(i, CB - 1)
                softplus(i)
                for b in range(CB, CB + ZB):
                    silu(i, b)
                after(ve, W["csm"], i + 1)
                link(ve.tensor_scalar(ncs[:, :], PS[:, B_YT, 0:NT], -1.0, None, ALU.mult), E["ncs"], i + 1)

            def body(i, scan, nxt):
                if nxt:
                    n = (i + 1) * CH
                    if scan:
                        prep0(n, 0)
                    norm0(n, 0)
                for j in range(CH):
                    c = i * CH + j
                    if scan and j < CH - 1:
                        masked(c + 1, j + 1)
                    if nxt:
                        lo0(n + j, j)
                        if j < CH - 1:
                            prep0(n + (j + 1), j + 1)
                    if scan and j < CH - 1:
                        scan1(c + 1, j + 1)
                    if nxt:
                        if j < CH - 1:
                            norm0(n + (j + 1), j + 1)
                        x1_stats(n + j, j)
                    if scan:
                        scan2(c, j)
                    if nxt and j:
                        lo1(n + (j - 1), j - 1)
                    if scan:
                        residual2(c, j)
                    if nxt:
                        norm1(n + j, j)
                    if scan and j:
                        lo2(c + -1)
                if nxt:
                    if not scan:
                        w_in_scales()
                    lo1(n + (CH - 1), CH - 1)
                    if not scan:
                        w_in_lo()
                    after(ve, W["rr"], n + CH)
                    ve.tensor_copy(muC[:, :], mvN[:, :, 0:1].rearrange("p c o -> p (c o)"))
                    link(ve.tensor_copy(rC[:, :], rN[:, :]), E["mrc"], i + 2)
                    win(i + 1, scan)
                    masked(n, 0)
                    scan1(n, 0)
                else:
                    lo2(c)

            body(-1, False, True)
            with ve.Fori(0, NS - 1) as reg:
                body(Index(reg, 0), True, True)
            body(NS - 1, True, False)

            N_FOLD = 4

            def fold(p):
                after(ve, s_raw, (p + 1) * 48)
                lnb = ln2[:, :].unsqueeze(2).broadcast_to([P, KB, PAIR])
                base = p * 2
                for g in range(2):
                    link(ve.tensor_tensor(raw_gu[:, g, :, :], raw_gu[:, g, :, :], lnb, ALU.mult), E["fdx"], base + (g + 1))
                for g in range(2):
                    ve.tensor_reduce(mx3[:, g:g + 1], raw_gu[:, g, :, :], mybir.AxisListType.XY, ALU.max, apply_absolute_value=True)
                ve.tensor_reduce(mx3[:, 2:3], raw_d[:, :, :], mybir.AxisListType.XY, ALU.max, apply_absolute_value=True).then_inc(E["mxb"], 1)

            def scales(p):
                n = [0]

                def lk(ins):
                    n[0] += 1
                    link(ins, E["scx"], p * 4 + n[0])

                after(ve, W["alb"], p + 1)
                power_of_two(pw3[:, :], sw3[:, :], mxa3[:, :], lk)
                assert n[0] == 4
                ve.sem_inc(E["scb"], 1)

            def lo_gu(x):
                cols = slice(x * P, (x + 1) * P)
                for g in range(2):
                    last = ve.scalar_tensor_tensor(w_gu[1][:, g, :, cols], raw_gu[:, g, :, cols], sw3[:, g:g + 1], w_gu[0][:, g, :, cols],
                                                   ALU.mult, ALU.subtract)
                return last

            def cut_a(p):
                after(ve, W["whb"], p * 2 + 1)
                lo_gu(0).then_inc(E["wa"], 1)

            def cut_b(p):
                after(ve, W["whb"], p * 2 + 2)
                lo_gu(1).then_inc(E["wb"], 1)
                ve.scalar_tensor_tensor(w_dn[1].rearrange("p b n -> p (b n)"), raw_d[:, :, :].rearrange("p b n -> p (b n)"), sw3[:, 2:3],
                                        w_dn[0].rearrange("p b n -> p (b n)"), ALU.mult, ALU.subtract).then_inc(E["wb"], 1)

            def descale(p):
                back = 2.0 ** -W_TOP / ACT_SCALE
                ve.tensor_scalar(dgh[:, :], pw3[:, 0:1], 0.5 * back, None, ALU.mult)
                link(ve.tensor_scalar(d_tmp[:, :], pw3[:, 0:1], pw3[:, 1:2], pw3[:, 2:3], ALU.mult, ALU.mult), E["dsx"], p + 1)
                ve.tensor_scalar(d_d[:, :], d_tmp[:, :], 0.5 * back * back / GATED_SCALE * 2.0 ** -W_TOP, None, ALU.mult).then_inc(E["dsc"], 1)

            def step(p, k):
                s = p * (2 * NS) + k
                w = k % 2
                after(ve, W["tnb"], s + 1)
                link(ve.scalar_tensor_tensor(gt[:, w, :], gt[:, w, :], 1.0, bank(2 * w), ALU.add, ALU.mult), E["vb"], s + 1)
                ve.scalar_tensor_tensor(gp[:, w, :], gt[:, w, :], GATED_SCALE, bank(2 * w + 1), ALU.mult, ALU.mult).then_inc(E["pr"], 1)
                after(ve, W["hib"], s + 1)
                hi, lo_ = (mB[0][:, k % 2, :], mB[1][:, k % 2, :]) if k >= NS else (mA[0][:, k, :], mA[1][:, k, :])
                ve.tensor_tensor(lo_, gp[:, w, :], hi, ALU.subtract).then_inc(E["lob"], 1)

            def down(p, i):
                for t in range(CH):
                    after(ve, W["d"], p * (NS * CH) + (i * CH + t + 1))
                    c = i * CH + t
                    ve.scalar_tensor_tensor(xs[:, c, :], bank(4 + t), d_d[:, :], xs[:, c, :], ALU.mult, ALU.add).then_inc(E["dev"], 1)

            def pair(p, nxt):
                descale(p)
                for k in range(2 * NS):
                    if k >= NS + 2:
                        down(p, k - NS - 2)
                    step(p, k)
                    if k == 0:
                        cut_b(p)
                    if nxt and k == NS:
                        fold(p + 1)
                    if nxt and k == NS + 1:
                        scales(p + 1)
                    if nxt and k == 2 * NS - 2:
                        cut_a(p + 1)
                down(p, NS - 2)
                down(p, NS - 1)

            fold(0)
            scales(0)
            cut_a(0)
            after(ve, W["xsd"], NCH)
            pair(0, True)
            with ve.Fori(1, NP - 1) as reg:
                pair(Index(reg, 1), True)
            pair(NP - 1, False)

            def c_prep(c, k):
                after(ve, W["c_xb"], c + -1)
                stats(chunk_of(xs, c), mvN[:, k, :], st6[:, k, :], E["c_st"], c * 2, E["c_ve"])
                after(ve, W["c_r"], c + 1)
                after(ve, W["c_t"], c + -1)
                ve.tensor_scalar(c_n[k][:, :], chunk_of(xs, c), mvN[:, k, 0:1], rN[:, k:k + 1], ALU.subtract, ALU.mult).then_inc(E["c_n"], 1)

            def c_lo(c, k):
                after(ve, W["c_hi"], c + 1)
                lo(cT[k][1], k, cT[k][0]).then_inc(E["c_lo"], 1)

            def c_out(c, k, first):
                after(ve, W["c_f"], c + 1)
                after(ve, W["c_xb"], c + 1)
                if not first:
                    after(ve, s_o[k], (c + (2 - k)) * 8)
                ve.scalar_tensor_tensor(o_t[k], bank(2 + k), d_f[:, :], chunk_of(xs, c), ALU.mult, ALU.add).then_inc(E["c_o"], 1)

            ve.wait_ge(E["dev"], NP * NCH)
            c_prep(0, 0)
            c_lo(0, 0)
            c_prep(1, 1)
            c_lo(1, 1)
            c_out(0, 0, True)
            with ve.Fori(1, NCH // 2) as reg:
                c = Index(reg, 1) * 2
                c_prep(c, 0)
                c_lo(c, 0)
                c_out_prev = c + -1
                after(ve, W["c_f"], c_out_prev + 1)
                after(ve, W["c_xb"], c_out_prev + 1)
                after(ve, s_o[1], c * 8)
                ve.scalar_tensor_tensor(o_t[1], bank(3), d_f[:, :], chunk_of(xs, c_out_prev), ALU.mult, ALU.add).then_inc(E["c_o"], 1)
                c_prep(c + 1, 1)
                c_lo(c + 1, 1)
                c_out(c, 0, False)
            c_out(NCH - 1, 1, False)

        @block.tensor
        def _(pe):
            start(pe, "tensor")

            def transpose4(b, src):
                for k in range(KB):
                    last = pe.transpose(blocks(b)[:, k, :], src[:, k * P:(k + 1) * P], ident[:, :])
                return last

            def product(out_, lhs, rhs, n_k, first=True, last=True):
                todo = [(k, a, b) for k in range(n_k) for a, b in PARTS]
                for n, (k, a, b) in enumerate(todo):
                    ins = pe.matmul(out_, lhs(a, b, k), rhs(a, b, k), start=first and n == 0, stop=last and n == len(todo) - 1)
                return ins

            pe.wait_ge(s_la, 32)
            for k in range(KB):
                last = pe.matmul(bank(B_G + k), la[:, k * P:(k + 1) * P], lb[:, :], start=True, stop=True)
            last.then_inc(e_lora, 1)
            pe.wait_ge(e_const, 1)

            def t0(c, j):
                after(pe, W["n0"], c + 1)
                if j >= 2:
                    after(pe, W["lo1"], c + -1)
                transpose4(B_TA, n0).then_inc(E["t0"], 1)

            def f(c, j):
                after(pe, W["lo0"], c + 1)
                after(pe, W["x1"], c)
                product(bank(B_FO), lambda a, b, k: nT[j % 2][a][:, k, :], lambda a, b, k: w_ffn[b][:, k, :], KB).then_inc(E["f"], 1)

            def t1(c, j):
                after(pe, W["hn"], c + 1)
                after(pe, W["lo1"], c)
                transpose4(B_TA, hn).then_inc(E["t1"], 1)

            def t2(c, scans_copied):
                after(pe, W["h2n"], c + 1)
                after(pe, W["bxc"], scans_copied)
                after(pe, W["lo2"], c)
                transpose4(B_TB, h2n).then_inc(E["t2"], 1)

            col_of = [DI + b * P for b in range(CB)] + [h * P for h in range(ZB)]

            def win(i, scan):
                NB = CB + ZB
                after(pe, W["lo1"], i * CH + CH)
                for b in range(NB):
                    if b == 0:
                        after(pe, W["Sm"], i * CH)
                    elif b == 1:
                        after(pe, W["gl"], i * CH)
                    elif b < CB + 2:
                        after(pe, W["cva"], i * CB + (b - 1))
                    else:
                        after(pe, W["sl"], i * NB + (b - 1))
                    product(bank(B_G + b % 2), lambda a, q, k: w_in[q][:, k, col_of[b]:col_of[b] + P], lambda a, q, k: hT[a][:, k, :], KB).then_inc(E["pi"], 1)
                    if scan and b == 1:
                        t2(i * CH + -1, i * CH)
                    if b == CB - 1:
                        after(pe, W["stt"], i * CH)
                        for j in range(CH):
                            last = product(PS[:, B_SS, j * H:(j + 1) * H], lambda a, q, k: hT[a][:, k, j * P:(j + 1) * P],
                                           lambda a, q, k: w_in[q][:, k, NPROJ - H:NPROJ], KB)
                        last.then_inc(E["dtm"], 1)
                after(pe, W["dta"], i + 1)
                after(pe, W["y"], i * CH)
                pe.matmul(PS[:, B_YT, 0:NT], tri[:, :], dA[:, :], start=True, stop=True).then_inc(E["csm"], 1)

            def s1(c, i, j):
                cols = slice(j * P, (j + 1) * P)
                if j == 0:
                    after(pe, W["sl"], (i + 1) * (CB + ZB))
                after(pe, W["bxc"], c)
                if j == 0:
                    after(pe, W["lo2"], c)
                if j == CH - 1:
                    after(pe, W["lo2"], c + -2)
                for n in range(2):
                    last = pe.transpose(PS[:, B_TB, n * P:(n + 1) * P], xbc[:, n, cols], ident[:, :])
                last.then_inc(E["bx"], 1)
                after(pe, W["gl"], c)
                for h in range(H):
                    n = j * H + h
                    last = pe.matmul(heads(B_CS)[:, h, :], dA[:, n:n + 1].broadcast_to([P, P]), tri[:, :], start=True, stop=True)
                last.then_inc(E["cs"], 1)
                after(pe, W["Sm"], c)
                pe.matmul(heads(B_G), xbc[:, 1, cols], xbc[:, 2:CB, cols], start=True, stop=True).then_inc(E["g"], 1)

            def s2(c, j):
                s = j % 2
                cols = slice(j * P, (j + 1) * P)
                after(pe, W["Sd"], c + 1)
                after(pe, W["bxc"], c + 1)
                after(pe, W["y"], c)
                pe.matmul(heads(B_YT), tm[:, s, 0, :], S[:, s, :, :], start=True, stop=False)
                after(pe, W["cp"], c + 1)
                after(pe, W["stt"], c)
                for h in range(H):
                    last = pe.matmul(heads(B_YT)[:, h, :], state[:, h, :], xbc[:, 2 + h, cols], start=False, stop=h == H - 1)
                last.then_inc(E["yt"], 1)
                after(pe, W["xd"], c + 1)
                pe.matmul(heads(B_SS), tm[:, s, 1, :], xds[:, s, :, :], start=True, stop=True).then_inc(E["ss"], 1)

            def w(c, j):
                after(pe, W["y"], c + 1)
                after(pe, W["x2"], c)
                for h in range(H):
                    last = pe.matmul(bank(B_WO), szs[:, h, j * P:(j + 1) * P], w_out[:, h, :], start=h == 0, stop=h == H - 1)
                last.then_inc(E["wo"], 1)

            def body(i, scan, nxt):
                if nxt:
                    n = (i + 1) * CH
                for j in range(CH):
                    c = i * CH + j
                    if scan and j < CH - 1:
                        s1(c + 1, i, j + 1)
                    if nxt:
                        t0(n + j, j)
                        if not scan and j == 0:
                            pe.wait_ge(e_wlo, 1)
                        f(n + j, j)
                    if scan:
                        s2(c, j)
                    if nxt and j:
                        t1(n + (j - 1), j - 1)
                    if scan:
                        w(c, j)
                        if j:
                            t2(c + -1, i * CH + (min(j + 1, CH - 1) + 1))
                if nxt:
                    t1(n + (CH - 1), CH - 1)
                    if not scan:
                        pe.wait_ge(e_wlo, 2)
                        pe.wait_ge(s_wout, 16)
                    win(i + 1, scan)
                    s1(n, i + 1, 0)
                else:
                    t2(c, NCH)

            body(-1, False, True)
            with pe.Fori(0, NS - 1) as reg:
                body(Index(reg, 0), True, True)
            body(NS - 1, True, False)

            def gate_up(p, k):
                i, x = k % NS, k // NS
                s = p * (2 * NS) + k
                if k == 0:
                    after(pe, W["wa"], p + 1)
                if k == NS:
                    after(pe, W["wb"], p * 2 + 1)
                after(pe, W["pr"], s + -1)
                for g in range(2):
                    last = product(bank(2 * (k % 2) + g), lambda a, b, kb: w_gu[b][:, g, kb, x * P:(x + 1) * P],
                                   lambda a, b, kb: h2T[a][:, kb, i * ST:(i + 1) * ST], KB)
                last.then_inc(E["gu"], 1)

            def down(p, i):
                if i == 0:
                    after(pe, W["wb"], p * 2 + 2)
                after(pe, W["lob"], p * (2 * NS) + (NS + i + 1))
                for t in range(CH):
                    n = p * (NS * CH) + (i * CH + t)
                    after(pe, W["dev"], n + -(CH - 1))
                    cols = slice(t * P, (t + 1) * P)
                    product(bank(4 + t), lambda a, b, kb: (mA[a][:, i, cols] if kb == 0 else mB[a][:, i % 2, cols]),
                            lambda a, b, kb: w_dn[b][:, kb, :], 2).then_inc(E["d"], 1)

            def pair(p):
                for k in range(NS + 2):
                    gate_up(p, k)
                for k in range(NS + 2, 2 * NS):
                    down(p, k - NS - 2)
                    gate_up(p, k)
                down(p, NS - 2)
                down(p, NS - 1)

            after(pe, W["lo2"], NCH)
            after(pe, W["x2"], NCH)
            after(pe, W["stt"], NCH)
            pair(0)
            with pe.Fori(1, NP) as reg:
                pair(Index(reg, 1))

            def c_t(c, k):
                after(pe, W["c_n"], c + 1)
                after(pe, W["c_lo"], c + -1)
                transpose4(k, c_n[k]).then_inc(E["c_t"], 1)

            def c_f(c, k):
                after(pe, W["c_lo"], c + 1)
                after(pe, W["c_o"], c + -1)
                product(bank(2 + k), lambda a, b, kb: cT[k][a][:, kb, :], lambda a, b, kb: w_ffn[b][:, kb, :], KB).then_inc(E["c_f"], 1)

            pe.wait_ge(E["lob"], NP * 2 * NS)
            c_t(0, 0)
            c_t(1, 1)
            c_f(0, 0)
            with pe.Fori(1, NCH // 2) as reg:
                c = Index(reg, 1) * 2
                c_t(c, 0)
                c_f(c + -1, 1)
                c_t(c + 1, 1)
                c_f(c, 0)
            c_f(NCH - 1, 1)


def kernel(L0_attn_hidden_states, L0_attn_w_in, L0_attn_conv_w, L0_attn_conv_b, L0_attn_A_log, L0_attn_D,
           L0_attn_dt_bias, L0_attn_w_out, L0_attn_ln1_w, L0_attn_ln2_w, L0_attn_gate_w, L0_attn_up_w,
           L0_attn_down_w, L0_ffn_qweight, L0_ffn_scales, L0_ffn_zeros, L0_ffn_lora_A, L0_ffn_lora_B, L0_ffn_bias):
    import numpy as np
    import concourse.bacc as bacc
    from concourse.bass_utils import run_bass_kernel_spmd

    x = np.asarray(L0_attn_hidden_states)

    def columns(v):
        return np.asarray(v).reshape(-1, P).T

    arrays = {
        "x_in": x.reshape(-1, x.shape[-1]),
        "w_in_t": np.asarray(L0_attn_w_in).T,
        "conv_w": np.asarray(L0_attn_conv_w),
        "conv_b": columns(L0_attn_conv_b),
        "a_log": np.asarray(L0_attn_A_log).reshape(1, -1),
        "d_skip": np.asarray(L0_attn_D).reshape(1, -1),
        "dt_bias": np.asarray(L0_attn_dt_bias).reshape(1, -1),
        "w_out_t": np.asarray(L0_attn_w_out).T,
        "ln1_w": columns(L0_attn_ln1_w),
        "ln2_w": columns(L0_attn_ln2_w),
        "gate_t": np.asarray(L0_attn_gate_w).T,
        "up_t": np.asarray(L0_attn_up_w).T,
        "down_t": np.asarray(L0_attn_down_w).T,
        "q_t": np.asarray(L0_ffn_qweight).T,
        "scales_t": np.asarray(L0_ffn_scales).T,
        "zeros_t": np.asarray(L0_ffn_zeros).T,
        "lora_a": np.asarray(L0_ffn_lora_A),
        "lora_b_t": np.asarray(L0_ffn_lora_B).T,
        "bias": np.asarray(L0_ffn_bias).reshape(1, -1),
    }
    arrays = {n: np.ascontiguousarray(a) for n, a in arrays.items()}
    nc = bacc.Bacc("TRN2", target_bir_lowering=False, num_devices=1)
    args = {n: nc.dram_tensor(n, a.shape, mybir.dt.from_np(a.dtype), kind="ExternalInput").ap() for n, a in arrays.items()}
    out = nc.dram_tensor("out", arrays["x_in"].shape, F32, kind="ExternalOutput").ap()
    build(nc, out=out, **args)
    r = run_bass_kernel_spmd(nc, [arrays], core_ids=[0])
    return r.results[0]["out"].reshape(x.shape)
```

```python
from contextlib import ExitStack

import concourse.bass as bass
from concourse import mybir

ALU = mybir.AluOpType
ACT = mybir.ActivationFunctionType
F32 = mybir.dt.float32
F16 = mybir.dt.float16
BF16 = mybir.dt.bfloat16
I32 = mybir.dt.int32
AX_X = mybir.AxisListType.X

P = 128
EPS = 1e-5
ACT_SCALE = 2.0 ** 10
GATED_SCALE = 2.0 ** -54
W_TOP = 14
TINY = 2.0 ** -90
MASKED = -1e30
GROUP = 64
PARTS = ((0, 0), (0, 1), (1, 0))


class Index:

    def __init__(self, value, least):
        self.value, self.least = value, least

    def __mul__(self, k):
        return Index(self.value * k, self.least * k)

    def __add__(self, k):
        return Index(self.value + k, self.least + k)


def at(i):
    return i.value if isinstance(i, Index) else i


def after(eng, event, count):
    sem, start = event if isinstance(event, tuple) else (event, 0)
    if isinstance(count, Index):
        assert count.least + start > 0, (sem, count.least)
        eng.wait_ge(sem, count.value + start)
    elif count > 0:
        eng.wait_ge(sem, count + start)


def build(nc, x_in, w_in_t, conv_w, conv_b, a_log, d_skip, dt_bias, w_out_t, ln1_w, ln2_w,
          gate_t, up_t, down_t, q_t, scales_t, zeros_t, lora_a, lora_b_t, bias, out):
    T, DM = x_in.shape
    KB = DM // P
    NPROJ = w_in_t.shape[1]
    H = a_log.shape[1]
    DI = w_out_t.shape[0]
    CONV = conv_w.shape[0]
    CB = CONV // P
    NTAP = conv_w.shape[1]
    ZB = DI // P
    INTER = gate_t.shape[1]
    RANK = lora_a.shape[0]
    ST = 512
    NS = T // ST
    CH = ST // P
    NCH = T // P
    PAIR = 2 * P
    NP = INTER // PAIR
    assert ZB == H == KB == 4 and CB == 2 + H and NTAP == 4 and INTER % PAIR == 0
    LORA_SCALE = 1.0 / RANK

    ctx = ExitStack()
    with ctx:
        def sb(name, shape, dt=F32):
            return ctx.enter_context(nc.sbuf_tensor(name, shape, dt))

        def sem(name):
            return ctx.enter_context(nc.semaphore(name))

        w_ffn = [sb(f"w_ffn{p}", [P, KB, DM], F16) for p in range(2)]
        w_in = [sb(f"w_in{p}", [P, KB, NPROJ], F16) for p in range(2)]
        w_out = sb("w_out", [P, H, DM])
        raw_gu = sb("raw_gu", [P, 2, KB, PAIR])
        raw_d = sb("raw_d", [P, 2, DM])
        xs = sb("xs", [P, NCH, DM])
        h2T = [sb(f"h2T{p}", [P, KB, T], F16) for p in range(2)]
        stage = sb("stage", [P, KB * NPROJ])
        raw_in = stage[:, :].rearrange("p (k n) -> p k n", k=KB)
        xbc = stage[:, 0:CB * ST].rearrange("p (b t) -> p b t", b=CB)
        szs = stage[:, CB * ST:(CB + ZB) * ST].rearrange("p (h t) -> p h t", h=ZB)
        mA = [stage[:, 1024 * p:1024 * (p + 1)].bitcast(F16).rearrange("p (i t) -> p i t", i=NS) for p in range(2)]
        mB = [stage[:, 2048 + 512 * p:2560 + 512 * p].bitcast(F16).rearrange("p (i t) -> p i t", i=2) for p in range(2)]
        gt = stage[:, 3072:4096].rearrange("p (i t) -> p i t", i=2)
        gp = stage[:, 4096:5120].rearrange("p (i t) -> p i t", i=2)
        half = sb("half", [P, 2 * (2 * KB * P + KB * ST)], F16)
        nT = [[half[:, (2 * s + p) * KB * P:(2 * s + p + 1) * KB * P].rearrange("p (k t) -> p k t", k=KB)
               for p in range(2)] for s in range(2)]
        hT = [half[:, 4 * KB * P + p * KB * ST:4 * KB * P + (p + 1) * KB * ST].rearrange("p (k t) -> p k t", k=KB)
              for p in range(2)]
        w_gu = [half[:, 2048 * p:2048 * (p + 1)].rearrange("p (g k n) -> p g k n", g=2, k=KB) for p in range(2)]
        w_dn = [half[:, 4096 + 1024 * p:5120 + 1024 * p].rearrange("p (b n) -> p b n", b=2) for p in range(2)]
        x_t = sb("x_t", [P, CH, DM])
        n0 = sb("n0", [P, DM])
        hn = sb("hn", [P, DM])
        h2n = sb("h2n", [P, DM])
        n1 = sb("n1", [P, DM])
        x2 = sb("x2", [P, 2, DM])
        junk = sb("junk", [P, DM], BF16)
        pre = sb("pre", [P, 2, ST + NTAP - 1])
        hist = sb("hist", [P, CB, NTAP - 1])
        th = sb("th", [P, 2, ST])
        tm = sb("tm", [P, 2, 2, P])
        Ld = sb("Ld", [P, H, P])
        S = sb("S", [P, 2, H, P])
        ecs = sb("ecs", [P, H, P])
        xds = sb("xds", [P, 2, H, P])
        state = sb("state", [P, H, P])
        q_raw = h2T[0][:, :, :].rearrange("p k t -> p (k t)").bitcast(I32)[:, 0:KB * DM].rearrange("p (k n) -> p k n", k=KB)
        wf = h2T[1][:, :, :].rearrange("p k t -> p (k t)").bitcast(F32)[:, KB * DM:2 * KB * DM].rearrange("p (k n) -> p k n", k=KB)
        NG = zeros_t.shape[0]
        zt = sb("zt", [NG, DM])
        sc = sb("sc", [NG, DM])
        sel = sb("sel", [NG, KB, P])
        la = sb("la", [RANK, DM])
        lb = sb("lb", [RANK, DM])
        cT = [[x_t[:, s, p * 256:(p + 1) * 256].bitcast(F16).rearrange("p (k t) -> p k t", k=KB)
               for p in range(2)] for s in range(2)]
        o_t = [x_t[:, 2 + s, :] for s in range(2)]
        c_n = [n0, hn]

        ident = sb("ident", [P, P])
        tri = sb("tri", [P, P])
        mask = sb("mask", [P, P])
        d_diag = sb("d_diag", [P, H, P])
        hb = sb("hb", [P, DM])
        cw = sb("cw", [P, CB, NTAP])
        cb = sb("cb", [P, CB])
        al = sb("al", [P, H])
        dsk = sb("dsk", [P, H])
        dtb = sb("dtb", [P, H])
        ln1 = sb("ln1", [P, KB])
        ln2 = sb("ln2", [P, KB])
        mhalf = sb("mhalf", [P, 1])
        mx = sb("mx", [P, 2])
        mxk = sb("mxk", [P, KB])
        mxa = sb("mxa", [P, 2])
        pw = sb("pw", [P, 2])
        sw = sb("sw", [P, 2])
        d_f = sb("d_f", [P, 1])
        d_i = sb("d_i", [P, 1])
        d_ih = sb("d_ih", [P, 1])
        mx3 = sb("mx3", [P, 3])
        mxa3 = sb("mxa3", [P, 3])
        pw3 = sb("pw3", [P, 3])
        sw3 = sb("sw3", [P, 3])
        dgh = sb("dgh", [P, 1])
        d_tmp = sb("d_tmp", [P, 1])
        d_d = sb("d_d", [P, 1])
        st6 = sb("st6", [P, 2, 6])
        mv0 = sb("mv0", [P, 3])
        r0 = sb("r0", [P, 1])
        mvN = sb("mvN", [P, CH, 3])
        rN = sb("rN", [P, CH])
        muC = sb("muC", [P, CH])
        rC = sb("rC", [P, CH])
        rt = sb("rt", [P, 4])
        rr = sb("rr", [P, 1])
        ssq = sb("ssq", [P, 1])
        r2 = sb("r2", [P, 2])
        NT = CH * H
        dt = sb("dt", [P, NT])
        dA = sb("dA", [P, NT])
        a_neg = sb("a_neg", [P, H])
        ncs = sb("ncs", [P, NT])
        sp = sb("sp", [P, 6, NT])
        dec = sb("dec", [P, H])
        wv = sb("wv", [P, 2, H])
        g_last = sb("g_last", [P, 2, H])

        PS = ctx.enter_context(nc.psum_tensor("PS", [P, 8, 512], F32))
        B_FO, B_WO, B_TA, B_TB, B_G, B_CS, B_YT, B_SS = range(8)

        PLACE = [0, 1] + [2 + 2 * h for h in range(H)]
        PLACE_Z = [3 + 2 * h for h in range(H)]

        def bank(b):
            return PS[:, b, :]

        def heads(b):
            return PS[:, b, :].rearrange("p (h q) -> p h q", h=H)

        def blocks(b):
            return PS[:, b, :].rearrange("p (k t) -> p k t", k=KB)

        def chunk_of(t, c):
            return t[:, bass.ds(at(c), 1), :].rearrange("p o n -> p (o n)")

        def tokens_of(t, c):
            return t[:, :, bass.ds(at(c * P), P)]

        s_x = [sem(f"s_x{j}") for j in range(CH)]
        s_q = [sem(f"s_q{k}") for k in range(KB)]; s_la = sem("s_la"); s_small = sem("s_small")
        s_win = [sem(f"s_win{k}") for k in range(KB)]; s_wout = sem("s_wout"); s_raw = sem("s_raw")
        s_o = [sem(f"s_o{k}") for k in range(2)]
        e_const = sem("e_const"); e_lora = sem("e_lora"); e_prep = sem("e_prep")
        e_max = sem("e_max"); e_all = sem("e_all"); e_scale = sem("e_scale"); e_whi = sem("e_whi"); e_wlo = sem("e_wlo")
        e_aexp = sem("e_aexp"); e_fold = sem("e_fold"); e_sel = sem("e_sel"); e_wf = sem("e_wf"); e_dve = sem("e_dve"); e_pool = sem("e_pool")
        spare = {n: sem("e_spare_" + n) for n in ("vector", "gpsimd")}
        names = ("st0 ve0 r0 n0 xb t0 hi0 lo0 f x1 st1 ve1 lc rr hn t1 hi1 lo1 mrc "
                 "pi cva hst tapx tap tnh sl tnz slz dtm spx dtp spu dta csm ncs "
                 "bx bxc cs msk lex dcx wv ecs gl g Sm Sd cp xd yt y ss stt "
                 "n1 wo x2 sq ms r2 h2n t2 hi2 lo2 xsd").split()
        E = {n: sem("e_" + n) for n in names}
        for n in "gu tnb vb pr hib lob d dev wa wb whb fdx mxb alb scx scb dsx dsc".split():
            E[n] = sem("b_" + n)
        for n in "ve r n t hi lo f xb o st".split():
            E["c_" + n] = sem("c_" + n)
        FIRST = 2
        STARTED = {"vector": "x2 y stt lo2 Sm c_o".split(), "gpsimd": ["xsd"], "scalar": [],
                   "tensor": "yt ss t2".split()}
        W = {n: (s, FIRST if any(n in of for of in STARTED.values()) else 0) for n, s in E.items()}

        def start(eng, which):
            for n in STARTED[which]:
                eng.sem_inc(E[n], FIRST)

        def apart(eng):
            eng.sem_inc(spare["vector" if eng is nc.vector else "gpsimd"], 1)

        block = ctx.enter_context(nc.Block())

        @block.sync
        def _(sp_):
            def load_x(c, j):
                sp_.dma_start(x_t[:, j, :], x_in[bass.ds(at(c * P), P), :]).then_inc(s_x[j], 16)

            for k in range(2):
                sp_.sem_inc(s_o[k], 16)
            q_v = q_t.rearrange("(k p) n -> p k n", p=P)
            w_in_v = w_in_t.rearrange("(k p) n -> p k n", p=P)
            sp_.dma_start(zt[:, :], zeros_t).then_inc(s_la, 16)
            sp_.dma_start(sc[:, :], scales_t).then_inc(s_la, 16)
            sp_.dma_start(la[:, :], lora_a).then_inc(s_la, 16)
            sp_.dma_start(lb[:, :], lora_b_t).then_inc(s_la, 16)
            for k in range(KB):
                sp_.dma_start(q_raw[:, k, :], q_v[:, k, :]).then_inc(s_q[k], 16)
            load_x(0, 0)
            sp_.dma_start(hb[:, :], bias.broadcast_to([P, DM])).then_inc(s_small, 16)
            sp_.dma_start(cw[:, :, :], conv_w.rearrange("(b p) t -> p b t", p=P)).then_inc(s_small, 16)
            sp_.dma_start(cb[:, :], conv_b).then_inc(s_small, 16)
            for dst, src in ((al, a_log), (dsk, d_skip), (dtb, dt_bias)):
                sp_.dma_start(dst[:, :], src.broadcast_to([P, H])).then_inc(s_small, 16)
            sp_.dma_start(ln1[:, :], ln1_w).then_inc(s_small, 16)
            sp_.dma_start(ln2[:, :], ln2_w).then_inc(s_small, 16)
            for j in range(1, CH):
                load_x(j, j)
            for k in range(KB):
                sp_.dma_start(raw_in[:, k, :], w_in_v[:, k, :]).then_inc(s_win[k], 16)
            sp_.dma_start(w_out[:, :, :], w_out_t.rearrange("(h p) n -> p h n", p=P)).then_inc(s_wout, 16)

            gate_v = gate_t.rearrange("(k p) f -> p k f", p=P)
            up_v = up_t.rearrange("(k p) f -> p k f", p=P)

            def load_pair(p):
                cols = bass.ds(at(p * PAIR), PAIR)
                sp_.dma_start(raw_gu[:, 0, :, :], gate_v[:, :, cols]).then_inc(s_raw, 16)
                sp_.dma_start(raw_gu[:, 1, :, :], up_v[:, :, cols]).then_inc(s_raw, 16)
                sp_.dma_start(raw_d[:, :, :], down_t[cols, :].rearrange("(b p) n -> p b n", p=P)).then_inc(s_raw, 16)

            load_pair(0)
            with sp_.Fori(1, NS) as reg:
                i = Index(reg, 1)
                for j in range(CH):
                    after(sp_, W["x1"], (i + -1) * CH + (j + 1))
                    load_x(i * CH + j, j)
            with sp_.Fori(1, NP) as reg:
                p = Index(reg, 1)
                after(sp_, W["wb"], p * 2)
                load_pair(p)

            out_v = out
            with sp_.Fori(0, NCH // 2) as reg:
                m = Index(reg, 0)
                for k in range(2):
                    after(sp_, W["c_o"], m * 2 + (k + 1))
                    sp_.dma_start(out_v[bass.ds(at((m * 2 + k) * P), P), :], o_t[k]).then_inc(s_o[k], 16)
            for k in range(2):
                sp_.wait_ge(s_o[k], 16 * (NCH // 2 + 1))

        @block.gpsimd
        def _(po):
            n_self = [0]

            def chain(ins):
                n_self[0] += 1
                ins.then_inc(e_pool, 1)
                po.wait_ge(e_pool, n_self[0])

            start(po, "gpsimd")
            chain(po.memset(sel[:, :, :], 1.0))
            chain(po.affine_select(out=sel[:, :, :], in_=sel[:, :, :], compare_op=ALU.is_ge, fill=0.0,
                                   base=0, pattern=[[P, KB], [1, P]], channel_multiplier=-GROUP))
            chain(po.affine_select(out=sel[:, :, :], in_=sel[:, :, :], compare_op=ALU.is_ge, fill=0.0,
                                   base=GROUP - 1, pattern=[[-P, KB], [-1, P]], channel_multiplier=GROUP))
            po.sem_inc(e_sel, 1)
            chain(po.memset(ident[:, :], 0.0))
            chain(po.affine_select(out=ident[:, :], in_=ident[:, :], compare_op=ALU.not_equal, fill=1.0,
                                   base=0, pattern=[[-1, P]], channel_multiplier=1))
            chain(po.memset(tri[:, :], 1.0))
            chain(po.affine_select(out=tri[:, :], in_=tri[:, :], compare_op=ALU.is_ge, fill=0.0,
                                   base=0, pattern=[[1, P]], channel_multiplier=-1))
            chain(po.memset(mask[:, :], 0.0))
            chain(po.affine_select(out=mask[:, :], in_=mask[:, :], compare_op=ALU.is_ge, fill=MASKED,
                                   base=0, pattern=[[1, P]], channel_multiplier=-1))
            chain(po.memset(mhalf[:, :], -0.5))
            po.wait_ge(s_small, 16 * 8)
            chain(po.tensor_scalar(hb[:, :], hb[:, :], 0.5, None, ALU.mult))
            for h in range(H):
                chain(po.tensor_scalar(d_diag[:, h, :], ident[:, :], dsk[:, h:h + 1], None, ALU.mult))
            po.sem_inc(e_const, 1)

            def rsqrt(dst, src):
                return po.tensor_tensor(dst, src, mhalf[:, :], ALU.pow)

            def ln0(c, j):
                after(po, W["ve0"], c + 1)
                rsqrt(r0[:, :], mv0[:, 2:3]).then_inc(E["r0"], 1)

            def xb(c, j):
                after(po, W["n0"], c + 1)
                po.tensor_tensor(x_t[:, j, :], x_t[:, j, :], hb[:, :], ALU.add).then_inc(E["xb"], 1)

            def ln1_chain(c, j):
                v = mvN[:, j, 1:2]
                base = c * 4
                after(po, W["ve1"], c + 1)
                rsqrt(rN[:, j:j + 1], mvN[:, j, 2:3]).then_inc(E["lc"], 1)
                after(po, W["lc"], base + 1)
                apart(po)
                po.tensor_scalar(rt[:, 0:1], v, rN[:, j:j + 1], rN[:, j:j + 1], ALU.mult, ALU.mult).then_inc(E["lc"], 1)
                after(po, W["lc"], base + 2)
                apart(po)
                po.tensor_scalar(rt[:, 1:2], rt[:, 0:1], EPS, None, ALU.add).then_inc(E["lc"], 1)
                after(po, W["lc"], base + 3)
                rsqrt(rt[:, 2:3], rt[:, 1:2]).then_inc(E["lc"], 1)
                after(po, W["lc"], base + 4)
                after(po, W["hn"], c)
                po.tensor_tensor(rr[:, :], rN[:, j:j + 1], rt[:, 2:3], ALU.mult).then_inc(E["rr"], 1)

            def scan_help1(c, j):
                cols = slice(j * P, (j + 1) * P)
                after(po, W["ecs"], c + 1)
                after(po, W["g"], c + 1)
                po.tensor_tensor(xbc[:, 2:CB, cols], xbc[:, 2:CB, cols], ecs[:, :, :], ALU.mult).then_inc(E["cp"], 1)
                after(po, W["Sm"], c + 1)
                po.tensor_tensor(S[:, j % 2, :, :], S[:, j % 2, :, :], d_diag[:, :, :], ALU.add).then_inc(E["Sd"], 1)

            def rms2(c, j):
                after(po, W["sq"], c + 1)
                apart(po)
                po.tensor_scalar(rt[:, 3:4], ssq[:, :], 1.0 / DM, EPS, ALU.mult, ALU.add).then_inc(E["ms"], 1)
                after(po, W["ms"], c + 1)
                rsqrt(r2[:, j % 2:j % 2 + 1], rt[:, 3:4]).then_inc(E["r2"], 1)
                after(po, W["x2"], c + 1)
                po.tensor_tensor(chunk_of(xs, c), chunk_of(xs, c), x2[:, j % 2, :], ALU.add).then_inc(E["xsd"], 1)

            def resident_max(n):
                po.wait_ge(e_max, n + 1)
                po.partition_all_reduce(mxa[:, n:n + 1], mx[:, n:n + 1], P, bass.bass_isa.ReduceOp.max).then_inc(e_all, 1)

            def pair_max(p):
                after(po, W["mxb"], p + 1)
                apart(po)
                po.partition_all_reduce(mxa3[:, :], mx3[:, :], P, bass.bass_isa.ReduceOp.max).then_inc(E["alb"], 1)

            resident_max(0)
            def body(i, scan, nxt):
                if nxt:
                    n = (i + 1) * CH
                    ln0(n, 0)
                    xb(n, 0)
                    ln0(n + 1, 1)
                for j in range(CH):
                    c = i * CH + j
                    if nxt and j < CH - 1:
                        xb(n + (j + 1), j + 1)
                    if nxt and j < CH - 2:
                        ln0(n + (j + 2), j + 2)
                    if nxt and not scan and j == 1:
                        resident_max(1)
                    if nxt:
                        ln1_chain(n + j, j)
                    if scan and j < CH - 1:
                        scan_help1(c + 1, j + 1)
                    if scan:
                        rms2(c, j)
                    if not nxt and j == 1:
                        pair_max(0)
                if nxt:
                    scan_help1(n, 0)

            body(-1, False, True)
            with po.Fori(0, NS - 1) as reg:
                body(Index(reg, 0), True, True)
            body(NS - 1, True, False)
            with po.Fori(1, NP) as reg:
                pair_max(Index(reg, 1))

            def c_norm(c, k):
                after(po, W["c_ve"], c + 1)
                rsqrt(rN[:, k:k + 1], mvN[:, k, 2:3]).then_inc(E["c_r"], 1)
                after(po, W["c_n"], c + 1)
                po.tensor_tensor(chunk_of(xs, c), chunk_of(xs, c), hb[:, :], ALU.add).then_inc(E["c_xb"], 1)

            with po.Fori(0, NCH // 2) as reg:
                for k in range(2):
                    c_norm(Index(reg, 0) * 2 + k, k)

        @block.scalar
        def _(ac):
            ac.wait_ge(s_small, 16 * 8)
            ac.activation(a_neg[:, :], al[:, :], ACT.Exp).then_inc(e_aexp, 1)
            for k in range(KB):
                ac.wait_ge(s_win[k], 16)
                ac.activation(raw_in[:, k, :], raw_in[:, k, :], ACT.Copy, scale=ln1[:, k:k + 1]).then_inc(e_fold, 1)
            ac.wait_ge(e_scale, 1)
            ac.activation(w_ffn[0][:, :, :], wf, ACT.Copy, scale=sw[:, 0:1]).then_inc(e_whi, 1)

            def w_in_hi():
                ac.wait_ge(e_scale, 2)
                ac.activation(w_in[0][:, :, :], raw_in, ACT.Copy, scale=sw[:, 1:2]).then_inc(e_whi, 1)

            def hi0(c, j):
                after(ac, W["t0"], c + 1)
                after(ac, W["f"], c + -1)
                ac.activation(nT[j % 2][0], blocks(B_TA), ACT.Copy, scale=ACT_SCALE).then_inc(E["hi0"], 1)

            def hi1(c, j):
                after(ac, W["t1"], c + 1)
                ac.activation(hT[0][:, :, j * P:(j + 1) * P], blocks(B_TA), ACT.Copy, scale=ACT_SCALE).then_inc(E["hi1"], 1)

            def hi2(c):
                after(ac, W["t2"], c + 1)
                ac.activation(tokens_of(h2T[0], c), blocks(B_TB), ACT.Copy, scale=ACT_SCALE).then_inc(E["hi2"], 1)

            def norm2(c, j):
                after(ac, W["r2"], c + 1)
                after(ac, W["t2"], c)
                ac.activation(h2n[:, :], x2[:, j % 2, :], ACT.Copy, scale=r2[:, j % 2:j % 2 + 1]).then_inc(E["h2n"], 1)

            def square(c, j):
                after(ac, W["x2"], c + 1)
                ac.activation(junk[:, :], x2[:, j % 2, :], ACT.Square, accum_out=ssq[:, :]).then_inc(E["sq"], 1)

            def scan1(c, j):
                s = j % 2
                after(ac, W["bx"], c + 1)
                after(ac, W["ss"], c + -1)
                ac.activation(tm[:, s, :, :], PS[:, B_TB, 0:2 * P].rearrange("p (a t) -> p a t", a=2), ACT.Copy).then_inc(E["bxc"], 1)
                after(ac, W["msk"], c + 1)
                ac.activation(dec[:, :], dec[:, :], ACT.Exp).then_inc(E["dcx"], 1)
                for h in range(H):
                    last = ac.activation(Ld[:, h, :], Ld[:, h, :], ACT.Exp, bias=ncs[:, j * H + h:j * H + h + 1])
                last.then_inc(E["lex"], 1)

            def scan_exp(c, j):
                s = j % 2
                after(ac, W["cp"], c)
                ac.activation(ecs[:, :, :], heads(B_CS), ACT.Exp).then_inc(E["ecs"], 1)
                ac.activation(g_last[:, s, :], heads(B_CS)[:, :, P - 1:P].rearrange("p h o -> p (h o)"), ACT.Exp).then_inc(E["gl"], 1)

            def scan2(c, j):
                s = j % 2
                after(ac, W["wv"], c + 1)
                for h in range(H):
                    last = ac.activation(xds[:, s, h, :], tm[:, s, 0, :], ACT.Copy, scale=wv[:, s, h:h + 1])
                last.then_inc(E["xd"], 1)

            def hi_gu(x):
                for g in range(2):
                    last = ac.activation(w_gu[0][:, g, :, x * P:(x + 1) * P], raw_gu[:, g, :, x * P:(x + 1) * P], ACT.Copy, scale=sw3[:, g:g + 1])
                return last

            def cut_a(p):
                after(ac, W["scb"], p + 1)
                after(ac, W["gu"], p * (2 * NS) + (-NS))
                hi_gu(0).then_inc(E["whb"], 1)

            def conv(i, b):
                w = b % 2
                after(ac, W["pi"], i * (CB + ZB) + (PLACE[b] + 1))
                after(ac, W["tap"], i * CB + (b - 1))
                after(ac, W["hst"], i * CB + (b + 1 - CB))
                ac.activation(pre[:, w, 0:NTAP - 1], hist[:, b, :], ACT.Copy)
                ac.activation(pre[:, w, NTAP - 1:], bank(B_G + PLACE[b] % 2), ACT.Copy)
                last = ac.activation(xbc[:, b, :], bank(B_G + PLACE[b] % 2), ACT.Identity, scale=cw[:, b, NTAP - 1:NTAP], bias=cb[:, b:b + 1])
                last.then_inc(E["cva"], 1)
                after(ac, W["cva"], i * CB + (b + 1))
                ac.activation(hist[:, b, :], pre[:, w, ST:], ACT.Copy).then_inc(E["hst"], 1)

            def tanh(i, b):
                after(ac, W["sl"], i * CB + b)
                after(ac, W["tap"], i * CB + (b + 1))
                ac.activation(th[:, 0, :], xbc[:, b, :], ACT.Tanh).then_inc(E["tnh"], 1)

            def tanh_z(i, h):
                after(ac, W["slz"], i * ZB + h)
                after(ac, W["pi"], i * (CB + ZB) + (PLACE_Z[h] + 1))
                ac.activation(th[:, 1, :], bank(B_CS), ACT.Tanh, scale=d_ih[:, :]).then_inc(E["tnz"], 1)

            def win(i, scan):
                conv(i, 0)
                if scan:
                    norm2(i * CH + -1, CH - 1)
                conv(i, 1)
                tanh(i, 0)
                if scan:
                    hi2(i * CH + -1)
                tanh(i, 1)
                for h in range(H):
                    conv(i, 2 + h)
                    tanh_z(i, h)
                    tanh(i, 2 + h)
                    if h == 2:
                        after(ac, W["dtp"], i + 1)
                        ac.activation(sp[:, 2, :], sp[:, 1, :], ACT.Exp).then_inc(E["spu"], 1)

            def body(i, scan, nxt):
                if nxt:
                    n = (i + 1) * CH
                for j in range(CH):
                    c = i * CH + j
                    if nxt and j:
                        hi1(n + (j - 1), j - 1)
                    if scan and j:
                        norm2(c + -1, j - 1)
                    if scan and j < CH - 1:
                        scan1(c + 1, j + 1)
                    if nxt and j == 0:
                        hi0(n, 0)
                    if scan and j < CH - 1:
                        scan_exp(c + 1, j + 1)
                        scan2(c + 1, j + 1)
                    if nxt and j < CH - 1:
                        hi0(n + (j + 1), j + 1)
                    if scan and j:
                        hi2(c + -1)
                    if nxt and j == CH - 1:
                        hi1(n + j, j)
                    if scan:
                        square(c, j)
                    if nxt and not scan and j == 2:
                        w_in_hi()
                    if not nxt and j == 2:
                        cut_a(0)
                if nxt:
                    win(i + 1, scan)
                    scan1(n, 0)
                    scan_exp(n, 0)
                    scan2(n, 0)
                else:
                    norm2(c, CH - 1)
                    hi2(c)

            body(-1, False, True)
            with ac.Fori(0, NS - 1) as reg:
                body(Index(reg, 0), True, True)
            body(NS - 1, True, False)

            def cut_b(p):
                after(ac, W["gu"], p * (2 * NS))
                after(ac, W["d"], p * (NS * CH))
                hi_gu(1)
                ac.activation(w_dn[0], raw_d[:, :, :], ACT.Copy, scale=sw3[:, 2:3]).then_inc(E["whb"], 1)

            def step(p, k):
                s = p * (2 * NS) + k
                after(ac, W["gu"], s + 1)
                after(ac, W["dsc"], p + 1)
                ac.activation(gt[:, k % 2, :], bank(2 * (k % 2)), ACT.Tanh, scale=dgh[:, :]).then_inc(E["tnb"], 1)
                after(ac, W["pr"], s + 1)
                if k >= NS:
                    i = k - NS
                    if i >= 2:
                        after(ac, W["d"], p * (NS * CH) + (i - 1) * CH)
                    dst = mB[0][:, i % 2, :]
                else:
                    dst = mA[0][:, k, :]
                ac.activation(dst, gp[:, k % 2, :], ACT.Copy).then_inc(E["hib"], 1)

            def pair(p, nxt):
                for k in range(2 * NS):
                    step(p, k)
                    if k == 0:
                        cut_b(p)
                    if nxt and k == 2 * NS - 2:
                        cut_a(p + 1)

            pair(0, True)
            with ac.Fori(1, NP - 1) as reg:
                pair(Index(reg, 1), True)
            pair(NP - 1, False)

            def c_hi(c, k):
                after(ac, W["c_t"], c + 1)
                after(ac, W["c_f"], c + -1)
                ac.activation(cT[k][0], blocks(k), ACT.Copy, scale=ACT_SCALE).then_inc(E["c_hi"], 1)

            c_hi(0, 0)
            c_hi(1, 1)
            with ac.Fori(1, NCH // 2) as reg:
                for k in range(2):
                    c_hi(Index(reg, 1) * 2 + k, k)

        @block.vector
        def _(ve):
            n_self = [0]

            def chain(ins):
                n_self[0] += 1
                ins.then_inc(e_dve, 1)
                ve.wait_ge(e_dve, n_self[0])

            def link(ins, s, count):
                ins.then_inc(s, 1)
                after(ve, (s, 0), count)

            start(ve, "vector")
            chain(ve.memset(hist[:, :, :], 0.0))
            chain(ve.memset(state[:, :, :], 0.0))

            def power_of_two(pw_, sw_, top, link_):
                link_(ve.tensor_scalar(top, top, TINY, None, ALU.max))
                link_(ve.tensor_scalar(pw_.bitcast(I32), top.bitcast(I32), 0x7F800000, None, ALU.bitwise_and))
                link_(ve.tensor_scalar(sw_.bitcast(I32), pw_.bitcast(I32), 0x7F800000, None, ALU.bitwise_xor))
                link_(ve.tensor_scalar(sw_, sw_, 2.0 ** (W_TOP - 1), None, ALU.mult))

            def stats(src, mv, stat, e_link, base, e_ve):
                apart(ve)
                link(ve.bn_stats(stat, src), e_link, base + 1)
                apart(ve)
                link(ve.bn_aggr(mv[:, 0:2], stat), e_link, base + 2)
                ve.tensor_scalar(mv[:, 2:3], mv[:, 1:2], EPS, None, ALU.add).then_inc(e_ve, 1)

            def prep0(c, j):
                after(ve, s_x[j], (c * 1 + (CH - j)) * (16 // CH))
                stats(x_t[:, j, :], mv0[:, :], st6[:, 0, :], E["st0"], c * 2, E["ve0"])

            def norm0(c, j):
                after(ve, W["r0"], c + 1)
                after(ve, W["t0"], c)
                ve.tensor_scalar(n0[:, :], x_t[:, j, :], mv0[:, 0:1], r0[:, :], ALU.subtract, ALU.mult).then_inc(E["n0"], 1)

            for k in range(KB):
                b = 4 * (k % 2)
                ve.wait_ge(s_q[k], 16)
                ve.wait_ge(e_lora, k + 1)
                chain(ve.tensor_tensor(wf[:, k, :], q_raw[:, k, :], bank(b), ALU.subtract))
                chain(ve.tensor_tensor(wf[:, k, :], wf[:, k, :], bank(b + 1), ALU.mult))
                ve.scalar_tensor_tensor(wf[:, k, :], bank(b + 2), LORA_SCALE, wf[:, k, :], ALU.mult, ALU.add).then_inc(e_wf, 1)
            ve.wait_ge(e_wf, KB)
            ve.tensor_reduce(mx[:, 0:1], wf, mybir.AxisListType.XY, ALU.max, apply_absolute_value=True).then_inc(e_max, 1)
            ve.wait_ge(e_all, 1)
            power_of_two(pw[:, 0:1], sw[:, 0:1], mxa[:, 0:1], chain)
            ve.sem_inc(e_scale, 1)
            chain(ve.tensor_scalar(d_f[:, :], pw[:, 0:1], 0.5 * 2.0 ** -W_TOP / ACT_SCALE, None, ALU.mult))
            prep0(0, 0)
            ve.wait_ge(e_whi, 1)
            ve.scalar_tensor_tensor(w_ffn[1][:, :, :].rearrange("p k n -> p (k n)"), wf.rearrange("p k n -> p (k n)"),
                                    sw[:, 0:1], w_ffn[0][:, :, :].rearrange("p k n -> p (k n)"),
                                    ALU.mult, ALU.subtract).then_inc(e_wlo, 1)

            def w_in_max(ks):
                for k in ks:
                    ve.wait_ge(e_fold, k + 1)
                    chain(ve.tensor_reduce(mxk[:, k:k + 1], raw_in[:, k, :], AX_X, ALU.max, apply_absolute_value=True))
                if KB - 1 not in ks:
                    return
                ve.tensor_reduce(mx[:, 1:2], mxk[:, :], AX_X, ALU.max).then_inc(e_max, 1)
                ve.wait_ge(e_all, 2)
                power_of_two(pw[:, 1:2], sw[:, 1:2], mxa[:, 1:2], chain)
                ve.sem_inc(e_scale, 1)
                chain(ve.tensor_scalar(d_i[:, :], pw[:, 1:2], 2.0 ** -W_TOP / ACT_SCALE, None, ALU.mult))
                chain(ve.tensor_scalar(d_ih[:, :], d_i[:, :], 0.5, None, ALU.mult))
                chain(ve.tensor_scalar(cw[:, :, :], cw[:, :, :], d_ih[:, :], None, ALU.mult))
                chain(ve.tensor_scalar(cb[:, :], cb[:, :], 0.5, None, ALU.mult))
                ve.wait_ge(e_aexp, 1)
                chain(ve.tensor_scalar(a_neg[:, :], a_neg[:, :], -1.0, None, ALU.mult))

            def w_in_lo():
                ve.wait_ge(e_whi, 2)
                ve.scalar_tensor_tensor(w_in[1][:, :, :].rearrange("p k n -> p (k n)"), raw_in.rearrange("p k n -> p (k n)"),
                                        sw[:, 1:2], w_in[0][:, :, :].rearrange("p k n -> p (k n)"),
                                        ALU.mult, ALU.subtract).then_inc(e_wlo, 1)

            def lo(dst, src_bank, hi):
                return ve.scalar_tensor_tensor(dst, blocks(src_bank), ACT_SCALE, hi, ALU.mult, ALU.subtract)

            def lo0(c, j):
                after(ve, W["hi0"], c + 1)
                lo(nT[j % 2][1], B_TA, nT[j % 2][0]).then_inc(E["lo0"], 1)

            def lo1(c, j):
                after(ve, W["hi1"], c + 1)
                cols = slice(j * P, (j + 1) * P)
                lo(hT[1][:, :, cols], B_TA, hT[0][:, :, cols]).then_inc(E["lo1"], 1)

            def lo2(c):
                after(ve, W["hi2"], c + 1)
                lo(tokens_of(h2T[1], c), B_TB, tokens_of(h2T[0], c)).then_inc(E["lo2"], 1)

            def x1_stats(c, j):
                after(ve, W["f"], c + 1)
                after(ve, W["xb"], c + 1)
                link(ve.scalar_tensor_tensor(chunk_of(xs, c), bank(B_FO), d_f[:, :], x_t[:, j, :], ALU.mult, ALU.add),
                     E["x1"], c + 1)
                stats(chunk_of(xs, c), mvN[:, j, :], st6[:, 1, :], E["st1"], c * 2, E["ve1"])

            def norm1(c, j):
                after(ve, W["rr"], c + 1)
                after(ve, W["t1"], c)
                ve.tensor_scalar(hn[:, :], chunk_of(xs, c), mvN[:, j, 0:1], rr[:, :], ALU.subtract, ALU.mult).then_inc(E["hn"], 1)

            def masked(c, j):
                after(ve, W["cs"], c + 1)
                after(ve, W["Sm"], c)
                ve.tensor_tensor(Ld[:, :, :], heads(B_CS), mask[:, :].unsqueeze(1).broadcast_to([P, H, P]), ALU.add)
                ve.tensor_tensor(dec[:, :], heads(B_CS)[:, :, P - 1:P].rearrange("p h o -> p (h o)"), ncs[:, j * H:(j + 1) * H], ALU.add).then_inc(E["msk"], 1)

            def weights(c, j):
                s = j % 2
                after(ve, W["dcx"], c + 1)
                ve.tensor_tensor(wv[:, s, :], dec[:, :], dt[:, j * H:(j + 1) * H], ALU.mult).then_inc(E["wv"], 1)

            def scan1(c, j):
                s = j % 2
                after(ve, W["g"], c + 1)
                after(ve, W["lex"], c + 1)
                after(ve, W["yt"], c + -1)
                for h in range(H):
                    last = ve.scalar_tensor_tensor(S[:, s, h, :], heads(B_G)[:, h, :], dt[:, j * H + h:j * H + h + 1], Ld[:, h, :],
                                                   ALU.mult, ALU.mult)
                last.then_inc(E["Sm"], 1)

            def gated(c, j):
                cols = slice(j * P, (j + 1) * P)
                after(ve, W["yt"], c + 1)
                ve.scalar_tensor_tensor(szs[:, :, cols], heads(B_YT), d_ih[:, :], szs[:, :, cols], ALU.mult, ALU.mult).then_inc(E["y"], 1)

            def advance(c, j):
                s = j % 2
                after(ve, W["ss"], c + 1)
                after(ve, W["gl"], c + 1)
                for h in range(H):
                    last = ve.scalar_tensor_tensor(state[:, h, :], state[:, h, :], g_last[:, s, h:h + 1], heads(B_SS)[:, h, :],
                                                   ALU.mult, ALU.add)
                last.then_inc(E["stt"], 1)

            def renorm(c, j):
                after(ve, W["x2"], c)
                ve.tensor_scalar(n1[:, :], chunk_of(xs, c), muC[:, j:j + 1], rC[:, j:j + 1], ALU.subtract, ALU.mult).then_inc(E["n1"], 1)

            def residual2(c, j):
                after(ve, W["n1"], c + 1)
                after(ve, W["wo"], c + 1)
                after(ve, W["xsd"], c + -1)
                ve.tensor_tensor(x2[:, j % 2, :], n1[:, :], bank(B_WO), ALU.add).then_inc(E["x2"], 1)

            def taps(i, b):
                w = b % 2
                after(ve, W["cva"], i * CB + (b + 1))
                base = (i * CB + b) * 2
                for k in range(NTAP - 1):
                    ins = ve.scalar_tensor_tensor(xbc[:, b, :], pre[:, w, k:k + ST], cw[:, b, k:k + 1], xbc[:, b, :],
                                                  ALU.mult, ALU.add)
                    if k < NTAP - 2:
                        link(ins, E["tapx"], base + (k + 1))
                ins.then_inc(E["tap"], 1)

            def silu(i, b):
                after(ve, W["tnh"], i * CB + (b + 1))
                ve.scalar_tensor_tensor(xbc[:, b, :], th[:, 0, :], 1.0, xbc[:, b, :], ALU.add, ALU.mult).then_inc(E["sl"], 1)

            def silu_z(i, h):
                after(ve, W["tnz"], i * ZB + (h + 1))
                ve.scalar_tensor_tensor(szs[:, h, :], th[:, 1, :], 1.0, bank(B_CS), ALU.add, ALU.mult).then_inc(E["slz"], 1)

            def fold(p):
                after(ve, s_raw, (p + 1) * 48)
                lnb = ln2[:, :].unsqueeze(2).broadcast_to([P, KB, PAIR])
                base = p * 2
                for g in range(2):
                    link(ve.tensor_tensor(raw_gu[:, g, :, :], raw_gu[:, g, :, :], lnb, ALU.mult), E["fdx"], base + (g + 1))
                for g in range(2):
                    ve.tensor_reduce(mx3[:, g:g + 1], raw_gu[:, g, :, :], mybir.AxisListType.XY, ALU.max, apply_absolute_value=True)
                ve.tensor_reduce(mx3[:, 2:3], raw_d[:, :, :], mybir.AxisListType.XY, ALU.max, apply_absolute_value=True).then_inc(E["mxb"], 1)

            def scales(p):
                n = [0]

                def lk(ins):
                    n[0] += 1
                    link(ins, E["scx"], p * 4 + n[0])

                after(ve, W["alb"], p + 1)
                power_of_two(pw3[:, :], sw3[:, :], mxa3[:, :], lk)
                assert n[0] == 4
                ve.sem_inc(E["scb"], 1)

            def lo_gu(x):
                cols = slice(x * P, (x + 1) * P)
                for g in range(2):
                    last = ve.scalar_tensor_tensor(w_gu[1][:, g, :, cols], raw_gu[:, g, :, cols], sw3[:, g:g + 1], w_gu[0][:, g, :, cols],
                                                   ALU.mult, ALU.subtract)
                return last

            def cut_a(p):
                after(ve, W["whb"], p * 2 + 1)
                lo_gu(0).then_inc(E["wa"], 1)

            def cut_b(p):
                after(ve, W["whb"], p * 2 + 2)
                lo_gu(1).then_inc(E["wb"], 1)
                ve.scalar_tensor_tensor(w_dn[1].rearrange("p b n -> p (b n)"), raw_d[:, :, :].rearrange("p b n -> p (b n)"), sw3[:, 2:3],
                                        w_dn[0].rearrange("p b n -> p (b n)"), ALU.mult, ALU.subtract).then_inc(E["wb"], 1)

            N_SP = 16

            def softplus(i):
                base = i * N_SP
                n = [0]

                def lk(ins):
                    n[0] += 1
                    link(ins, E["spx"], base + n[0])

                v, m, u, s1, s2, q = (sp[:, k, :] for k in range(6))

                def rep(t):
                    return t[:, :].unsqueeze(1).broadcast_to([P, CH, H])

                def four(t):
                    return t.rearrange("p (c h) -> p c h", c=CH)

                after(ve, W["dtm"], i + 1)
                lk(ve.scalar_tensor_tensor(four(v), four(PS[:, B_SS, 0:NT]), d_i[:, :], rep(dtb), ALU.mult, ALU.add))
                lk(ve.tensor_scalar(m, v, -1.0, None, ALU.mult))
                ve.tensor_tensor(m, m, v, ALU.min).then_inc(E["dtp"], 1)
                after(ve, W["spu"], i + 1)
                lk(ve.tensor_scalar(s1, u, 2.0, None, ALU.add))
                lk(ve.reciprocal(s2, s1))
                lk(ve.tensor_tensor(s1, u, s2, ALU.mult))
                lk(ve.tensor_tensor(s2, s1, s1, ALU.mult))
                lk(ve.tensor_scalar(q, s2, 1.0 / 15, None, ALU.mult))
                for k in (13, 11, 9, 7, 5, 3):
                    lk(ve.scalar_tensor_tensor(q, q, 1.0 / k, s2, ALU.add, ALU.mult))
                lk(ve.scalar_tensor_tensor(q, q, 1.0, s1, ALU.add, ALU.mult))
                lk(ve.tensor_scalar(v, v, 0.0, None, ALU.max))
                lk(ve.scalar_tensor_tensor(dt[:, :], q, 2.0, v, ALU.mult, ALU.add))
                assert n[0] == N_SP, n[0]
                ve.tensor_tensor(four(dA[:, :]), four(dt[:, :]), rep(a_neg), ALU.mult).then_inc(E["dta"], 1)

            def win(i, scan):
                taps(i, 0)
                taps(i, 1)
                silu(i, 0)
                if scan:
                    lo2(i * CH + -1)
                silu(i, 1)
                for h in range(H):
                    taps(i, 2 + h)
                    silu_z(i, h)
                    silu(i, 2 + h)
                    if h == 2:
                        softplus(i)
                after(ve, W["csm"], i + 1)
                link(ve.tensor_scalar(ncs[:, :], PS[:, B_YT, 0:NT], -1.0, None, ALU.mult), E["ncs"], i + 1)

            def body(i, scan, nxt):
                if nxt:
                    n = (i + 1) * CH
                    if scan:
                        prep0(n, 0)
                for j in range(CH):
                    c = i * CH + j
                    if j == 0:
                        if scan:
                            masked(c + 1, 1)
                        if nxt:
                            norm0(n, 0)
                            prep0(n + 1, 1)
                        if scan:
                            weights(c + 1, 1)
                        if nxt:
                            lo0(n, 0)
                            norm0(n + 1, 1)
                        if scan:
                            gated(c, 0)
                            advance(c, 0)
                            scan1(c + 1, 1)
                        if nxt:
                            prep0(n + 2, 2)
                        if scan:
                            renorm(c, 0)
                        if nxt and not scan:
                            w_in_max(range(0, 2))
                        if nxt:
                            x1_stats(n, 0)
                            lo0(n + 1, 1)
                    else:
                        if nxt:
                            if j < CH - 1:
                                norm0(n + (j + 1), j + 1)
                            lo1(n + (j - 1), j - 1)
                        if scan:
                            renorm(c, j)
                        if nxt:
                            if j < CH - 2:
                                prep0(n + (j + 2), j + 2)
                            x1_stats(n + j, j)
                        if scan and j < CH - 1:
                            masked(c + 1, j + 1)
                        if scan:
                            if j < CH - 1:
                                weights(c + 1, j + 1)
                            gated(c, j)
                            advance(c, j)
                            if j < CH - 1:
                                scan1(c + 1, j + 1)
                        if nxt and j < CH - 1:
                            lo0(n + (j + 1), j + 1)
                    if nxt and not scan and j == 1:
                        w_in_max(range(2, KB))
                    if nxt:
                        norm1(n + j, j)
                    if scan and j:
                        lo2(c + -1)
                    if nxt and j == CH - 1:
                        lo1(n + j, j)
                    if scan:
                        residual2(c, j)
                    if nxt and not scan and j == 2:
                        w_in_lo()
                    if not nxt:
                        (lambda: None, lambda: fold(0), lambda: (scales(0), cut_a(0)), lambda: None)[j]()
                if nxt:
                    after(ve, W["rr"], n + CH)
                    ve.tensor_copy(muC[:, :], mvN[:, :, 0:1].rearrange("p c o -> p (c o)"))
                    link(ve.tensor_copy(rC[:, :], rN[:, :]), E["mrc"], i + 2)
                    win(i + 1, scan)
                    masked(n, 0)
                    weights(n, 0)
                    scan1(n, 0)
                else:
                    lo2(c)

            body(-1, False, True)
            with ve.Fori(0, NS - 1) as reg:
                body(Index(reg, 0), True, True)
            body(NS - 1, True, False)

            def descale(p):
                back = 2.0 ** -W_TOP / ACT_SCALE
                ve.tensor_scalar(dgh[:, :], pw3[:, 0:1], 0.5 * back, None, ALU.mult)
                link(ve.tensor_scalar(d_tmp[:, :], pw3[:, 0:1], pw3[:, 1:2], pw3[:, 2:3], ALU.mult, ALU.mult), E["dsx"], p + 1)
                ve.tensor_scalar(d_d[:, :], d_tmp[:, :], 0.5 * back * back / GATED_SCALE * 2.0 ** -W_TOP, None, ALU.mult).then_inc(E["dsc"], 1)

            def step(p, k):
                s = p * (2 * NS) + k
                w = k % 2
                after(ve, W["tnb"], s + 1)
                link(ve.scalar_tensor_tensor(gt[:, w, :], gt[:, w, :], 1.0, bank(2 * w), ALU.add, ALU.mult), E["vb"], s + 1)
                ve.scalar_tensor_tensor(gp[:, w, :], gt[:, w, :], GATED_SCALE, bank(2 * w + 1), ALU.mult, ALU.mult).then_inc(E["pr"], 1)
                after(ve, W["hib"], s + 1)
                hi, lo_ = (mB[0][:, k % 2, :], mB[1][:, k % 2, :]) if k >= NS else (mA[0][:, k, :], mA[1][:, k, :])
                ve.tensor_tensor(lo_, gp[:, w, :], hi, ALU.subtract).then_inc(E["lob"], 1)

            def down(p, i):
                for t in range(CH):
                    after(ve, W["d"], p * (NS * CH) + (i * CH + t + 1))
                    c = i * CH + t
                    ve.scalar_tensor_tensor(xs[:, c, :], bank(4 + t), d_d[:, :], xs[:, c, :], ALU.mult, ALU.add).then_inc(E["dev"], 1)

            def pair(p, nxt):
                descale(p)
                for k in range(2 * NS):
                    if k >= NS + 2:
                        down(p, k - NS - 2)
                    if not nxt and k == 2 * NS - 1:
                        c_begin()
                    step(p, k)
                    if k == 0:
                        cut_b(p)
                    if nxt and k == NS:
                        fold(p + 1)
                    if nxt and k == NS + 1:
                        scales(p + 1)
                    if nxt and k == 2 * NS - 2:
                        cut_a(p + 1)
                if not nxt:
                    c_lo(0, 0)
                down(p, NS - 2)
                down(p, NS - 1)

            def c_stats(c, k):
                stats(chunk_of(xs, c), mvN[:, k, :], st6[:, k, :], E["c_st"], c * 2, E["c_ve"])

            def c_norm(c, k):
                after(ve, W["c_r"], c + 1)
                after(ve, W["c_t"], c + -1)
                ve.tensor_scalar(c_n[k][:, :], chunk_of(xs, c), mvN[:, k, 0:1], rN[:, k:k + 1], ALU.subtract, ALU.mult).then_inc(E["c_n"], 1)

            def c_lo(c, k):
                after(ve, W["c_hi"], c + 1)
                lo(cT[k][1], k, cT[k][0]).then_inc(E["c_lo"], 1)

            def c_out(c, k):
                after(ve, W["c_f"], c + 1)
                after(ve, W["c_xb"], c + 1)
                after(ve, s_o[k], (c + (2 - k)) * 8)
                ve.scalar_tensor_tensor(o_t[k], bank(2 + k), d_f[:, :], chunk_of(xs, c), ALU.mult, ALU.add).then_inc(E["c_o"], 1)

            def c_begin():
                after(ve, W["dev"], (NP - 1) * NCH + CH)
                c_stats(0, 0)
                c_norm(0, 0)
                c_stats(1, 1)
                c_norm(1, 1)
                c_stats(2, 0)

            def c_step(c, k, first=False, left=NCH):
                if left > 2:
                    c_norm(c + 2, k)
                if left > 1:
                    c_lo(c + 1, 1 - k)
                if not first:
                    c_out(c + -1, 1 - k)
                if left > 3:
                    c_stats(c + 3, 1 - k)

            after(ve, W["xsd"], NCH)
            pair(0, True)
            with ve.Fori(1, NP - 1) as reg:
                pair(Index(reg, 1), True)
            pair(NP - 1, False)
            c_step(0, 0, first=True)
            after(ve, W["dev"], NP * NCH)
            with ve.Fori(0, NCH // 2 - 2) as reg:
                for k in range(2):
                    c_step(Index(reg, 0) * 2 + (1 + k), 1 - k)
            for c in range(NCH - 3, NCH + 1):
                c_step(c, c % 2, left=NCH - c)

        @block.tensor
        def _(pe):
            start(pe, "tensor")

            def transpose4(b, src):
                for k in range(KB):
                    last = pe.transpose(blocks(b)[:, k, :], src[:, k * P:(k + 1) * P], ident[:, :])
                return last

            def product(out_, lhs, rhs, n_k, first=True, last=True):
                todo = [(k, a, b) for k in range(n_k) for a, b in PARTS]
                for n, (k, a, b) in enumerate(todo):
                    ins = pe.matmul(out_, lhs(a, b, k), rhs(a, b, k), start=first and n == 0, stop=last and n == len(todo) - 1)
                return ins

            pe.wait_ge(s_la, 64)
            pe.wait_ge(e_sel, 1)
            for k in range(KB):
                b = 4 * (k % 2)
                pe.wait_ge(e_wf, k - 1) if k >= 2 else None
                pe.matmul(bank(b), sel[:, k, :], zt[:, :], start=True, stop=True)
                pe.matmul(bank(b + 1), sel[:, k, :], sc[:, :], start=True, stop=True)
                pe.matmul(bank(b + 2), la[:, k * P:(k + 1) * P], lb[:, :], start=True, stop=True).then_inc(e_lora, 1)
            pe.wait_ge(e_const, 1)

            def t0(c, j):
                after(pe, W["n0"], c + 1)
                if j == 1:
                    after(pe, W["lo0"], c)
                if j >= 2:
                    after(pe, W["lo1"], c + -1)
                transpose4(B_TA, n0).then_inc(E["t0"], 1)

            def f(c, j):
                after(pe, W["lo0"], c + 1)
                after(pe, W["x1"], c)
                product(bank(B_FO), lambda a, b, k: nT[j % 2][a][:, k, :], lambda a, b, k: w_ffn[b][:, k, :], KB).then_inc(E["f"], 1)

            def t1(c, j):
                after(pe, W["hn"], c + 1)
                after(pe, W["lo0"], (c + 2) if j < CH - 1 else (c + 1))
                after(pe, W["lo1"], c)
                transpose4(B_TA, hn).then_inc(E["t1"], 1)

            def t2(c, scans_copied):
                after(pe, W["h2n"], c + 1)
                after(pe, W["bxc"], scans_copied)
                after(pe, W["lo2"], c)
                transpose4(B_TB, h2n).then_inc(E["t2"], 1)

            at_place = {PLACE[b]: DI + b * P for b in range(CB)} | {PLACE_Z[h]: h * P for h in range(ZB)}

            def win(i, scan):
                NB = CB + ZB
                after(pe, W["lo1"], i * CH + CH)
                for q in range(NB):
                    if q == 0:
                        after(pe, W["Sm"], i * CH)
                    elif q == 1:
                        after(pe, W["gl"], i * CH)
                    elif q == 2:
                        after(pe, W["cva"], i * CB + 1)
                    elif q == 3:
                        after(pe, W["cva"], i * CB + 2)
                    elif q % 2:
                        after(pe, W["slz"], i * ZB + (q // 2 - 1))
                    else:
                        after(pe, W["cva"], i * CB + (q // 2 + 1))
                    product(bank(B_G + q % 2), lambda a, b, k: w_in[b][:, k, at_place[q]:at_place[q] + P], lambda a, b, k: hT[a][:, k, :], KB).then_inc(E["pi"], 1)
                    if scan and q == 1:
                        t2(i * CH + -1, i * CH)
                    if q == 5:
                        after(pe, W["stt"], i * CH)
                        for j in range(CH):
                            last = product(PS[:, B_SS, j * H:(j + 1) * H], lambda a, b, k: hT[a][:, k, j * P:(j + 1) * P],
                                           lambda a, b, k: w_in[b][:, k, NPROJ - H:NPROJ], KB)
                        last.then_inc(E["dtm"], 1)
                after(pe, W["dta"], i + 1)
                after(pe, W["y"], i * CH)
                pe.matmul(PS[:, B_YT, 0:NT], tri[:, :], dA[:, :], start=True, stop=True).then_inc(E["csm"], 1)

            def s1(c, i, j):
                cols = slice(j * P, (j + 1) * P)
                if j == 0:
                    after(pe, W["sl"], i * CB + 2)
                after(pe, W["bxc"], c)
                if j == 0:
                    after(pe, W["lo2"], c)
                if j == CH - 1:
                    after(pe, W["lo2"], c + -2)
                for n in range(2):
                    last = pe.transpose(PS[:, B_TB, n * P:(n + 1) * P], xbc[:, n, cols], ident[:, :])
                last.then_inc(E["bx"], 1)
                if j == 0:
                    after(pe, W["slz"], (i + 1) * ZB)
                else:
                    after(pe, W["gl"], c)
                for h in range(H):
                    n = j * H + h
                    last = pe.matmul(heads(B_CS)[:, h, :], dA[:, n:n + 1].broadcast_to([P, P]), tri[:, :], start=True, stop=True)
                last.then_inc(E["cs"], 1)

            def s1_bc(c, i, j):
                cols = slice(j * P, (j + 1) * P)
                if j == 0:
                    after(pe, W["sl"], (i + 1) * CB)
                else:
                    after(pe, W["Sm"], c)
                pe.matmul(heads(B_G), xbc[:, 1, cols], xbc[:, 2:CB, cols], start=True, stop=True).then_inc(E["g"], 1)

            def s2_diag(c, j):
                s = j % 2
                cols = slice(j * P, (j + 1) * P)
                after(pe, W["Sd"], c + 1)
                after(pe, W["bxc"], c + 1)
                after(pe, W["y"], c)
                pe.matmul(heads(B_YT), tm[:, s, 0, :], S[:, s, :, :], start=True, stop=False)

            def s2_state(c, j):
                s = j % 2
                cols = slice(j * P, (j + 1) * P)
                after(pe, W["cp"], c + 1)
                after(pe, W["stt"], c)
                for h in range(H):
                    last = pe.matmul(heads(B_YT)[:, h, :], state[:, h, :], xbc[:, 2 + h, cols], start=False, stop=h == H - 1)
                last.then_inc(E["yt"], 1)
                after(pe, W["xd"], c + 1)
                pe.matmul(heads(B_SS), tm[:, s, 1, :], xds[:, s, :, :], start=True, stop=True).then_inc(E["ss"], 1)

            def w(c, j, with_t1):
                after(pe, W["y"], c + 1)
                after(pe, W["x2"], c)
                for h in range(H):
                    if with_t1 and h == H // 2:
                        t1(c + CH, j)
                    last = pe.matmul(bank(B_WO), szs[:, h, j * P:(j + 1) * P], w_out[:, h, :], start=h == 0, stop=h == H - 1)
                last.then_inc(E["wo"], 1)

            def body(i, scan, nxt):
                if nxt:
                    n = (i + 1) * CH
                for j in range(CH):
                    c = i * CH + j
                    if j == 0:
                        if scan:
                            s1(c + 1, i, 1)
                        if nxt:
                            t0(n, 0)
                        if scan:
                            s2_diag(c, 0)
                            s2_state(c, 0)
                            s1_bc(c + 1, i, 1)
                        if nxt:
                            if not scan:
                                pe.wait_ge(e_wlo, 1)
                            f(n, 0)
                            t0(n + 1, 1)
                    else:
                        if nxt:
                            t1(n + (j - 1), j - 1)
                            f(n + j, j)
                        if scan and j < CH - 1:
                            s1(c + 1, i, j + 1)
                        if scan:
                            s2_diag(c, j)
                            s2_state(c, j)
                            if j < CH - 1:
                                s1_bc(c + 1, i, j + 1)
                        if nxt and j < CH - 1:
                            t0(n + (j + 1), j + 1)
                    if scan:
                        if j:
                            t2(c + -1, i * CH + (min(j + 1, CH - 1) + 1))
                        w(c, j, nxt and j == CH - 1)
                if nxt:
                    if not scan:
                        t1(n + (CH - 1), CH - 1)
                        pe.wait_ge(e_wlo, 2)
                        pe.wait_ge(s_wout, 16)
                    win(i + 1, scan)
                    s1(n, i + 1, 0)
                    s1_bc(n, i + 1, 0)

            body(-1, False, True)
            with pe.Fori(0, NS - 1) as reg:
                body(Index(reg, 0), True, True)
            body(NS - 1, True, False)

            def gate_up(p, k):
                i, x = k % NS, k // NS
                s = p * (2 * NS) + k
                if k == 0:
                    after(pe, W["wa"], p + 1)
                if k == NS:
                    after(pe, W["wb"], p * 2 + 1)
                after(pe, W["pr"], s + -1)
                for g in range(2):
                    last = product(bank(2 * (k % 2) + g), lambda a, b, kb: w_gu[b][:, g, kb, x * P:(x + 1) * P],
                                   lambda a, b, kb: h2T[a][:, kb, i * ST:(i + 1) * ST], KB)
                last.then_inc(E["gu"], 1)

            def down(p, i):
                if i == 0:
                    after(pe, W["wb"], p * 2 + 2)
                after(pe, W["lob"], p * (2 * NS) + (NS + i + 1))
                for t in range(CH):
                    n = p * (NS * CH) + (i * CH + t)
                    after(pe, W["dev"], n + -(CH - 1))
                    cols = slice(t * P, (t + 1) * P)
                    product(bank(4 + t), lambda a, b, kb: (mA[a][:, i, cols] if kb == 0 else mB[a][:, i % 2, cols]),
                            lambda a, b, kb: w_dn[b][:, kb, :], 2).then_inc(E["d"], 1)

            def pair(p, first=False, last=False):
                for k in range(NS + 2):
                    if first and k == 1:
                        t2(NCH - 1, NCH)
                        after(pe, W["lo2"], NCH)
                    gate_up(p, k)
                for k in range(NS + 2, 2 * NS):
                    down(p, k - NS - 2)
                    gate_up(p, k)
                if last:
                    after(pe, W["pr"], NP * 2 * NS - 1)
                    c_t(0, 0)
                    c_t(1, 1)
                down(p, NS - 2)
                down(p, NS - 1)

            def c_t(c, k):
                after(pe, W["c_n"], c + 1)
                after(pe, W["c_lo"], c + -1)
                transpose4(k, c_n[k]).then_inc(E["c_t"], 1)

            def c_f(c, k):
                after(pe, W["c_lo"], c + 1)
                after(pe, W["c_o"], c + -1)
                product(bank(2 + k), lambda a, b, kb: cT[k][a][:, kb, :], lambda a, b, kb: w_ffn[b][:, kb, :], KB).then_inc(E["c_f"], 1)

            after(pe, W["x2"], NCH)
            after(pe, W["stt"], NCH)
            pair(0, first=True)
            with pe.Fori(1, NP - 1) as reg:
                pair(Index(reg, 1))
            pair(NP - 1, last=True)
            after(pe, W["pr"], NP * 2 * NS)
            c_f(0, 0)
            c_t(2, 0)
            with pe.Fori(0, NCH // 2 - 2) as reg:
                for k in range(2):
                    c = Index(reg, 0) * 2 + (1 + k)
                    c_f(c, 1 - k)
                    c_t(c + 2, 1 - k)
            for c in range(NCH - 3, NCH):
                c_f(c, c % 2)
                if c + 2 < NCH:
                    c_t(c + 2, c % 2)


def kernel(L0_attn_hidden_states, L0_attn_w_in, L0_attn_conv_w, L0_attn_conv_b, L0_attn_A_log, L0_attn_D,
           L0_attn_dt_bias, L0_attn_w_out, L0_attn_ln1_w, L0_attn_ln2_w, L0_attn_gate_w, L0_attn_up_w,
           L0_attn_down_w, L0_ffn_qweight, L0_ffn_scales, L0_ffn_zeros, L0_ffn_lora_A, L0_ffn_lora_B, L0_ffn_bias):
    import numpy as np
    import concourse.bacc as bacc
    from concourse.bass_utils import run_bass_kernel_spmd

    x = np.asarray(L0_attn_hidden_states)

    def columns(v):
        return np.asarray(v).reshape(-1, P).T

    arrays = {
        "x_in": x.reshape(-1, x.shape[-1]),
        "w_in_t": np.asarray(L0_attn_w_in).T,
        "conv_w": np.asarray(L0_attn_conv_w),
        "conv_b": columns(L0_attn_conv_b),
        "a_log": np.asarray(L0_attn_A_log).reshape(1, -1),
        "d_skip": np.asarray(L0_attn_D).reshape(1, -1),
        "dt_bias": np.asarray(L0_attn_dt_bias).reshape(1, -1),
        "w_out_t": np.asarray(L0_attn_w_out).T,
        "ln1_w": columns(L0_attn_ln1_w),
        "ln2_w": columns(L0_attn_ln2_w),
        "gate_t": np.asarray(L0_attn_gate_w).T,
        "up_t": np.asarray(L0_attn_up_w).T,
        "down_t": np.asarray(L0_attn_down_w).T,
        "q_t": np.asarray(L0_ffn_qweight).T,
        "scales_t": np.asarray(L0_ffn_scales).T,
        "zeros_t": np.asarray(L0_ffn_zeros).T,
        "lora_a": np.asarray(L0_ffn_lora_A),
        "lora_b_t": np.asarray(L0_ffn_lora_B).T,
        "bias": np.asarray(L0_ffn_bias).reshape(1, -1),
    }
    arrays = {n: np.ascontiguousarray(a) for n, a in arrays.items()}
    nc = bacc.Bacc("TRN2", target_bir_lowering=False, num_devices=1)
    args = {n: nc.dram_tensor(n, a.shape, mybir.dt.from_np(a.dtype), kind="ExternalInput").ap() for n, a in arrays.items()}
    out = nc.dram_tensor("out", arrays["x_in"].shape, F32, kind="ExternalOutput").ap()
    build(nc, out=out, **args)
    r = run_bass_kernel_spmd(nc, [arrays], core_ids=[0])
    return r.results[0]["out"].reshape(x.shape)
```

```python
from contextlib import ExitStack

import concourse.bass as bass
from concourse import mybir

ALU = mybir.AluOpType
ACT = mybir.ActivationFunctionType
F32 = mybir.dt.float32
F16 = mybir.dt.float16
BF16 = mybir.dt.bfloat16
I32 = mybir.dt.int32
AX_X = mybir.AxisListType.X

P = 128
EPS = 1e-5
ACT_SCALE = 2.0 ** 10
GATED_SCALE = 2.0 ** -54
W_TOP = 14
TINY = 2.0 ** -90
MASKED = -1e30
GROUP = 64
N_WARM = 9
PARTS = ((0, 0), (0, 1), (1, 0))


class Index:

    def __init__(self, value, least):
        self.value, self.least = value, least

    def __mul__(self, k):
        return Index(self.value * k, self.least * k)

    def __add__(self, k):
        return Index(self.value + k, self.least + k)


def at(i):
    return i.value if isinstance(i, Index) else i


def after(eng, event, count):
    sem, start = event if isinstance(event, tuple) else (event, 0)
    if isinstance(count, Index):
        assert count.least + start > 0, (sem, count.least)
        eng.wait_ge(sem, count.value + start)
    elif count > 0:
        eng.wait_ge(sem, count + start)


def build(nc, x_in, w_in_t, conv_w, conv_b, a_log, d_skip, dt_bias, w_out_t, ln1_w, ln2_w,
          gate_t, up_t, down_t, q_t, scales_t, zeros_t, lora_a, lora_b_t, bias, out):
    T, DM = x_in.shape
    KB = DM // P
    NPROJ = w_in_t.shape[1]
    H = a_log.shape[1]
    DI = w_out_t.shape[0]
    CONV = conv_w.shape[0]
    CB = CONV // P
    NTAP = conv_w.shape[1]
    ZB = DI // P
    INTER = gate_t.shape[1]
    RANK = lora_a.shape[0]
    ST = 512
    NS = T // ST
    CH = ST // P
    NCH = T // P
    PAIR = 2 * P
    NP = INTER // PAIR
    assert ZB == H == KB == 4 and CB == 2 + H and NTAP == 4 and INTER % PAIR == 0
    LORA_SCALE = 1.0 / RANK

    ctx = ExitStack()
    with ctx:
        def sb(name, shape, dt=F32):
            return ctx.enter_context(nc.sbuf_tensor(name, shape, dt))

        def sem(name):
            return ctx.enter_context(nc.semaphore(name))

        w_ffn = [sb(f"w_ffn{p}", [P, KB, DM], F16) for p in range(2)]
        w_in = [sb(f"w_in{p}", [P, KB, NPROJ], F16) for p in range(2)]
        w_out = sb("w_out", [P, H, DM])
        raw_gu = sb("raw_gu", [P, 2, KB, PAIR])
        raw_d = sb("raw_d", [P, 2, DM])
        xs = sb("xs", [P, NCH, DM])
        h2 = sb("h2", [P, 2, KB, T], F16)
        h2T = [h2[:, p, :, :] for p in range(2)]
        stage = sb("stage", [P, KB * NPROJ])
        raw_in = stage[:, :].rearrange("p (k n) -> p k n", k=KB)
        xbc = stage[:, 0:CB * ST].rearrange("p (b t) -> p b t", b=CB)
        szs = stage[:, CB * ST:(CB + ZB) * ST].rearrange("p (h t) -> p h t", h=ZB)
        mA = [stage[:, 1024 * p:1024 * (p + 1)].bitcast(F16).rearrange("p (i t) -> p i t", i=NS) for p in range(2)]
        mB = [stage[:, 2048 + 512 * p:2560 + 512 * p].bitcast(F16).rearrange("p (i t) -> p i t", i=2) for p in range(2)]
        gt = stage[:, 3072:4096].rearrange("p (i t) -> p i t", i=2)
        gp = stage[:, 4096:5120].rearrange("p (i t) -> p i t", i=2)
        half = sb("half", [P, 2 * (2 * KB * P + KB * ST)], F16)
        nT = [half[:, 2 * s * KB * P:2 * (s + 1) * KB * P].rearrange("p (a k t) -> p a k t", a=2, k=KB)
              for s in range(2)]
        hT = half[:, 4 * KB * P:4 * KB * P + 2 * KB * ST].rearrange("p (a k t) -> p a k t", a=2, k=KB)
        w_gu = [half[:, 2048 * p:2048 * (p + 1)].rearrange("p (g k n) -> p g k n", g=2, k=KB) for p in range(2)]
        w_dn = [half[:, 4096 + 1024 * p:5120 + 1024 * p].rearrange("p (b n) -> p b n", b=2) for p in range(2)]
        x_t = sb("x_t", [P, CH, DM])
        n0 = sb("n0", [P, DM])
        hn = sb("hn", [P, DM])
        h2n = sb("h2n", [P, DM])
        n1 = sb("n1", [P, DM])
        n0_p, hn_p, h2n_p = (sb(name, [P, 2, DM], F16) for name in ("n0_p", "hn_p", "h2n_p"))
        x2 = sb("x2", [P, 2, DM])
        junk = sb("junk", [P, DM], BF16)
        pre = sb("pre", [P, 2, ST + NTAP - 1])
        hist = sb("hist", [P, CB, NTAP - 1])
        th = sb("th", [P, 2, ST])
        tm = sb("tm", [P, 2, 2, P])
        Ld = sb("Ld", [P, H, P])
        S = sb("S", [P, 2, H, P])
        ecs = sb("ecs", [P, H, P])
        xds = sb("xds", [P, 2, H, P])
        state = sb("state", [P, H, P])
        early = h2[:, :, :, :].rearrange("p a k t -> p (a k t)")
        q_raw = early.bitcast(I32)[:, 0:KB * DM].rearrange("p (k n) -> p k n", k=KB)
        wf = early.bitcast(F32)[:, KB * DM:2 * KB * DM].rearrange("p (k n) -> p k n", k=KB)
        NG = zeros_t.shape[0]
        zt, sc, la, lb = (early.bitcast(F32)[:, (2 * KB + n) * DM:(2 * KB + n + 1) * DM] for n in range(4))
        sel = early.bitcast(F32)[:, (2 * KB + 4) * DM:(2 * KB + 4) * DM + KB * P].rearrange("p (k r) -> p k r", k=KB)
        cT = [x_t[:, s, :].bitcast(F16).rearrange("p (a k t) -> p a k t", a=2, k=KB) for s in range(2)]
        o_t = [x_t[:, 2 + s, :] for s in range(2)]
        c_n = [n0, hn]
        c_np = [n0_p, hn_p]

        ident = sb("ident", [P, P])
        ident16 = sb("ident16", [P, P], F16)
        tri = sb("tri", [P, P])
        mask = sb("mask", [P, P])
        d_diag = sb("d_diag", [P, H, P])
        hb = sb("hb", [P, DM])
        cw = sb("cw", [P, CB, NTAP])
        cb = sb("cb", [P, CB])
        al = sb("al", [P, H])
        dsk = sb("dsk", [P, H])
        dtb = sb("dtb", [P, H])
        ln1 = sb("ln1", [P, KB])
        ln2 = sb("ln2", [P, KB])
        mhalf = sb("mhalf", [P, 1])
        mx = sb("mx", [P, 2])
        mxf = sb("mxf", [P, KB])
        mxk = sb("mxk", [P, KB])
        mxa = sb("mxa", [P, 2])
        pw = sb("pw", [P, 2])
        lsw = sb("lsw", [P, KB])
        sw = sb("sw", [P, 2])
        d_f = sb("d_f", [P, 1])
        d_i = sb("d_i", [P, 1])
        d_ih = sb("d_ih", [P, 1])
        mx3 = sb("mx3", [P, 3])
        mxa3 = sb("mxa3", [P, 3])
        pw3 = sb("pw3", [P, 3])
        sw3 = sb("sw3", [P, 3])
        dgh = sb("dgh", [P, 1])
        d_tmp = sb("d_tmp", [P, 1])
        d_d = sb("d_d", [P, 1])
        st6 = sb("st6", [P, 2, 6])
        mv0 = sb("mv0", [P, 3])
        r0 = sb("r0", [P, 1])
        mvN = sb("mvN", [P, CH, 3])
        rN = sb("rN", [P, CH])
        muC = sb("muC", [P, CH])
        rC = sb("rC", [P, CH])
        rt = sb("rt", [P, 4])
        rr = sb("rr", [P, 1])
        ssq = sb("ssq", [P, 1])
        r2 = sb("r2", [P, 2])
        NT = CH * H
        dt = sb("dt", [P, NT])
        dA = sb("dA", [P, NT])
        a_neg = sb("a_neg", [P, H])
        ncs = sb("ncs", [P, NT])
        sp = sb("sp", [P, 6, NT])
        dec = sb("dec", [P, H])
        wv = sb("wv", [P, 2, H])
        g_last = sb("g_last", [P, 2, H])

        PS = ctx.enter_context(nc.psum_tensor("PS", [P, 8, 512], F32))
        B_FO, B_WO, B_TA, B_TB, B_G, B_CS, B_YT, B_SS = range(8)

        W_IN_PIECES = (slice(DI, DI + 2 * P), slice(DI + 2 * P, NPROJ), slice(0, DI))
        LORA_BANKS = ((0, 1, 3), (4, 5, 6))

        PLACE = [0, 1, 2, 4, 6, 7]
        PLACE_Z = [3, 5, 8, 9]
        SPLIT = 3
        BANK_AT = [B_G, B_CS] * 4 + [B_G, B_WO]

        def bank(b):
            return PS[:, b, :]

        def heads(b):
            return PS[:, b, :].rearrange("p (h q) -> p h q", h=H)

        def parts(b):
            return PS[:, b, :].bitcast(F16).rearrange("p (a k t) -> p a k t", a=2, k=KB)

        def chunk_of(t, c):
            return t[:, bass.ds(at(c), 1), :].rearrange("p o n -> p (o n)")

        def tokens_of(t, c):
            return t[:, :, :, bass.ds(at(c * P), P)]

        s_x = [sem(f"s_x{j}") for j in range(CH)]
        s_q = [sem(f"s_q{k}") for k in range(KB)]; s_la = sem("s_la"); s_small = sem("s_small")
        s_win = [sem(f"s_win{k}") for k in range(KB)]; s_wout = sem("s_wout"); s_raw = sem("s_raw")
        s_o = [sem(f"s_o{k}") for k in range(2)]
        e_const = sem("e_const"); e_lora = sem("e_lora")
        e_max = sem("e_max"); e_all = sem("e_all"); e_scale = sem("e_scale"); e_whi = sem("e_whi"); e_wlo = sem("e_wlo")
        e_id = sem("e_id"); e_zero = sem("e_zero"); e_zerop = sem("e_zerop")
        e_aexp = sem("e_aexp"); e_sel = sem("e_sel"); e_wf = sem("e_wf"); e_dve = sem("e_dve"); e_pool = sem("e_pool")
        spare = {n: sem("e_spare_" + n) for n in ("vector", "gpsimd")}
        names = ("st0 ve0 r0 n0 xb hi0 lo0 t0 tc0 f x1 st1 ve1 lc rr hn hi1 lo1 t1 tc1 mrc "
                 "pi cva hst tapx tap tnh sl tnz slz dtm spx dtp spu dta csm ncs "
                 "bx bxc cs msk lex dcx wv ecs gl g Sm Sd cp xd yt y ss stt "
                 "n1 wo x2 sq ms r2 h2n hi2 lo2 t2 tc2 xsd").split()
        E = {n: sem("e_" + n) for n in names}
        for n in "gu tnb vb pr hib lob d dev wa wb whb fdx mxb alb scx scb dsx dsc".split():
            E[n] = sem("b_" + n)
        for n in "ve r n hi lo t tc f xb o st".split():
            E["c_" + n] = sem("c_" + n)
        FIRST = 3
        STARTED = {"vector": "x2 y stt Sm slz c_o".split(), "gpsimd": ["xsd", "cp"], "scalar": ["tc2", "bxc", "hst"],
                   "tensor": "yt ss t2".split()}
        W = {n: (s, FIRST if any(n in of for of in STARTED.values()) else 0) for n, s in E.items()}

        def start(eng, which):
            for n in STARTED[which]:
                eng.sem_inc(E[n], FIRST)

        def apart(eng):
            eng.sem_inc(spare["vector" if eng is nc.vector else "gpsimd"], 1)

        block = ctx.enter_context(nc.Block())

        @block.sync
        def _(sp_):
            def load_x(c, j):
                sp_.dma_start(x_t[:, j, :], x_in[bass.ds(at(c * P), P), :]).then_inc(s_x[j], 16)

            for k in range(2):
                sp_.sem_inc(s_o[k], 16)
            q_v = q_t.rearrange("(k p) n -> p k n", p=P)
            w_in_v = w_in_t.rearrange("(k p) n -> p k n", p=P)
            load_x(0, 0)
            sp_.wait_ge(e_zero, 3)
            sp_.dma_start(zt[0:NG, :], zeros_t).then_inc(s_la, 16)
            sp_.dma_start(sc[0:NG, :], scales_t).then_inc(s_la, 16)
            sp_.wait_ge(e_zerop, 2)
            sp_.dma_start(la[0:RANK, :], lora_a).then_inc(s_la, 16)
            sp_.dma_start(lb[0:RANK, :], lora_b_t).then_inc(s_la, 16)
            for k in range(KB):
                if k == 2:
                    load_x(1, 1)
                sp_.dma_start(q_raw[:, k, :], q_v[:, k, :]).then_inc(s_q[k], 16)
            sp_.dma_start(hb[:, :], bias.broadcast_to([P, DM])).then_inc(s_small, 16)
            sp_.dma_start(cw[:, :, :], conv_w.rearrange("(b p) t -> p b t", p=P)).then_inc(s_small, 16)
            sp_.dma_start(cb[:, :], conv_b).then_inc(s_small, 16)
            for dst, src in ((al, a_log), (dsk, d_skip), (dtb, dt_bias)):
                sp_.dma_start(dst[:, :], src.broadcast_to([P, H])).then_inc(s_small, 16)
            sp_.dma_start(ln1[:, :], ln1_w).then_inc(s_small, 16)
            sp_.dma_start(ln2[:, :], ln2_w).then_inc(s_small, 16)
            for j in range(2, CH):
                load_x(j, j)
            for k in range(KB):
                sp_.dma_start(raw_in[:, k, :], w_in_v[:, k, :]).then_inc(s_win[k], 16)
            sp_.dma_start(w_out[:, :, :], w_out_t.rearrange("(h p) n -> p h n", p=P)).then_inc(s_wout, 16)

            gate_v = gate_t.rearrange("(k p) f -> p k f", p=P)
            up_v = up_t.rearrange("(k p) f -> p k f", p=P)

            def load_pair(p):
                cols = bass.ds(at(p * PAIR), PAIR)
                sp_.dma_start(raw_gu[:, 0, :, :], gate_v[:, :, cols]).then_inc(s_raw, 16)
                sp_.dma_start(raw_gu[:, 1, :, :], up_v[:, :, cols]).then_inc(s_raw, 16)
                sp_.dma_start(raw_d[:, :, :], down_t[cols, :].rearrange("(b p) n -> p b n", p=P)).then_inc(s_raw, 16)

            load_pair(0)
            with sp_.Fori(1, NS) as reg:
                i = Index(reg, 1)
                for j in range(CH):
                    after(sp_, W["x1"], (i + -1) * CH + (j + 1))
                    load_x(i * CH + j, j)
            with sp_.Fori(1, NP) as reg:
                p = Index(reg, 1)
                after(sp_, W["wb"], p * 2)
                load_pair(p)

            out_v = out
            with sp_.Fori(0, NCH // 2) as reg:
                m = Index(reg, 0)
                for k in range(2):
                    after(sp_, W["c_o"], m * 2 + (k + 1))
                    sp_.dma_start(out_v[bass.ds(at((m * 2 + k) * P), P), :], o_t[k]).then_inc(s_o[k], 16)
            for k in range(2):
                sp_.wait_ge(s_o[k], 16 * (NCH // 2 + 1))

        @block.gpsimd
        def _(po):
            n_self = [0]

            def chain(ins):
                n_self[0] += 1
                ins.then_inc(e_pool, 1)
                po.wait_ge(e_pool, n_self[0])

            def rsqrt(dst, src):
                return po.tensor_tensor(dst, src, mhalf[:, :], ALU.pow)

            def ln0(c, j):
                after(po, W["ve0"], c + 1)
                rsqrt(r0[:, :], mv0[:, 2:3]).then_inc(E["r0"], 1)

            def xb(c, j):
                after(po, W["n0"], c + 1)
                po.tensor_tensor(x_t[:, j, :], x_t[:, j, :], hb[:, :], ALU.add).then_inc(E["xb"], 1)

            def ln1_chain(c, j):
                v = mvN[:, j, 1:2]
                base = c * 4
                after(po, W["ve1"], c + 1)
                rsqrt(rN[:, j:j + 1], mvN[:, j, 2:3]).then_inc(E["lc"], 1)
                after(po, W["lc"], base + 1)
                apart(po)
                po.tensor_scalar(rt[:, 0:1], v, rN[:, j:j + 1], rN[:, j:j + 1], ALU.mult, ALU.mult).then_inc(E["lc"], 1)
                after(po, W["lc"], base + 2)
                apart(po)
                po.tensor_scalar(rt[:, 1:2], rt[:, 0:1], EPS, None, ALU.add).then_inc(E["lc"], 1)
                after(po, W["lc"], base + 3)
                rsqrt(rt[:, 2:3], rt[:, 1:2]).then_inc(E["lc"], 1)
                after(po, W["lc"], base + 4)
                after(po, W["hn"], c)
                po.tensor_tensor(rr[:, :], rN[:, j:j + 1], rt[:, 2:3], ALU.mult).then_inc(E["rr"], 1)

            def scan_c(c, j):
                cols = slice(j * P, (j + 1) * P)
                after(po, W["ecs"], c + 1)
                after(po, W["g"], c + 1)
                po.tensor_tensor(xbc[:, 2:CB, cols], xbc[:, 2:CB, cols], ecs[:, :, :], ALU.mult).then_inc(E["cp"], 1)

            def scan_d(c, j):
                after(po, W["Sm"], c + 1)
                po.tensor_tensor(S[:, j % 2, :, :], S[:, j % 2, :, :], d_diag[:, :, :], ALU.add).then_inc(E["Sd"], 1)

            def rms2(c, j):
                after(po, W["sq"], c + 1)
                apart(po)
                po.tensor_scalar(rt[:, 3:4], ssq[:, :], 1.0 / DM, EPS, ALU.mult, ALU.add).then_inc(E["ms"], 1)
                after(po, W["ms"], c + 1)
                rsqrt(r2[:, j % 2:j % 2 + 1], rt[:, 3:4]).then_inc(E["r2"], 1)
                after(po, W["x2"], c + 1)
                po.tensor_tensor(chunk_of(xs, c), chunk_of(xs, c), x2[:, j % 2, :], ALU.add).then_inc(E["xsd"], 1)

            def resident_max(n):
                po.wait_ge(e_max, n + 1)
                po.partition_all_reduce(mxa[:, n:n + 1], mx[:, n:n + 1], P, bass.bass_isa.ReduceOp.max).then_inc(e_all, 1)

            def pair_max(p):
                after(po, W["mxb"], p + 1)
                apart(po)
                po.partition_all_reduce(mxa3[:, :], mx3[:, :], P, bass.bass_isa.ReduceOp.max).then_inc(E["alb"], 1)

            start(po, "gpsimd")
            po.memset(la[:, :], 0.0).then_inc(e_zerop, 1)
            po.memset(lb[:, :], 0.0).then_inc(e_zerop, 1)
            chain(po.memset(sel[:, :, :], 1.0))
            chain(po.affine_select(out=sel[:, :, :], in_=sel[:, :, :], compare_op=ALU.is_ge, fill=0.0,
                                   base=0, pattern=[[P, KB], [1, P]], channel_multiplier=-GROUP))
            chain(po.affine_select(out=sel[:, :, :], in_=sel[:, :, :], compare_op=ALU.is_ge, fill=0.0,
                                   base=GROUP - 1, pattern=[[-P, KB], [-1, P]], channel_multiplier=GROUP))
            po.sem_inc(e_sel, 1)
            chain(po.memset(ident[:, :], 0.0))
            chain(po.affine_select(out=ident[:, :], in_=ident[:, :], compare_op=ALU.not_equal, fill=1.0,
                                   base=0, pattern=[[-1, P]], channel_multiplier=1))
            chain(po.tensor_copy(ident16[:, :], ident[:, :]))
            chain(po.memset(mhalf[:, :], -0.5))
            po.sem_inc(e_id, 1)
            ln0(0, 0)
            ln0(1, 1)
            chain(po.memset(tri[:, :], 1.0))
            chain(po.affine_select(out=tri[:, :], in_=tri[:, :], compare_op=ALU.is_ge, fill=0.0,
                                   base=0, pattern=[[1, P]], channel_multiplier=-1))
            chain(po.memset(mask[:, :], 0.0))
            chain(po.affine_select(out=mask[:, :], in_=mask[:, :], compare_op=ALU.is_ge, fill=MASKED,
                                   base=0, pattern=[[1, P]], channel_multiplier=-1))
            po.sem_inc(e_const, 1)
            po.wait_ge(s_small, 16 * 8)
            chain(po.tensor_scalar(hb[:, :], hb[:, :], 0.5, None, ALU.mult))
            xb(0, 0)
            xb(1, 1)
            ln0(2, 2)
            resident_max(0)
            xb(2, 2)
            ln0(3, 3)
            for h in range(H):
                chain(po.tensor_scalar(d_diag[:, h, :], ident[:, :], dsk[:, h:h + 1], None, ALU.mult))
            ln1_chain(0, 0)
            xb(3, 3)
            ln1_chain(1, 1)
            ln1_chain(2, 2)
            resident_max(1)
            ln1_chain(3, 3)

            def body(i, nxt):
                if nxt:
                    n = (i + 1) * CH
                    ln0(n, 0)
                    xb(n, 0)
                scan_c(i * CH, 0)
                scan_d(i * CH, 0)
                for j in range(CH):
                    c = i * CH + j
                    if nxt and 0 < j < CH - 1:
                        xb(n + (j + 1), j + 1)
                    if nxt:
                        ln1_chain(n + j, j)
                    if nxt and j == 0:
                        ln0(n + 1, 1)
                    if not nxt and j == 2:
                        pair_max(0)
                    if j < CH - 1:
                        scan_c(c + 1, j + 1)
                    if nxt and j == 0:
                        xb(n + 1, 1)
                    if nxt and j < CH - 2:
                        ln0(n + (j + 2), j + 2)
                    if j < CH - 1:
                        scan_d(c + 1, j + 1)
                    rms2(c, j)

            with po.Fori(0, NS - 1) as reg:
                body(Index(reg, 0), True)
            body(NS - 1, False)
            with po.Fori(1, NP) as reg:
                pair_max(Index(reg, 1))

            def c_norm(c, k):
                after(po, W["c_ve"], c + 1)
                rsqrt(rN[:, k:k + 1], mvN[:, k, 2:3]).then_inc(E["c_r"], 1)
                after(po, W["c_n"], c + 1)
                po.tensor_tensor(chunk_of(xs, c), chunk_of(xs, c), hb[:, :], ALU.add).then_inc(E["c_xb"], 1)

            with po.Fori(0, NCH // 2) as reg:
                for k in range(2):
                    c_norm(Index(reg, 0) * 2 + k, k)

        @block.scalar
        def _(ac):
            start(ac, "scalar")

            def hi0(c, j):
                after(ac, W["n0"], c + 1)
                after(ac, W["t0"], c)
                ac.activation(n0_p[:, 0, :], n0[:, :], ACT.Copy, scale=ACT_SCALE).then_inc(E["hi0"], 1)

            def tc0(c, j):
                after(ac, W["t0"], c + 1)
                after(ac, W["f"], c + -1)
                ac.activation(nT[j % 2], parts(B_TA), ACT.Copy).then_inc(E["tc0"], 1)

            def hi1(c, j):
                after(ac, W["hn"], c + 1)
                after(ac, W["t1"], c)
                ac.activation(hn_p[:, 0, :], hn[:, :], ACT.Copy, scale=ACT_SCALE).then_inc(E["hi1"], 1)

            def tc1(c, j, b=B_TA):
                after(ac, W["t1"], c + 1)
                ac.activation(hT[:, :, :, j * P:(j + 1) * P], parts(b), ACT.Copy).then_inc(E["tc1"], 1)

            def hi2(c):
                after(ac, W["h2n"], c + 1)
                after(ac, W["t2"], c)
                ac.activation(h2n_p[:, 0, :], h2n[:, :], ACT.Copy, scale=ACT_SCALE).then_inc(E["hi2"], 1)

            def tc2(c):
                after(ac, W["t2"], c + 1)
                ac.activation(tokens_of(h2, c), parts(B_TB), ACT.Copy).then_inc(E["tc2"], 1)

            def norm2(c, j):
                after(ac, W["r2"], c + 1)
                after(ac, W["t2"], c)
                ac.activation(h2n[:, :], x2[:, j % 2, :], ACT.Copy, scale=r2[:, j % 2:j % 2 + 1]).then_inc(E["h2n"], 1)

            def square(c, j):
                after(ac, W["x2"], c + 1)
                ac.activation(junk[:, :], x2[:, j % 2, :], ACT.Square, accum_out=ssq[:, :]).then_inc(E["sq"], 1)

            def scan1(c, j):
                s = j % 2
                after(ac, W["bx"], c + 1)
                after(ac, W["ss"], c + -1)
                ac.activation(tm[:, s, :, :], PS[:, B_TB, 0:2 * P].rearrange("p (a t) -> p a t", a=2), ACT.Copy).then_inc(E["bxc"], 1)

            def scan_decay(c, j):
                scan_exp(c, j)
                after(ac, W["msk"], c + 1)
                ac.activation(dec[:, :], dec[:, :], ACT.Exp).then_inc(E["dcx"], 1)
                for h in range(H):
                    last = ac.activation(Ld[:, h, :], Ld[:, h, :], ACT.Exp, bias=ncs[:, j * H + h:j * H + h + 1])
                last.then_inc(E["lex"], 1)

            def scan_exp(c, j):
                s = j % 2
                after(ac, W["msk"], c + 1)
                after(ac, W["cp"], c)
                ac.activation(ecs[:, :, :], heads(B_CS), ACT.Exp).then_inc(E["ecs"], 1)
                ac.activation(g_last[:, s, :], heads(B_CS)[:, :, P - 1:P].rearrange("p h o -> p (h o)"), ACT.Exp).then_inc(E["gl"], 1)

            def scan2(c, j):
                s = j % 2
                after(ac, W["wv"], c + 1)
                for h in range(H):
                    last = ac.activation(xds[:, s, h, :], tm[:, s, 0, :], ACT.Copy, scale=wv[:, s, h:h + 1])
                last.then_inc(E["xd"], 1)

            def hi_gu(x):
                for g in range(2):
                    last = ac.activation(w_gu[0][:, g, :, x * P:(x + 1) * P], raw_gu[:, g, :, x * P:(x + 1) * P], ACT.Copy, scale=sw3[:, g:g + 1])
                return last

            def cut_a(p):
                after(ac, W["scb"], p + 1)
                after(ac, W["gu"], p * (2 * NS) + (-NS))
                hi_gu(0).then_inc(E["whb"], 1)

            def conv(i, b):
                w = b % 2
                after(ac, W["pi"], i * (CB + ZB) + (PLACE[b] + 1))
                after(ac, W["tap"], i * CB + (b - 1))
                after(ac, W["hst"], i * CB + (b + 1 - CB))
                ac.activation(pre[:, w, 0:NTAP - 1], hist[:, b, :], ACT.Copy)
                ac.activation(pre[:, w, NTAP - 1:], bank(BANK_AT[PLACE[b]]), ACT.Copy)
                last = ac.activation(xbc[:, b, :], bank(BANK_AT[PLACE[b]]), ACT.Identity, scale=cw[:, b, NTAP - 1:NTAP], bias=cb[:, b:b + 1])
                last.then_inc(E["cva"], 1)
                after(ac, W["cva"], i * CB + (b + 1))
                ac.activation(hist[:, b, :], pre[:, w, ST:], ACT.Copy).then_inc(E["hst"], 1)

            def tanh(i, b):
                after(ac, W["sl"], i * CB + b)
                after(ac, W["tap"], i * CB + (b + 1))
                ac.activation(th[:, 0, :], xbc[:, b, :], ACT.Tanh).then_inc(E["tnh"], 1)

            def tanh_z(i, h):
                after(ac, W["slz"], i * ZB + h)
                after(ac, W["pi"], i * (CB + ZB) + (PLACE_Z[h] + 1))
                ac.activation(th[:, 1, :], bank(BANK_AT[PLACE_Z[h]]), ACT.Tanh, scale=d_ih[:, :]).then_inc(E["tnz"], 1)

            def win(i, scan):
                conv(i, 0)
                if scan:
                    norm2(i * CH + -1, CH - 1)
                    hi2(i * CH + -1)
                conv(i, 1)
                tanh(i, 0)
                tanh(i, 1)
                conv(i, 2)
                if scan:
                    tc2(i * CH + -1)

            def win_end(i, nxt):
                n = (i + 1) * CH
                after(ac, W["dtp"], i + 1)
                ac.activation(sp[:, 2, :], sp[:, 1, :], ACT.Exp).then_inc(E["spu"], 1)
                tanh_z(i, 0)
                tanh(i, 2)
                conv(i, 3)
                tanh_z(i, 1)
                tanh(i, 3)
                conv(i, 4)
                if nxt:
                    hi0(n, 0)
                conv(i, 5)
                tanh(i, 4)
                tanh_z(i, 2)
                tanh(i, 5)
                if nxt:
                    tc0(n, 0)
                tanh_z(i, 3)
                scan1(i * CH, 0)
                scan_decay(i * CH, 0)
                scan2(i * CH, 0)

            def w_in_hi(piece):
                for k in range(KB):
                    last = ac.activation(w_in[0][:, k, piece], raw_in[:, k, piece], ACT.Copy, scale=lsw[:, k:k + 1])
                last.then_inc(e_whi, 1)

            def body(i, nxt):
                if nxt:
                    n = (i + 1) * CH
                win_end(i, nxt)
                for j in range(CH):
                    c = i * CH + j
                    if nxt and 0 < j < CH - 1:
                        hi0(n + (j + 1), j + 1)
                    if j:
                        norm2(c + -1, j - 1)
                        hi2(c + -1)
                    if j < CH - 1:
                        scan1(c + 1, j + 1)
                    if nxt and 0 < j < CH - 1:
                        tc0(n + (j + 1), j + 1)
                    if j < CH - 1:
                        scan_decay(c + 1, j + 1)
                    if nxt:
                        hi1(n + j, j)
                    if nxt and j == 0:
                        hi0(n + 1, 1)
                        tc0(n + 1, 1)
                    if j < CH - 1:
                        scan2(c + 1, j + 1)
                    if not nxt and j == CH - 1:
                        cut_a(0)
                    if j:
                        tc2(c + -1)
                    if nxt:
                        tc1(n + j, j)
                    square(c, j)
                if nxt:
                    win(i + 1, True)
                else:
                    norm2(c, CH - 1)
                    hi2(c)
                    tc2(c)

            hi0(0, 0)
            ac.wait_ge(s_small, 16 * 8)
            ac.activation(a_neg[:, :], al[:, :], ACT.Exp).then_inc(e_aexp, 1)
            tc0(0, 0)
            hi0(1, 1)
            tc0(1, 1)
            ac.wait_ge(e_scale, 1)
            for k in range(KB):
                ac.activation(w_ffn[0][:, k, :], wf[:, k, :], ACT.Copy, scale=sw[:, 0:1]).then_inc(e_whi, 1)
            hi0(2, 2)
            tc0(2, 2)
            hi0(3, 3)
            hi1(0, 0)
            tc0(3, 3)
            tc1(0, 0, B_TB)
            hi1(1, 1)
            tc1(1, 1, B_TB)
            hi1(2, 2)
            ac.wait_ge(e_scale, 2)
            tc1(2, 2, B_TB)
            w_in_hi(W_IN_PIECES[0])
            w_in_hi(W_IN_PIECES[1])
            hi1(3, 3)
            tc1(3, 3, B_TB)
            w_in_hi(W_IN_PIECES[2])
            ac.wait_ge(e_wlo, KB + len(W_IN_PIECES))
            win(0, False)
            with ac.Fori(0, NS - 1) as reg:
                body(Index(reg, 0), True)
            body(NS - 1, False)

            def cut_b(p):
                after(ac, W["gu"], p * (2 * NS))
                after(ac, W["d"], p * (NS * CH))
                hi_gu(1)
                ac.activation(w_dn[0], raw_d[:, :, :], ACT.Copy, scale=sw3[:, 2:3]).then_inc(E["whb"], 1)

            def step(p, k):
                s = p * (2 * NS) + k
                after(ac, W["gu"], s + 1)
                after(ac, W["dsc"], p + 1)
                ac.activation(gt[:, k % 2, :], bank(2 * (k % 2)), ACT.Tanh, scale=dgh[:, :]).then_inc(E["tnb"], 1)
                after(ac, W["pr"], s + 1)
                if k >= NS:
                    i = k - NS
                    if i >= 2:
                        after(ac, W["d"], p * (NS * CH) + (i - 1) * CH)
                    dst = mB[0][:, i % 2, :]
                else:
                    dst = mA[0][:, k, :]
                ac.activation(dst, gp[:, k % 2, :], ACT.Copy).then_inc(E["hib"], 1)

            def pair(p, nxt):
                for k in range(2 * NS):
                    step(p, k)
                    if k == 0:
                        cut_b(p)
                    if nxt and k == 2 * NS - 2:
                        cut_a(p + 1)

            pair(0, True)
            with ac.Fori(1, NP - 1) as reg:
                pair(Index(reg, 1), True)
            pair(NP - 1, False)

            def c_hi(c, k):
                after(ac, W["c_n"], c + 1)
                after(ac, W["c_t"], c + -1)
                ac.activation(c_np[k][:, 0, :], c_n[k][:, :], ACT.Copy, scale=ACT_SCALE).then_inc(E["c_hi"], 1)

            def c_tc(c, k):
                after(ac, W["c_t"], c + 1)
                after(ac, W["c_f"], c + -1)
                ac.activation(cT[k], parts(k), ACT.Copy).then_inc(E["c_tc"], 1)

            c_hi(0, 0)
            c_hi(1, 1)
            c_tc(0, 0)
            c_tc(1, 1)
            with ac.Fori(1, NCH // 2) as reg:
                for k in range(2):
                    c_hi(Index(reg, 1) * 2 + k, k)
                    c_tc(Index(reg, 1) * 2 + k, k)

        @block.vector
        def _(ve):
            n_self = [0]

            def chain(ins):
                n_self[0] += 1
                ins.then_inc(e_dve, 1)
                ve.wait_ge(e_dve, n_self[0])

            def link(ins, s, count):
                ins.then_inc(s, 1)
                after(ve, (s, 0), count)

            start(ve, "vector")
            ve.memset(junk[:, :], 0.0).then_inc(e_zero, 1)
            ve.memset(zt[:, :], 0.0).then_inc(e_zero, 1)
            ve.memset(sc[:, :], 0.0).then_inc(e_zero, 1)
            chain(ve.memset(hist[:, :, :], 0.0))
            chain(ve.memset(state[:, :, :], 0.0))

            def power_of_two(pw_, sw_, top, link_):
                link_(ve.tensor_scalar(top, top, TINY, None, ALU.max))
                link_(ve.tensor_scalar(pw_.bitcast(I32), top.bitcast(I32), 0x7F800000, None, ALU.bitwise_and))
                link_(ve.tensor_scalar(sw_.bitcast(I32), pw_.bitcast(I32), 0x7F800000, None, ALU.bitwise_xor))
                link_(ve.tensor_scalar(sw_, sw_, 2.0 ** (W_TOP - 1), None, ALU.mult))

            def stats(src, mv, stat, e_link, base, e_ve):
                apart(ve)
                link(ve.bn_stats(stat, src), e_link, base + 1)
                apart(ve)
                link(ve.bn_aggr(mv[:, 0:2], stat), e_link, base + 2)
                ve.tensor_scalar(mv[:, 2:3], mv[:, 1:2], EPS, None, ALU.add).then_inc(e_ve, 1)

            def prep0(c, j):
                after(ve, s_x[j], (c * 1 + (CH - j)) * (16 // CH))
                stats(x_t[:, j, :], mv0[:, :], st6[:, 0, :], E["st0"], c * 2, E["ve0"])

            def norm0(c, j):
                after(ve, W["r0"], c + 1)
                after(ve, W["lo0"], c)
                ve.tensor_scalar(n0[:, :], x_t[:, j, :], mv0[:, 0:1], r0[:, :], ALU.subtract, ALU.mult).then_inc(E["n0"], 1)

            def ffn_weight(k):
                z, s_, l = LORA_BANKS[k % 2]
                ve.wait_ge(s_q[k], 16)
                ve.wait_ge(e_lora, k + 1)
                chain(ve.tensor_tensor(wf[:, k, :], q_raw[:, k, :], bank(z), ALU.subtract))
                chain(ve.tensor_tensor(wf[:, k, :], wf[:, k, :], bank(s_), ALU.mult))
                ve.scalar_tensor_tensor(wf[:, k, :], bank(l), LORA_SCALE, wf[:, k, :], ALU.mult, ALU.add).then_inc(e_wf, 1)
                ve.wait_ge(e_wf, k + 1)
                chain(ve.tensor_reduce(mxf[:, k:k + 1], wf[:, k, :], AX_X, ALU.max, apply_absolute_value=True))

            def ffn_scale():
                ve.tensor_reduce(mx[:, 0:1], mxf[:, :], AX_X, ALU.max).then_inc(e_max, 1)
                norm0(2, 2)
                ve.wait_ge(e_all, 1)
                power_of_two(pw[:, 0:1], sw[:, 0:1], mxa[:, 0:1], chain)
                ve.sem_inc(e_scale, 1)
                chain(ve.tensor_scalar(d_f[:, :], pw[:, 0:1], 0.5 * 2.0 ** -W_TOP / ACT_SCALE, None, ALU.mult))

            def ffn_lo():
                for k in range(KB):
                    ve.wait_ge(e_whi, k + 1)
                    ve.scalar_tensor_tensor(w_ffn[1][:, k, :], wf[:, k, :], sw[:, 0:1], w_ffn[0][:, k, :],
                                            ALU.mult, ALU.subtract).then_inc(e_wlo, 1)

            def w_in_max(k):
                ve.wait_ge(s_win[k], 16)
                chain(ve.tensor_reduce(mxk[:, k:k + 1], raw_in[:, k, :], AX_X, ALU.max, apply_absolute_value=True))

            def w_in_scale():
                ve.wait_ge(s_small, 16 * 8)
                chain(ve.tensor_tensor(mxk[:, :], mxk[:, :], ln1[:, :], ALU.mult))
                ve.tensor_reduce(mx[:, 1:2], mxk[:, :], AX_X, ALU.max, apply_absolute_value=True).then_inc(e_max, 1)
                ve.wait_ge(e_all, 2)
                power_of_two(pw[:, 1:2], sw[:, 1:2], mxa[:, 1:2], chain)
                chain(ve.tensor_scalar(lsw[:, :], ln1[:, :], sw[:, 1:2], None, ALU.mult))
                ve.sem_inc(e_scale, 1)
                chain(ve.tensor_scalar(d_i[:, :], pw[:, 1:2], 2.0 ** -W_TOP / ACT_SCALE, None, ALU.mult))
                chain(ve.tensor_scalar(d_ih[:, :], d_i[:, :], 0.5, None, ALU.mult))
                chain(ve.tensor_scalar(cw[:, :, :], cw[:, :, :], d_ih[:, :], None, ALU.mult))
                chain(ve.tensor_scalar(cb[:, :], cb[:, :], 0.5, None, ALU.mult))
                ve.wait_ge(e_aexp, 1)
                chain(ve.tensor_scalar(a_neg[:, :], a_neg[:, :], -1.0, None, ALU.mult))

            def w_in_lo(n):
                ve.wait_ge(e_whi, KB + n + 1)
                piece = W_IN_PIECES[n]
                for k in range(KB):
                    last = ve.scalar_tensor_tensor(w_in[1][:, k, piece], raw_in[:, k, piece], lsw[:, k:k + 1], w_in[0][:, k, piece],
                                                   ALU.mult, ALU.subtract)
                last.then_inc(e_wlo, 1)

            def lo(pair_, src):
                return ve.scalar_tensor_tensor(pair_[:, 1, :], src[:, :], ACT_SCALE, pair_[:, 0, :], ALU.mult, ALU.subtract)

            def lo0(c, j):
                after(ve, W["hi0"], c + 1)
                lo(n0_p, n0).then_inc(E["lo0"], 1)

            def lo1(c, j):
                after(ve, W["hi1"], c + 1)
                lo(hn_p, hn).then_inc(E["lo1"], 1)

            def lo2(c):
                after(ve, W["hi2"], c + 1)
                lo(h2n_p, h2n).then_inc(E["lo2"], 1)

            def x1_stats(c, j, b=B_FO):
                after(ve, W["f"], c + 1)
                after(ve, W["xb"], c + 1)
                link(ve.scalar_tensor_tensor(chunk_of(xs, c), bank(b), d_f[:, :], x_t[:, j, :], ALU.mult, ALU.add),
                     E["x1"], c + 1)
                stats(chunk_of(xs, c), mvN[:, j, :], st6[:, 1, :], E["st1"], c * 2, E["ve1"])

            def norm1(c, j):
                after(ve, W["rr"], c + 1)
                after(ve, W["lo1"], c)
                ve.tensor_scalar(hn[:, :], chunk_of(xs, c), mvN[:, j, 0:1], rr[:, :], ALU.subtract, ALU.mult).then_inc(E["hn"], 1)

            def masked(c, j):
                after(ve, W["cs"], c + 1)
                after(ve, W["Sm"], c)
                ve.tensor_tensor(Ld[:, :, :], heads(B_CS), mask[:, :].unsqueeze(1).broadcast_to([P, H, P]), ALU.add)
                ve.tensor_tensor(dec[:, :], heads(B_CS)[:, :, P - 1:P].rearrange("p h o -> p (h o)"), ncs[:, j * H:(j + 1) * H], ALU.add).then_inc(E["msk"], 1)

            def weights(c, j):
                s = j % 2
                after(ve, W["dcx"], c + 1)
                ve.tensor_tensor(wv[:, s, :], dec[:, :], dt[:, j * H:(j + 1) * H], ALU.mult).then_inc(E["wv"], 1)

            def scan1(c, j):
                s = j % 2
                after(ve, W["g"], c + 1)
                after(ve, W["lex"], c + 1)
                after(ve, W["yt"], c + -1)
                for h in range(H):
                    last = ve.scalar_tensor_tensor(S[:, s, h, :], heads(B_G)[:, h, :], dt[:, j * H + h:j * H + h + 1], Ld[:, h, :],
                                                   ALU.mult, ALU.mult)
                last.then_inc(E["Sm"], 1)

            def gated(c, j):
                cols = slice(j * P, (j + 1) * P)
                after(ve, W["yt"], c + 1)
                ve.scalar_tensor_tensor(szs[:, :, cols], heads(B_YT), d_ih[:, :], szs[:, :, cols], ALU.mult, ALU.mult).then_inc(E["y"], 1)

            def advance(c, j):
                s = j % 2
                after(ve, W["ss"], c + 1)
                after(ve, W["gl"], c + 1)
                for h in range(H):
                    last = ve.scalar_tensor_tensor(state[:, h, :], state[:, h, :], g_last[:, s, h:h + 1], heads(B_SS)[:, h, :],
                                                   ALU.mult, ALU.add)
                last.then_inc(E["stt"], 1)

            def renorm(c, j):
                after(ve, W["x2"], c)
                ve.tensor_scalar(n1[:, :], chunk_of(xs, c), muC[:, j:j + 1], rC[:, j:j + 1], ALU.subtract, ALU.mult).then_inc(E["n1"], 1)

            def residual2(c, j):
                after(ve, W["n1"], c + 1)
                after(ve, W["wo"], c + 1)
                after(ve, W["xsd"], c + -1)
                ve.tensor_tensor(x2[:, j % 2, :], n1[:, :], bank(B_WO), ALU.add).then_inc(E["x2"], 1)

            def taps(i, b, aside=None):
                w = b % 2
                after(ve, W["cva"], i * CB + (b + 1))
                base = (i * CB + b) * 2
                for k in range(NTAP - 1):
                    ins = ve.scalar_tensor_tensor(xbc[:, b, :], pre[:, w, k:k + ST], cw[:, b, k:k + 1], xbc[:, b, :],
                                                  ALU.mult, ALU.add)
                    ins.then_inc(E["tapx" if k < NTAP - 2 else "tap"], 1)
                    next(aside, None) if aside else None
                    if k < NTAP - 2:
                        after(ve, W["tapx"], base + (k + 1))

            def silu(i, b):
                after(ve, W["tnh"], i * CB + (b + 1))
                ve.scalar_tensor_tensor(xbc[:, b, :], th[:, 0, :], 1.0, xbc[:, b, :], ALU.add, ALU.mult).then_inc(E["sl"], 1)

            def silu_z(i, h):
                after(ve, W["tnz"], i * ZB + (h + 1))
                ve.scalar_tensor_tensor(szs[:, h, :], th[:, 1, :], 1.0, bank(BANK_AT[PLACE_Z[h]]), ALU.add, ALU.mult).then_inc(E["slz"], 1)

            def fold(p):
                after(ve, s_raw, (p + 1) * 48)
                lnb = ln2[:, :].unsqueeze(2).broadcast_to([P, KB, PAIR])
                base = p * 2
                for g in range(2):
                    link(ve.tensor_tensor(raw_gu[:, g, :, :], raw_gu[:, g, :, :], lnb, ALU.mult), E["fdx"], base + (g + 1))

            def maxima_gu():
                for g in range(2):
                    ve.tensor_reduce(mx3[:, g:g + 1], raw_gu[:, g, :, :], mybir.AxisListType.XY, ALU.max, apply_absolute_value=True)

            def maximum_d():
                ve.tensor_reduce(mx3[:, 2:3], raw_d[:, :, :], mybir.AxisListType.XY, ALU.max, apply_absolute_value=True).then_inc(E["mxb"], 1)

            def scales(p):
                n = [0]

                def lk(ins):
                    n[0] += 1
                    link(ins, E["scx"], p * 4 + n[0])

                after(ve, W["alb"], p + 1)
                power_of_two(pw3[:, :], sw3[:, :], mxa3[:, :], lk)
                assert n[0] == 4
                ve.sem_inc(E["scb"], 1)

            def lo_gu(x):
                cols = slice(x * P, (x + 1) * P)
                for g in range(2):
                    last = ve.scalar_tensor_tensor(w_gu[1][:, g, :, cols], raw_gu[:, g, :, cols], sw3[:, g:g + 1], w_gu[0][:, g, :, cols],
                                                   ALU.mult, ALU.subtract)
                return last

            def cut_a(p):
                after(ve, W["whb"], p * 2 + 1)
                lo_gu(0).then_inc(E["wa"], 1)

            def cut_b(p):
                after(ve, W["whb"], p * 2 + 2)
                lo_gu(1).then_inc(E["wb"], 1)
                ve.scalar_tensor_tensor(w_dn[1].rearrange("p b n -> p (b n)"), raw_d[:, :, :].rearrange("p b n -> p (b n)"), sw3[:, 2:3],
                                        w_dn[0].rearrange("p b n -> p (b n)"), ALU.mult, ALU.subtract).then_inc(E["wb"], 1)

            N_SP = 16

            def softplus(i):
                base = i * N_SP
                n = 0
                v, m, u, s1, s2, q = (sp[:, k, :] for k in range(6))

                def rep(t):
                    return t[:, :].unsqueeze(1).broadcast_to([P, CH, H])

                def four(t):
                    return t.rearrange("p (c h) -> p c h", c=CH)

                steps = [lambda: ve.scalar_tensor_tensor(four(v), four(PS[:, B_SS, 0:NT]), d_i[:, :], rep(dtb), ALU.mult, ALU.add),
                         lambda: ve.tensor_scalar(m, v, -1.0, None, ALU.mult),
                         "min",
                         lambda: ve.tensor_scalar(s1, u, 2.0, None, ALU.add),
                         lambda: ve.reciprocal(s2, s1),
                         lambda: ve.tensor_tensor(s1, u, s2, ALU.mult),
                         lambda: ve.tensor_tensor(s2, s1, s1, ALU.mult),
                         lambda: ve.tensor_scalar(q, s2, 1.0 / 15, None, ALU.mult)]
                steps += [lambda k=k: ve.scalar_tensor_tensor(q, q, 1.0 / k, s2, ALU.add, ALU.mult) for k in (13, 11, 9, 7, 5, 3)]
                steps += [lambda: ve.scalar_tensor_tensor(q, q, 1.0, s1, ALU.add, ALU.mult),
                          lambda: ve.tensor_scalar(v, v, 0.0, None, ALU.max),
                          lambda: ve.scalar_tensor_tensor(dt[:, :], q, 2.0, v, ALU.mult, ALU.add)]
                for step_ in steps:
                    if n:
                        after(ve, W["spx"], base + n)
                    else:
                        after(ve, W["dtm"], i + 1)
                    if step_ == "min":
                        ve.tensor_tensor(m, m, v, ALU.min).then_inc(E["dtp"], 1)
                        yield
                        after(ve, W["spu"], i + 1)
                    else:
                        step_().then_inc(E["spx"], 1)
                        n += 1
                        yield
                assert n == N_SP, n
                after(ve, W["spx"], base + n)
                ve.tensor_tensor(four(dA[:, :]), four(dt[:, :]), rep(a_neg), ALU.mult).then_inc(E["dta"], 1)
                yield

            def win(i, scan):
                taps(i, 0)
                if scan:
                    lo2(i * CH + -1)
                taps(i, 1)
                silu(i, 0)
                silu(i, 1)

            def win_end(i, nxt):
                n = (i + 1) * CH
                c = i * CH
                aside = softplus(i)
                next(aside)
                taps(i, 2, aside)
                silu_z(i, 0)
                next(aside)
                silu(i, 2)
                next(aside)
                if nxt:
                    prep0(n, 0)
                taps(i, 3, aside)
                silu_z(i, 1)
                next(aside)
                if nxt:
                    norm0(n, 0)
                silu(i, 3)
                next(aside)
                taps(i, 4, aside)
                if nxt:
                    lo0(n, 0)
                taps(i, 5, aside)
                for _ in aside:
                    pass
                silu(i, 4)
                silu_z(i, 2)
                silu(i, 5)
                after(ve, W["csm"], i + 1)
                link(ve.tensor_scalar(ncs[:, :], PS[:, B_YT, 0:NT], -1.0, None, ALU.mult), E["ncs"], i + 1)
                masked(c, 0)
                weights(c, 0)
                silu_z(i, 3)
                scan1(c, 0)

            def keep_stats(i):
                after(ve, W["rr"], i * CH + CH)
                ve.tensor_copy(muC[:, :], mvN[:, :, 0:1].rearrange("p c o -> p (c o)"))
                link(ve.tensor_copy(rC[:, :], rN[:, :]), E["mrc"], i + 1)

            def body(i, nxt):
                win_end(i, nxt)
                if nxt:
                    n = (i + 1) * CH
                for j in range(CH):
                    c = i * CH + j
                    if nxt and 0 < j < CH - 1:
                        lo0(n + (j + 1), j + 1)
                    if j:
                        renorm(c, j)
                    if nxt:
                        x1_stats(n + j, j)
                    if nxt and j:
                        lo2(c + -1)
                    if j < CH - 1:
                        masked(c + 1, j + 1)
                    if nxt and j == 0:
                        prep0(n + 1, 1)
                    gated(c, j)
                    if j < CH - 1:
                        weights(c + 1, j + 1)
                    if nxt:
                        norm1(n + j, j)
                    if nxt and j == 0:
                        norm0(n + 1, 1)
                    advance(c, j)
                    if nxt and j == 0:
                        lo0(n + 1, 1)
                    if nxt:
                        lo1(n + j, j)
                    if j == 0:
                        renorm(c, j)
                    if j < CH - 1:
                        scan1(c + 1, j + 1)
                    if nxt and j < CH - 2:
                        prep0(n + (j + 2), j + 2)
                        norm0(n + (j + 2), j + 2)
                    if not nxt and j:
                        lo2(c + -1)
                    if not nxt and j == CH - 1:
                        cut_a(0)
                    residual2(c, j)
                    if not nxt and j == 0:
                        fold(0)
                    if not nxt and j == 1:
                        maxima_gu()
                        maximum_d()
                    if not nxt and j == 2:
                        scales(0)
                if nxt:
                    keep_stats(i + 1)
                    win(i + 1, True)
                else:
                    lo2(c)

            prep0(0, 0)
            norm0(0, 0)
            prep0(1, 1)
            ffn_weight(0)
            lo0(0, 0)
            ffn_weight(1)
            norm0(1, 1)
            prep0(2, 2)
            ffn_weight(2)
            lo0(1, 1)
            ffn_weight(3)
            ffn_scale()
            ffn_lo()
            prep0(3, 3)
            w_in_max(0)
            lo0(2, 2)
            x1_stats(0, 0, B_FO)
            norm0(3, 3)
            w_in_max(1)
            norm1(0, 0)
            lo0(3, 3)
            x1_stats(1, 1, B_WO)
            lo1(0, 0)
            w_in_max(2)
            norm1(1, 1)
            x1_stats(2, 2, B_FO)
            lo1(1, 1)
            w_in_max(3)
            norm1(2, 2)
            w_in_scale()
            lo1(2, 2)
            x1_stats(3, 3, B_WO)
            w_in_lo(0)
            norm1(3, 3)
            lo1(3, 3)
            w_in_lo(1)
            w_in_lo(2)
            keep_stats(0)
            win(0, False)
            with ve.Fori(0, NS - 1) as reg:
                body(Index(reg, 0), True)
            body(NS - 1, False)

            def descale(p):
                back = 2.0 ** -W_TOP / ACT_SCALE
                ve.tensor_scalar(dgh[:, :], pw3[:, 0:1], 0.5 * back, None, ALU.mult)
                link(ve.tensor_scalar(d_tmp[:, :], pw3[:, 0:1], pw3[:, 1:2], pw3[:, 2:3], ALU.mult, ALU.mult), E["dsx"], p + 1)
                ve.tensor_scalar(d_d[:, :], d_tmp[:, :], 0.5 * back * back / GATED_SCALE * 2.0 ** -W_TOP, None, ALU.mult).then_inc(E["dsc"], 1)

            def step(p, k):
                s = p * (2 * NS) + k
                w = k % 2
                after(ve, W["tnb"], s + 1)
                link(ve.scalar_tensor_tensor(gt[:, w, :], gt[:, w, :], 1.0, bank(2 * w), ALU.add, ALU.mult), E["vb"], s + 1)
                ve.scalar_tensor_tensor(gp[:, w, :], gt[:, w, :], GATED_SCALE, bank(2 * w + 1), ALU.mult, ALU.mult).then_inc(E["pr"], 1)
                after(ve, W["hib"], s + 1)
                hi, lo_ = (mB[0][:, k % 2, :], mB[1][:, k % 2, :]) if k >= NS else (mA[0][:, k, :], mA[1][:, k, :])
                ve.tensor_tensor(lo_, gp[:, w, :], hi, ALU.subtract).then_inc(E["lob"], 1)

            def down(p, i):
                for t in range(CH):
                    after(ve, W["d"], p * (NS * CH) + (i * CH + t + 1))
                    c = i * CH + t
                    ve.scalar_tensor_tensor(xs[:, c, :], bank(4 + t), d_d[:, :], xs[:, c, :], ALU.mult, ALU.add).then_inc(E["dev"], 1)

            def pair(p, nxt):
                descale(p)
                for k in range(2 * NS):
                    if k >= NS + 2:
                        down(p, k - NS - 2)
                    if not nxt and k == 2 * NS - 1:
                        c_begin()
                    step(p, k)
                    if k == 0:
                        cut_b(p)
                    if nxt and k == NS:
                        fold(p + 1)
                        maxima_gu()
                        maximum_d()
                    if nxt and k == NS + 1:
                        scales(p + 1)
                    if nxt and k == 2 * NS - 2:
                        cut_a(p + 1)
                if not nxt:
                    c_lo(0, 0)
                    c_lo(1, 1)
                down(p, NS - 2)
                down(p, NS - 1)

            def c_stats(c, k):
                stats(chunk_of(xs, c), mvN[:, k, :], st6[:, k, :], E["c_st"], c * 2, E["c_ve"])

            def c_norm(c, k):
                after(ve, W["c_r"], c + 1)
                after(ve, W["c_t"], c + -1)
                ve.tensor_scalar(c_n[k][:, :], chunk_of(xs, c), mvN[:, k, 0:1], rN[:, k:k + 1], ALU.subtract, ALU.mult).then_inc(E["c_n"], 1)

            def c_lo(c, k):
                after(ve, W["c_hi"], c + 1)
                lo(c_np[k], c_n[k]).then_inc(E["c_lo"], 1)

            def c_out(c, k):
                after(ve, W["c_f"], c + 1)
                after(ve, W["c_xb"], c + 1)
                after(ve, s_o[k], (c + (2 - k)) * 8)
                ve.scalar_tensor_tensor(o_t[k], bank(2 + k), d_f[:, :], chunk_of(xs, c), ALU.mult, ALU.add).then_inc(E["c_o"], 1)

            def c_begin():
                after(ve, W["dev"], (NP - 1) * NCH + CH)
                c_stats(0, 0)
                c_norm(0, 0)
                c_stats(1, 1)
                c_norm(1, 1)
                c_stats(2, 0)

            def c_step(c, k, first=False, left=NCH):
                if left > 2:
                    c_norm(c + 2, k)
                if left > 3:
                    c_stats(c + 3, 1 - k)
                if left > 2:
                    c_lo(c + 2, k)
                if not first:
                    c_out(c + -1, 1 - k)

            after(ve, W["xsd"], NCH)
            pair(0, True)
            with ve.Fori(1, NP - 1) as reg:
                pair(Index(reg, 1), True)
            pair(NP - 1, False)
            c_step(0, 0, first=True)
            after(ve, W["dev"], NP * NCH)
            with ve.Fori(0, NCH // 2 - 2) as reg:
                for k in range(2):
                    c_step(Index(reg, 0) * 2 + (1 + k), 1 - k)
            for c in range(NCH - 3, NCH + 1):
                c_step(c, c % 2, left=NCH - c)

        @block.tensor
        def _(pe):
            start(pe, "tensor")

            def transposes(b, src):
                for a in range(2):
                    for k in range(KB):
                        last = pe.transpose(parts(b)[:, a, k, :], src[:, a, k * P:(k + 1) * P], ident16[:, :])
                return last

            def product(out_, lhs, rhs, n_k, first=True, last=True):
                todo = [(k, a, b) for k in range(n_k) for a, b in PARTS]
                for n, (k, a, b) in enumerate(todo):
                    ins = pe.matmul(out_, lhs(a, b, k), rhs(a, b, k), start=first and n == 0, stop=last and n == len(todo) - 1)
                return ins

            def ffn_parts(k):
                z, s_, l = LORA_BANKS[k % 2]
                if k >= 2:
                    pe.wait_ge(e_wf, k - 1)
                pe.matmul(bank(z), sel[:, k, :], zt[:, :], start=True, stop=True)
                pe.matmul(bank(s_), sel[:, k, :], sc[:, :], start=True, stop=True)
                pe.matmul(bank(l), la[:, k * P:(k + 1) * P], lb[:, :], start=True, stop=True).then_inc(e_lora, 1)

            def t0(c, j):
                after(pe, W["lo0"], c + 1)
                if j == 1:
                    after(pe, W["tc0"], c)
                if j >= 2:
                    after(pe, W["tc1"], c + -1)
                transposes(B_TA, n0_p).then_inc(E["t0"], 1)

            def f(c, j):
                after(pe, W["tc0"], c + 1)
                after(pe, W["x1"], c)
                product(bank(B_FO), lambda a, b, k: nT[j % 2][:, a, k, :], lambda a, b, k: w_ffn[b][:, k, :], KB).then_inc(E["f"], 1)

            def t1(c, j):
                after(pe, W["lo1"], c + 1)
                if j < CH - 1:
                    after(pe, W["tc0"], c + 2)
                else:
                    after(pe, W["tc1"], c)
                transposes(B_TA, hn_p).then_inc(E["t1"], 1)

            def t2(c, scans_copied):
                after(pe, W["lo2"], c + 1)
                after(pe, W["bxc"], scans_copied)
                transposes(B_TB, h2n_p).then_inc(E["t2"], 1)

            at_place = {PLACE[b]: DI + b * P for b in range(CB)} | {PLACE_Z[h]: h * P for h in range(ZB)}

            def win(i, places, scan=True):
                if places[0] == 0:
                    after(pe, W["tc1"], i * CH + CH)
                for q in places:
                    before = [r_ for r_ in range(q) if BANK_AT[r_] == BANK_AT[q]]
                    if not before:
                        last_use = {B_G: "Sm", B_CS: "gl", B_WO: "x2"}[BANK_AT[q]]
                        after(pe, W[last_use], i * CH)
                    elif before[-1] in PLACE:
                        after(pe, W["cva"], i * CB + (PLACE.index(before[-1]) + 1))
                    else:
                        after(pe, W["slz"], i * ZB + (PLACE_Z.index(before[-1]) + 1))
                    if not scan and q == 3:
                        pe.wait_ge(e_wlo, KB + 3)
                    product(bank(BANK_AT[q]), lambda a, b, k: w_in[b][:, k, at_place[q]:at_place[q] + P], lambda a, b, k: hT[:, a, k, :], KB).then_inc(E["pi"], 1)
                    if scan and q == 2:
                        t2(i * CH + -1, i * CH)
                    if q == 1:
                        if not scan:
                            pe.wait_ge(e_wlo, KB + 2)
                        after(pe, W["stt"], i * CH)
                        for j in range(CH):
                            last = product(PS[:, B_SS, j * H:(j + 1) * H], lambda a, b, k: hT[:, a, k, j * P:(j + 1) * P],
                                           lambda a, b, k: w_in[b][:, k, NPROJ - H:NPROJ], KB)
                        last.then_inc(E["dtm"], 1)

            def csm(i):
                after(pe, W["dta"], i + 1)
                after(pe, W["y"], i * CH)
                pe.matmul(PS[:, B_YT, 0:NT], tri[:, :], dA[:, :], start=True, stop=True).then_inc(E["csm"], 1)

            def s1(c, i, j):
                cols = slice(j * P, (j + 1) * P)
                if j == 0:
                    after(pe, W["sl"], i * CB + 2)
                after(pe, W["bxc"], c)
                if j == 0:
                    after(pe, W["tc2"], c)
                if j >= 2:
                    after(pe, W["tc2"], c + -2)
                for n in range(2):
                    last = pe.transpose(PS[:, B_TB, n * P:(n + 1) * P], xbc[:, n, cols], ident[:, :])
                last.then_inc(E["bx"], 1)
                if j == 0:
                    after(pe, W["cva"], (i + 1) * CB)
                else:
                    after(pe, W["gl"], c)
                for h in range(H):
                    n = j * H + h
                    last = pe.matmul(heads(B_CS)[:, h, :], dA[:, n:n + 1].broadcast_to([P, P]), tri[:, :], start=True, stop=True)
                last.then_inc(E["cs"], 1)

            def s1_bc(c, i, j):
                cols = slice(j * P, (j + 1) * P)
                if j == 0:
                    after(pe, W["sl"], (i + 1) * CB)
                    after(pe, W["slz"], i * ZB + (ZB - 1))
                else:
                    after(pe, W["Sm"], c)
                pe.matmul(heads(B_G), xbc[:, 1, cols], xbc[:, 2:CB, cols], start=True, stop=True).then_inc(E["g"], 1)

            def s2_diag(c, j):
                s = j % 2
                after(pe, W["Sd"], c + 1)
                after(pe, W["bxc"], c + 1)
                after(pe, W["y"], c)
                pe.matmul(heads(B_YT), tm[:, s, 0, :], S[:, s, :, :], start=True, stop=False)

            def s2_state(c, j):
                s = j % 2
                cols = slice(j * P, (j + 1) * P)
                after(pe, W["cp"], c + 1)
                after(pe, W["stt"], c)
                for h in range(H):
                    last = pe.matmul(heads(B_YT)[:, h, :], state[:, h, :], xbc[:, 2 + h, cols], start=False, stop=h == H - 1)
                last.then_inc(E["yt"], 1)
                after(pe, W["xd"], c + 1)
                pe.matmul(heads(B_SS), tm[:, s, 1, :], xds[:, s, :, :], start=True, stop=True).then_inc(E["ss"], 1)

            def w(c, i, j, nxt):
                after(pe, W["y"], c + 1)
                after(pe, W["x2"], c)
                for h in range(H):
                    if nxt and j == 0 and h == 1:
                        t0(c + CH + 1, 1)
                    if nxt and h == H - 1:
                        t1(c + CH, j)
                    if not nxt and j and h == H - 1:
                        t2(c + -1, i * CH + (min(j + 1, CH - 1) + 1))
                    last = pe.matmul(bank(B_WO), szs[:, h, j * P:(j + 1) * P], w_out[:, h, :], start=h == 0, stop=h == H - 1)
                last.then_inc(E["wo"], 1)

            def body(i, nxt):
                if nxt:
                    n = (i + 1) * CH
                win(i, range(SPLIT, CB + ZB - 1))
                if nxt:
                    t0(n, 0)
                win(i, range(CB + ZB - 1, CB + ZB))
                csm(i)
                s1(i * CH, i, 0)
                s1_bc(i * CH, i, 0)
                for j in range(CH):
                    c = i * CH + j
                    if nxt:
                        f(n + j, j)
                    if j < CH - 1:
                        s1(c + 1, i, j + 1)
                    s2_diag(c, j)
                    if nxt and 0 < j < CH - 1:
                        t0(n + (j + 1), j + 1)
                    s2_state(c, j)
                    if j < CH - 1:
                        s1_bc(c + 1, i, j + 1)
                    if nxt and j:
                        t2(c + -1, i * CH + (min(j + 1, CH - 1) + 1))
                    w(c, i, j, nxt)
                if nxt:
                    win(i + 1, range(SPLIT))

            def keep_warm():
                for _ in range(N_WARM):
                    pe.matmul(bank(B_SS), junk[:, 0:P], junk[:, :], start=True, stop=True)

            pe.wait_ge(e_zero, 1)
            keep_warm()

            def first_t0(c):
                after(pe, W["lo0"], c + 1)
                after(pe, W["tc0"], c)
                transposes(B_TA, n0_p).then_inc(E["t0"], 1)

            def first_t1(c):
                after(pe, W["lo1"], c + 1)
                after(pe, W["tc1"], c)
                transposes(B_TB, hn_p).then_inc(E["t1"], 1)

            def first_f(c):
                after(pe, W["tc0"], c + 1)
                after(pe, W["x1"], c - 1)
                for k in range(KB):
                    if c == 0:
                        pe.wait_ge(e_wlo, k + 1)
                    for a, b in PARTS:
                        last = pe.matmul(bank((B_FO, B_WO)[c % 2]), nT[c % 2][:, a, k, :], w_ffn[b][:, k, :],
                                         start=(k, a, b) == (0, *PARTS[0]), stop=(k, a, b) == (KB - 1, *PARTS[-1]))
                last.then_inc(E["f"], 1)

            pe.wait_ge(s_la, 64)
            pe.wait_ge(e_sel, 1)
            ffn_parts(0)
            ffn_parts(1)
            pe.wait_ge(e_id, 1)
            first_t0(0)
            ffn_parts(2)
            ffn_parts(3)
            first_t0(1)
            keep_warm()
            first_f(0)
            first_t0(2)
            first_f(1)
            first_t0(3)
            first_t1(0)
            first_f(2)
            first_t1(1)
            first_f(3)
            first_t1(2)
            keep_warm()
            first_t1(3)
            pe.wait_ge(e_const, 1)
            pe.wait_ge(e_wlo, KB + 1)
            pe.wait_ge(s_wout, 16)
            win(0, range(SPLIT), False)
            with pe.Fori(0, NS - 1) as reg:
                body(Index(reg, 0), True)
            body(NS - 1, False)

            def gate_up(p, k, first=False):
                i, x = k % NS, k // NS
                s = p * (2 * NS) + k
                if k == 0:
                    after(pe, W["wa"], p + 1)
                if k == NS:
                    after(pe, W["wb"], p * 2 + 1)
                after(pe, W["pr"], s + -1)
                for g in range(2):
                    if first and g == 1:
                        after(pe, W["x2"], NCH)
                    if p == 0 and k == 1 and g == 1:
                        after(pe, W["tc2"], NCH)
                    last = product(bank(2 * (k % 2) + g), lambda a, b, kb: w_gu[b][:, g, kb, x * P:(x + 1) * P],
                                   lambda a, b, kb: h2T[a][:, kb, i * ST:(i + 1) * ST], KB)
                last.then_inc(E["gu"], 1)

            def down(p, i):
                if i == 0:
                    after(pe, W["wb"], p * 2 + 2)
                after(pe, W["lob"], p * (2 * NS) + (NS + i + 1))
                for t in range(CH):
                    n = p * (NS * CH) + (i * CH + t)
                    after(pe, W["dev"], n + -(CH - 1))
                    cols = slice(t * P, (t + 1) * P)
                    product(bank(4 + t), lambda a, b, kb: (mA[a][:, i, cols] if kb == 0 else mB[a][:, i % 2, cols]),
                            lambda a, b, kb: w_dn[b][:, kb, :], 2).then_inc(E["d"], 1)

            def pair(p, first=False, last=False):
                for k in range(NS + 2):
                    if first and k == 1:
                        t2(NCH - 1, NCH)
                    gate_up(p, k, first and k == 0)
                if first:
                    after(pe, W["stt"], NCH)
                for k in range(NS + 2, 2 * NS):
                    down(p, k - NS - 2)
                    gate_up(p, k)
                down(p, NS - 2)
                if last:
                    after(pe, W["pr"], NP * 2 * NS - 1)
                    c_t(0, 0)
                    c_t(1, 1)
                down(p, NS - 1)

            def c_t(c, k):
                after(pe, W["c_lo"], c + 1)
                after(pe, W["c_tc"], c + -1)
                transposes(k, c_np[k]).then_inc(E["c_t"], 1)

            def c_f(c, k):
                after(pe, W["c_tc"], c + 1)
                after(pe, W["c_o"], c + -1)
                product(bank(2 + k), lambda a, b, kb: cT[k][:, a, kb, :], lambda a, b, kb: w_ffn[b][:, kb, :], KB).then_inc(E["c_f"], 1)

            pair(0, first=True)
            with pe.Fori(1, NP - 1) as reg:
                pair(Index(reg, 1))
            pair(NP - 1, last=True)
            after(pe, W["pr"], NP * 2 * NS)
            c_f(0, 0)
            c_t(2, 0)
            with pe.Fori(0, NCH // 2 - 2) as reg:
                for k in range(2):
                    c = Index(reg, 0) * 2 + (1 + k)
                    c_f(c, 1 - k)
                    c_t(c + 2, 1 - k)
            for c in range(NCH - 3, NCH):
                c_f(c, c % 2)
                if c + 2 < NCH:
                    c_t(c + 2, c % 2)


def kernel(L0_attn_hidden_states, L0_attn_w_in, L0_attn_conv_w, L0_attn_conv_b, L0_attn_A_log, L0_attn_D,
           L0_attn_dt_bias, L0_attn_w_out, L0_attn_ln1_w, L0_attn_ln2_w, L0_attn_gate_w, L0_attn_up_w,
           L0_attn_down_w, L0_ffn_qweight, L0_ffn_scales, L0_ffn_zeros, L0_ffn_lora_A, L0_ffn_lora_B, L0_ffn_bias):
    import numpy as np
    import concourse.bacc as bacc
    from concourse.bass_utils import run_bass_kernel_spmd

    x = np.asarray(L0_attn_hidden_states)

    def columns(v):
        return np.asarray(v).reshape(-1, P).T

    arrays = {
        "x_in": x.reshape(-1, x.shape[-1]),
        "w_in_t": np.asarray(L0_attn_w_in).T,
        "conv_w": np.asarray(L0_attn_conv_w),
        "conv_b": columns(L0_attn_conv_b),
        "a_log": np.asarray(L0_attn_A_log).reshape(1, -1),
        "d_skip": np.asarray(L0_attn_D).reshape(1, -1),
        "dt_bias": np.asarray(L0_attn_dt_bias).reshape(1, -1),
        "w_out_t": np.asarray(L0_attn_w_out).T,
        "ln1_w": columns(L0_attn_ln1_w),
        "ln2_w": columns(L0_attn_ln2_w),
        "gate_t": np.asarray(L0_attn_gate_w).T,
        "up_t": np.asarray(L0_attn_up_w).T,
        "down_t": np.asarray(L0_attn_down_w).T,
        "q_t": np.asarray(L0_ffn_qweight).T,
        "scales_t": np.asarray(L0_ffn_scales).T,
        "zeros_t": np.asarray(L0_ffn_zeros).T,
        "lora_a": np.asarray(L0_ffn_lora_A),
        "lora_b_t": np.asarray(L0_ffn_lora_B).T,
        "bias": np.asarray(L0_ffn_bias).reshape(1, -1),
    }
    arrays = {n: np.ascontiguousarray(a) for n, a in arrays.items()}
    nc = bacc.Bacc("TRN2", target_bir_lowering=False, num_devices=1)
    args = {n: nc.dram_tensor(n, a.shape, mybir.dt.from_np(a.dtype), kind="ExternalInput").ap() for n, a in arrays.items()}
    out = nc.dram_tensor("out", arrays["x_in"].shape, F32, kind="ExternalOutput").ap()
    build(nc, out=out, **args)
    r = run_bass_kernel_spmd(nc, [arrays], core_ids=[0])
    return r.results[0]["out"].reshape(x.shape)
```
